# Optimizing a Trainium2 kernel written in Bass

```python
import numpy as np
import jax
import jax.numpy as jnp

def _softmax(x, axis=-1):
    return jax.nn.softmax(x, axis=axis)

def _gelu(x):
    return jax.nn.gelu(x, approximate=True)

def _silu(x):
    return jax.nn.silu(x)

def _sigmoid(x):
    return jax.nn.sigmoid(x)

def _layernorm(x, axis=-1, eps=1e-05):
    m = jnp.mean(x, axis=axis, keepdims=True)
    v = jnp.var(x, axis=axis, keepdims=True)
    return (x - m) / jnp.sqrt(v + eps)

def _scatter_add(tgt, idx, src, axis=0):
    return tgt.at[idx].add(src)

def _segment_sum(src, seg, n):
    return jax.ops.segment_sum(src, seg, n)
kernel_name = 'mk_gps_d2_gnn_r8_980010'

def setup_inputs(seed: int=0):
    np.random.seed(seed)
    _w = jnp.asarray

    def _rec_inputs():
        import jax
        import jax.numpy as jnp
        _gk = jax.random.key(seed)
        x = -8.776e-05 + 1 * jax.random.normal(jax.random.fold_in(_gk, 1), (2500, 256), jnp.float32)
        src = jax.random.randint(jax.random.fold_in(_gk, 2), (40000,), 0, 2500, jnp.int32)
        dst = jax.random.randint(jax.random.fold_in(_gk, 3), (40000,), 0, 2500, jnp.int32)
        _o = jnp.argsort(dst, stable=True)
        src = src[_o]
        dst = dst[_o]
        edge_attr_256 = 2.93046e-05 + 1.00006 * jax.random.normal(jax.random.fold_in(_gk, 11), (40000, 256), jnp.float32)
        return (x, src, dst, edge_attr_256)
    x, src, dst, edge_attr_256 = _rec_inputs()

    def _L0_gnn_setup():
        import jax, jax.numpy as jnp
        import numpy as np
        N_NODES = 2500
        BN_EPS = 1e-05

        def _sage(x, src, dst, W_l, b_l, W_r):
            msg_sum = jax.ops.segment_sum(x[src], dst, num_segments=N_NODES)
            cnt = jax.ops.segment_sum(jnp.ones((src.shape[0],), x.dtype), dst, num_segments=N_NODES)
            aggr = msg_sum / jnp.maximum(cnt, 1.0)[:, None]
            return aggr @ W_l.T + b_l + x @ W_r.T
        key = jax.random.key(seed)
        ks = jax.random.split(key, 8)
        in_dim, half, out_dim, n_edges = (256, 128, 256, 40000)
        s = 1.0 / np.sqrt(in_dim)
        return {'x': jax.random.normal(ks[0], (N_NODES, in_dim), dtype=jnp.float32), 'edge_index': jax.random.randint(ks[1], (2, n_edges), 0, N_NODES, dtype=jnp.int64), 'W_l_f': jax.random.normal(ks[2], (half, in_dim), dtype=jnp.float32) * s, 'b_l_f': jnp.zeros((half,), dtype=jnp.float32), 'W_r_f': jax.random.normal(ks[3], (half, in_dim), dtype=jnp.float32) * s, 'W_l_b': jax.random.normal(ks[4], (half, in_dim), dtype=jnp.float32) * s, 'b_l_b': jnp.zeros((half,), dtype=jnp.float32), 'W_r_b': jax.random.normal(ks[5], (half, in_dim), dtype=jnp.float32) * s, 'gamma': jnp.ones((out_dim,), dtype=jnp.float32), 'beta': jnp.zeros((out_dim,), dtype=jnp.float32)}
    _L0_gnn_all = _L0_gnn_setup()
    _L0_gnn_in = {k: v for k, v in _L0_gnn_all.items() if k in ('W_l_f', 'b_l_f', 'W_r_f', 'W_l_b', 'b_l_b', 'W_r_b', 'gamma', 'beta')}
    del _L0_gnn_all

    def _L0_mix_setup():
        import jax, jax.numpy as jnp
        import numpy as np
        import math
        EMBED = 256
        HEADS = 4
        HEAD_DIM = EMBED // HEADS
        OUT_DIM = 256
        LN_EPS = 1e-05

        def _qkv_init(key):
            spread = math.sqrt(3.0 / EMBED)
            gain, delta = (0.01, 0.01)
            w = jax.random.uniform(key, (EMBED, EMBED), minval=-spread, maxval=spread) * gain
            return w + delta * jnp.eye(EMBED, dtype=w.dtype)

        def _layer_norm(x, g, b):
            mu = jnp.mean(x, axis=-1, keepdims=True)
            var = jnp.mean(jnp.square(x - mu), axis=-1, keepdims=True)
            return (x - mu) * jax.lax.rsqrt(var + LN_EPS) * g + b

        def _split_heads(x, B, S):
            return x.reshape(B, S, HEADS, HEAD_DIM).transpose(0, 2, 1, 3)
        key = jax.random.key(seed)
        ks = jax.random.split(key, 6)
        seq = jax.random.normal(ks[0], (4, 1024, EMBED), dtype=jnp.float32)
        wq = _qkv_init(ks[1])
        wk = _qkv_init(ks[2])
        wv = _qkv_init(ks[3])
        bound = 1.0 / math.sqrt(EMBED)
        wo = jax.random.uniform(ks[4], (OUT_DIM, EMBED), minval=-bound, maxval=bound)
        bo = jax.random.uniform(ks[5], (OUT_DIM,), minval=-bound, maxval=bound)
        ln_k_g = jnp.ones((HEAD_DIM,), jnp.float32)
        ln_k_b = jnp.zeros((HEAD_DIM,), jnp.float32)
        ln_v_g = jnp.ones((HEAD_DIM,), jnp.float32)
        ln_v_b = jnp.zeros((HEAD_DIM,), jnp.float32)
        return {'seq': seq, 'wq': wq, 'wk': wk, 'wv': wv, 'wo': wo, 'bo': bo, 'ln_k_g': ln_k_g, 'ln_k_b': ln_k_b, 'ln_v_g': ln_v_g, 'ln_v_b': ln_v_b}
    _L0_mix_all = _L0_mix_setup()
    _L0_mix_in = {k: v for k, v in _L0_mix_all.items() if k in ('wq', 'wk', 'wv', 'wo', 'bo', 'ln_k_g', 'ln_k_b', 'ln_v_g', 'ln_v_b')}
    del _L0_mix_all

    def _L0_ffn_setup():
        import jax, jax.numpy as jnp
        import numpy as np
        NUM_EXPERTS = 8
        TOP_K = 2
        B, S, D = (8, 1024, 256)

        def _moe(tokens, router_w, w1, b1, w2, b2):
            N = tokens.shape[0]
            E = router_w.shape[0]
            logits = tokens.astype(jnp.float32) @ router_w.astype(jnp.float32).T
            probs = jax.nn.softmax(logits, axis=-1)
            rw, re = jax.lax.top_k(probs, TOP_K)
            if TOP_K > 1:
                rw = rw / jnp.maximum(rw.sum(-1, keepdims=True), 1e-12)
            rw = rw.astype(tokens.dtype)
            combine = jnp.zeros((N, E), tokens.dtype).at[jnp.arange(N)[:, None], re].set(rw)
            out = tokens
            for e in range(E):
                h = jax.nn.gelu(tokens @ w1[e] + b1[e], approximate=False)
                y = h @ w2[e] + b2[e]
                out = out + combine[:, e:e + 1] * y
            return out
        key = jax.random.key(seed)
        ks = jax.random.split(key, 4)
        scale = 1.0 / np.sqrt(D).astype(np.float32)
        return {'input_embeddings': jax.random.normal(ks[0], (B, S, D), jnp.float32), 'router_w': jax.random.normal(ks[1], (NUM_EXPERTS, D), jnp.float32) * scale, 'w1': jax.random.normal(ks[2], (NUM_EXPERTS, D, D), jnp.float32) * scale, 'b1': jnp.zeros((NUM_EXPERTS, D), jnp.float32), 'w2': jax.random.normal(ks[3], (NUM_EXPERTS, D, D), jnp.float32) * scale, 'b2': jnp.zeros((NUM_EXPERTS, D), jnp.float32)}
    _L0_ffn_all = _L0_ffn_setup()
    _L0_ffn_in = {k: v for k, v in _L0_ffn_all.items() if k in ('router_w', 'w1', 'b1', 'w2', 'b2')}
    del _L0_ffn_all

    def _L1_gnn_setup():
        import jax, jax.numpy as jnp
        import numpy as np
        N_NODES = 1250
        N_EDGES = 40000
        DIM = 256
        key = jax.random.key(seed)
        ks = jax.random.split(key, 6)
        h = jax.random.normal(ks[0], (N_NODES, DIM), dtype=jnp.float32)
        edge_index = jax.random.randint(ks[1], (2, N_EDGES), 0, N_NODES, dtype=jnp.int64)
        edge_rel_emb = jax.random.normal(ks[2], (N_EDGES, DIM), dtype=jnp.float32)
        s = 1.0 / np.sqrt(DIM)
        W1 = jax.random.normal(ks[3], (DIM, DIM), dtype=jnp.float32) * s
        b1 = jnp.zeros((DIM,), dtype=jnp.float32)
        W2 = jax.random.normal(ks[4], (DIM, DIM), dtype=jnp.float32) * s
        b2 = jnp.zeros((DIM,), dtype=jnp.float32)
        return {'h': h, 'edge_index': edge_index, 'edge_rel_emb': edge_rel_emb, 'W1': W1, 'b1': b1, 'W2': W2, 'b2': b2, 'num_nodes': N_NODES}
    _L1_gnn_all = _L1_gnn_setup()
    _L1_gnn_in = {k: v for k, v in _L1_gnn_all.items() if k in ('W1', 'b1', 'W2', 'b2')}
    del _L1_gnn_all

    def _L1_mix_setup():
        import jax, jax.numpy as jnp
        import numpy as np
        HEADS = 8
        DIM_HEAD = 32
        SCALE = DIM_HEAD ** (-0.5)
        EPS = 1e-05

        def _layernorm_gamma(x, gamma):
            mu = jnp.mean(x, axis=-1, keepdims=True)
            var = jnp.var(x, axis=-1, keepdims=True)
            return (x - mu) * jax.lax.rsqrt(var + EPS) * gamma
        key = jax.random.key(seed)
        k1, k2, k3 = jax.random.split(key, 3)
        B, N, D = (8, 2048, 256)
        hidden = HEADS * DIM_HEAD
        x = jax.random.normal(k1, (B, N, D), dtype=jnp.float32)
        Wqkv = jax.random.normal(k2, (D, 3 * hidden), dtype=jnp.float32) * D ** (-0.5)
        Wout = jax.random.normal(k3, (hidden, D), dtype=jnp.float32) * hidden ** (-0.5)
        gamma = jnp.ones((D,), dtype=jnp.float32)
        return {'x': x, 'Wqkv': Wqkv, 'Wout': Wout, 'gamma': gamma}
    _L1_mix_all = _L1_mix_setup()
    _L1_mix_in = {k: v for k, v in _L1_mix_all.items() if k in ('Wqkv', 'Wout', 'gamma')}
    del _L1_mix_all

    def _L1_ffn_setup():
        import jax, jax.numpy as jnp
        import numpy as np
        C = 256
        HID = 1024
        E = 8
        TEMP = 1.0
        key = jax.random.key(seed)
        ks = jax.random.split(key, 7)
        x = jax.random.normal(ks[0], (8, 2048, C), dtype=jnp.float32)
        W1 = jax.random.normal(ks[1], (C, HID), dtype=jnp.float32) * 0.02
        b1 = jnp.zeros((HID,), dtype=jnp.float32)
        Wg = jax.random.normal(ks[2], (HID, E), dtype=jnp.float32) * 0.02
        bg = jnp.zeros((E,), dtype=jnp.float32)
        Wd = jax.random.normal(ks[3], (E, HID, C), dtype=jnp.float32) * 0.02
        bd = jnp.zeros((E, C), dtype=jnp.float32)
        return {'x': x, 'W1': W1, 'b1': b1, 'Wg': Wg, 'bg': bg, 'Wd': Wd, 'bd': bd}
    _L1_ffn_all = _L1_ffn_setup()
    _L1_ffn_in = {k: v for k, v in _L1_ffn_all.items() if k in ('W1', 'b1', 'Wg', 'bg', 'Wd', 'bd')}
    del _L1_ffn_all
    return {'x': x, 'src': src, 'dst': dst, 'edge_attr_256': edge_attr_256, 'L0_gnn_W_l_f': _L0_gnn_in['W_l_f'], 'L0_gnn_b_l_f': _L0_gnn_in['b_l_f'], 'L0_gnn_W_r_f': _L0_gnn_in['W_r_f'], 'L0_gnn_W_l_b': _L0_gnn_in['W_l_b'], 'L0_gnn_b_l_b': _L0_gnn_in['b_l_b'], 'L0_gnn_W_r_b': _L0_gnn_in['W_r_b'], 'L0_gnn_gamma': _L0_gnn_in['gamma'], 'L0_gnn_beta': _L0_gnn_in['beta'], 'L0_mix_wq': _L0_mix_in['wq'], 'L0_mix_wk': _L0_mix_in['wk'], 'L0_mix_wv': _L0_mix_in['wv'], 'L0_mix_wo': _L0_mix_in['wo'], 'L0_mix_bo': _L0_mix_in['bo'], 'L0_mix_ln_k_g': _L0_mix_in['ln_k_g'], 'L0_mix_ln_k_b': _L0_mix_in['ln_k_b'], 'L0_mix_ln_v_g': _L0_mix_in['ln_v_g'], 'L0_mix_ln_v_b': _L0_mix_in['ln_v_b'], 'L0_ffn_router_w': _L0_ffn_in['router_w'], 'L0_ffn_w1': _L0_ffn_in['w1'], 'L0_ffn_b1': _L0_ffn_in['b1'], 'L0_ffn_w2': _L0_ffn_in['w2'], 'L0_ffn_b2': _L0_ffn_in['b2'], 'L1_gnn_W1': _L1_gnn_in['W1'], 'L1_gnn_b1': _L1_gnn_in['b1'], 'L1_gnn_W2': _L1_gnn_in['W2'], 'L1_gnn_b2': _L1_gnn_in['b2'], 'L1_mix_Wqkv': _L1_mix_in['Wqkv'], 'L1_mix_Wout': _L1_mix_in['Wout'], 'L1_mix_gamma': _L1_mix_in['gamma'], 'L1_ffn_W1': _L1_ffn_in['W1'], 'L1_ffn_b1': _L1_ffn_in['b1'], 'L1_ffn_Wg': _L1_ffn_in['Wg'], 'L1_ffn_bg': _L1_ffn_in['bg'], 'L1_ffn_Wd': _L1_ffn_in['Wd'], 'L1_ffn_bd': _L1_ffn_in['bd']}

def reference(x, src, dst, edge_attr_256, L0_gnn_W_l_f, L0_gnn_b_l_f, L0_gnn_W_r_f, L0_gnn_W_l_b, L0_gnn_b_l_b, L0_gnn_W_r_b, L0_gnn_gamma, L0_gnn_beta, L0_mix_wq, L0_mix_wk, L0_mix_wv, L0_mix_wo, L0_mix_bo, L0_mix_ln_k_g, L0_mix_ln_k_b, L0_mix_ln_v_g, L0_mix_ln_v_b, L0_ffn_router_w, L0_ffn_w1, L0_ffn_b1, L0_ffn_w2, L0_ffn_b2, L1_gnn_W1, L1_gnn_b1, L1_gnn_W2, L1_gnn_b2, L1_mix_Wqkv, L1_mix_Wout, L1_mix_gamma, L1_ffn_W1, L1_ffn_b1, L1_ffn_Wg, L1_ffn_bg, L1_ffn_Wd, L1_ffn_bd):
    import jax
    import jax.numpy as jnp

    def _L0_gnn_ref(x, edge_index, W_l_f, b_l_f, W_r_f, W_l_b, b_l_b, W_r_b, gamma, beta):
        import jax, jax.numpy as jnp
        import numpy as np
        N_NODES = 2500
        BN_EPS = 1e-05

        def _sage(x, src, dst, W_l, b_l, W_r):
            msg_sum = jax.ops.segment_sum(x[src], dst, num_segments=N_NODES)
            cnt = jax.ops.segment_sum(jnp.ones((src.shape[0],), x.dtype), dst, num_segments=N_NODES)
            aggr = msg_sum / jnp.maximum(cnt, 1.0)[:, None]
            return aggr @ W_l.T + b_l + x @ W_r.T
        src, dst = (edge_index[0], edge_index[1])
        h_fwd = _sage(x, src, dst, W_l_f, b_l_f, W_r_f)
        h_bwd = _sage(x, dst, src, W_l_b, b_l_b, W_r_b)
        h = jnp.concatenate([h_fwd, h_bwd], axis=-1)
        mean = jnp.mean(h, axis=0)
        var = jnp.mean(jnp.square(h - mean), axis=0)
        h = (h - mean) * jax.lax.rsqrt(var + BN_EPS) * gamma + beta
        return jax.nn.relu(h)

    def _L0_mix_ref(seq, wq, wk, wv, wo, bo, ln_k_g, ln_k_b, ln_v_g, ln_v_b):
        import jax, jax.numpy as jnp
        import numpy as np
        import math
        EMBED = 256
        HEADS = 4
        HEAD_DIM = EMBED // HEADS
        OUT_DIM = 256
        LN_EPS = 1e-05

        def _qkv_init(key):
            spread = math.sqrt(3.0 / EMBED)
            gain, delta = (0.01, 0.01)
            w = jax.random.uniform(key, (EMBED, EMBED), minval=-spread, maxval=spread) * gain
            return w + delta * jnp.eye(EMBED, dtype=w.dtype)

        def _layer_norm(x, g, b):
            mu = jnp.mean(x, axis=-1, keepdims=True)
            var = jnp.mean(jnp.square(x - mu), axis=-1, keepdims=True)
            return (x - mu) * jax.lax.rsqrt(var + LN_EPS) * g + b

        def _split_heads(x, B, S):
            return x.reshape(B, S, HEADS, HEAD_DIM).transpose(0, 2, 1, 3)
        B, S, _ = seq.shape
        q = _split_heads(seq @ wq.T, B, S)
        k = _split_heads(seq @ wk.T, B, S)
        v = _split_heads(seq @ wv.T, B, S)
        k = _layer_norm(k, ln_k_g, ln_k_b)
        v = _layer_norm(v, ln_v_g, ln_v_b)
        kv = jnp.einsum('bhsd,bhse->bhde', k, v) / S
        ga = jnp.einsum('bhsd,bhde->bhse', q, kv)
        ga = ga.transpose(0, 2, 1, 3).reshape(B, S, EMBED)
        return ga @ wo.T + bo

    def _L0_ffn_ref(input_embeddings, router_w, w1, b1, w2, b2):
        import jax, jax.numpy as jnp
        import numpy as np
        NUM_EXPERTS = 8
        TOP_K = 2
        B, S, D = (8, 1024, 256)

        def _moe(tokens, router_w, w1, b1, w2, b2):
            N = tokens.shape[0]
            E = router_w.shape[0]
            logits = tokens.astype(jnp.float32) @ router_w.astype(jnp.float32).T
            probs = jax.nn.softmax(logits, axis=-1)
            rw, re = jax.lax.top_k(probs, TOP_K)
            if TOP_K > 1:
                rw = rw / jnp.maximum(rw.sum(-1, keepdims=True), 1e-12)
            rw = rw.astype(tokens.dtype)
            combine = jnp.zeros((N, E), tokens.dtype).at[jnp.arange(N)[:, None], re].set(rw)
            out = tokens
            for e in range(E):
                h = jax.nn.gelu(tokens @ w1[e] + b1[e], approximate=False)
                y = h @ w2[e] + b2[e]
                out = out + combine[:, e:e + 1] * y
            return out
        b, s, d = input_embeddings.shape
        tokens = input_embeddings.reshape(b * s, d)
        return _moe(tokens, router_w, w1, b1, w2, b2).reshape(b, s, d)

    def _L1_gnn_ref(h, edge_index, edge_rel_emb, W1, b1, W2, b2, num_nodes):
        import jax, jax.numpy as jnp
        import numpy as np
        N_NODES = 1250
        N_EDGES = 40000
        DIM = 256
        src, dst = (edge_index[0], edge_index[1])
        x = h[src] + edge_rel_emb
        hid = jax.nn.relu(x @ W1 + b1)
        msg = hid @ W2 + b2
        agg = jax.ops.segment_sum(msg, dst, num_segments=num_nodes)
        return h + agg

    def _L1_mix_ref(x, Wqkv, Wout, gamma):
        import jax, jax.numpy as jnp
        import numpy as np
        HEADS = 8
        DIM_HEAD = 32
        SCALE = DIM_HEAD ** (-0.5)
        EPS = 1e-05

        def _layernorm_gamma(x, gamma):
            mu = jnp.mean(x, axis=-1, keepdims=True)
            var = jnp.var(x, axis=-1, keepdims=True)
            return (x - mu) * jax.lax.rsqrt(var + EPS) * gamma
        B, N, D = x.shape
        qkv = x @ Wqkv
        q, k, v = jnp.split(qkv, 3, axis=-1)

        def to_heads(t):
            return t.reshape(B, N, HEADS, DIM_HEAD).transpose(0, 2, 1, 3)
        q, k, v = map(to_heads, (q, k, v))
        q = jax.nn.softmax(q, axis=-1) * SCALE
        k = jax.nn.softmax(k, axis=2)
        context = jnp.einsum('bhnd,bhne->bhde', k, v)
        out = jnp.einsum('bhde,bhnd->bhne', context, q)
        out = out.transpose(0, 2, 1, 3).reshape(B, N, HEADS * DIM_HEAD)
        out = out @ Wout
        return _layernorm_gamma(out, gamma)

    def _L1_ffn_ref(x, W1, b1, Wg, bg, Wd, bd):
        import jax, jax.numpy as jnp
        import numpy as np
        C = 256
        HID = 1024
        E = 8
        TEMP = 1.0
        orig_shape = x.shape
        xf = x.reshape(-1, orig_shape[-1])
        H = jax.nn.gelu(xf @ W1 + b1, approximate=False)
        probs = jax.nn.softmax((H @ Wg + bg) / TEMP, axis=-1)
        assign = jnp.argmax(probs, axis=-1)
        out = jnp.zeros_like(xf)
        for e in range(Wd.shape[0]):
            y = H @ Wd[e] + bd[e]
            sel = (assign == e)[:, None]
            out = out + jnp.where(sel, probs[:, e:e + 1] * y, 0.0)
        return out.reshape(orig_shape)
    edge_index = jnp.stack([src, dst])
    xn = _layernorm(x, axis=-1)
    x = x + _L0_gnn_ref(xn, edge_index, L0_gnn_W_l_f, L0_gnn_b_l_f, L0_gnn_W_r_f, L0_gnn_W_l_b, L0_gnn_b_l_b, L0_gnn_W_r_b, L0_gnn_gamma, L0_gnn_beta) + _L0_mix_ref(xn[None], L0_mix_wq, L0_mix_wk, L0_mix_wv, L0_mix_wo, L0_mix_bo, L0_mix_ln_k_g, L0_mix_ln_k_b, L0_mix_ln_v_g, L0_mix_ln_v_b)[0]
    x = x + _L0_ffn_ref(_layernorm(x, axis=-1)[None], L0_ffn_router_w, L0_ffn_w1, L0_ffn_b1, L0_ffn_w2, L0_ffn_b2)[0]
    xn = _layernorm(x, axis=-1)
    x = x + _L1_gnn_ref(xn, edge_index, edge_attr_256, L1_gnn_W1, L1_gnn_b1, L1_gnn_W2, L1_gnn_b2, 2500) + _L1_mix_ref(xn[None], L1_mix_Wqkv, L1_mix_Wout, L1_mix_gamma)[0]
    x = x + _L1_ffn_ref(_layernorm(x, axis=-1)[None], L1_ffn_W1, L1_ffn_b1, L1_ffn_Wg, L1_ffn_bg, L1_ffn_Wd, L1_ffn_bd)[0]
    return x

_drawn_inputs = setup_inputs


def setup_inputs(seed=0):
    import zlib

    import numpy as np

    out = dict(_drawn_inputs(seed))
    spreads = {'L0_gnn_b_l_f': (0.0, 0.8),
     'L0_gnn_b_l_b': (0.0, 0.8),
     'L0_gnn_gamma': (1.0, 0.2),
     'L0_gnn_beta': (0.0, 0.1),
     'L0_mix_ln_k_g': (1.0, 0.6),
     'L0_mix_ln_k_b': (0.0, 0.8),
     'L0_mix_ln_v_g': (1.0, 0.6),
     'L0_mix_ln_v_b': (0.0, 0.8),
     'L0_ffn_b1': (0.0, 0.578),
     'L0_ffn_b2': (0.0, 0.314),
     'L1_gnn_b1': (0.0, 0.1),
     'L1_gnn_b2': (0.0, 0.1),
     'L1_mix_gamma': (1.0, 0.6),
     'L1_ffn_b1': (0.0, 0.8),
     'L1_ffn_bg': (0.0, 0.8),
     'L1_ffn_bd': (0.0, 0.8)}
    factors = {'L0_mix_wq': 8.0,
     'L0_mix_wk': 8.0,
     'L0_mix_wv': 8.0,
     'L0_mix_wo': 8.0,
     'L1_ffn_W1': 8.0,
     'L1_ffn_Wg': 8.0,
     'L1_ffn_Wd': 8.0}
    for name, (base, spread) in spreads.items():
        noise = np.random.default_rng([zlib.crc32(name.encode()), seed]).standard_normal(out[name].shape)
        drawn = base * np.exp(spread * noise) if base else spread * noise
        out[name] = jnp.asarray(drawn.astype(out[name].dtype))
    for name, factor in factors.items():
        out[name] = (out[name] * factor).astype(out[name].dtype)
    return out
```

```python
from contextlib import ExitStack

import concourse.bass as bass
from concourse import mybir

F32 = mybir.dt.float32
BF16 = mybir.dt.bfloat16
I32 = mybir.dt.int32
I16 = mybir.dt.int16
ALU = mybir.AluOpType
ACT = mybir.ActivationFunctionType
AX = mybir.AxisListType

NODES, DIM, EDGES = 2500, 256, 40000
P = 125
TILES = NODES // P
KB = DIM // 128
CHUNK = 4 * P
CHUNKS = NODES // CHUNK
EDGE_TILES = EDGES // P
RANGE_ROWS = 80
HEADS0, HEADS1, EXPERTS, HIDDEN = 4, 8, 8, 1024
HEAD0, HEAD1 = DIM // HEADS0, DIM // HEADS1
GROUP = 4
LN_EPS = 1e-5


class Chain:

    def __init__(self, sem):
        self.sem, self.n = sem, 0

    def tick(self, instruction):
        self.n += 1
        instruction.then_inc(self.sem, 1)

    def wait(self, engine):
        engine.wait_ge(self.sem, self.n)


class Program:

    def __init__(self, nc, ctx):
        self.nc, self.ctx = nc, ctx
        self.used, self.free = [], []

    def sb(self, name, shape, dtype=F32, scope=None):
        return (scope or self.ctx).enter_context(self.nc.sbuf_tensor(name, shape, dtype))

    def ps(self, name, shape, dtype=F32, scope=None):
        return (scope or self.ctx).enter_context(self.nc.psum_tensor(name, shape, dtype))

    def sem(self, name):
        sem = self.free.pop() if self.free else self.ctx.enter_context(self.nc.semaphore(name))
        self.used.append(sem)
        return sem

    def clear_semaphores(self):
        done, self.used = self.used, []
        with self.nc.Block() as block:
            for n, engine in enumerate((block.sync, block.gpsimd, block.scalar, block.vector, block.tensor)):
                @engine
                def _(e, share=done[n::5]):
                    for sem in share:
                        e.sem_clear(sem)
        self.free = done + self.free


def row(x, t):
    return x[:, bass.ds(t, 1), :].rearrange("p a d -> p (a d)")


def inverse_root(dve, nc, chain, root, value, work):
    chain.tick(nc.vector.reciprocal(root[:], root[:]))
    chain.wait(dve)
    chain.tick(nc.vector.tensor_tensor(work[:], root[:], root[:], ALU.mult))
    chain.wait(dve)
    chain.tick(nc.vector.scalar_tensor_tensor(work[:], work[:], -0.5, value[:], ALU.mult, ALU.mult))
    chain.wait(dve)
    chain.tick(nc.vector.scalar_tensor_tensor(root[:], work[:], 1.5, root[:], ALU.add, ALU.mult))
    chain.wait(dve)


def constants(p, c):
    nc = p.nc
    c.ident = p.sb("ident", [128, 128])
    c.ones = p.sb("ones", [128, 128])
    c.iota_node_i = p.sb("iota_node_i", [P, NODES], I16)
    c.iota_tile_i = p.sb("iota_tile_i", [P, P], I16)
    c.iota_tile = p.sb("iota_tile", [P, P])
    made = p.sem("constants_made")
    with nc.Block() as block:
        @block.gpsimd
        def _(pool):
            nc.gpsimd.memset(c.ident[:], 0.0)
            nc.gpsimd.memset(c.ones[:], 1.0)
            nc.gpsimd.iota(c.iota_node_i[:], [[1, NODES]], base=0, channel_multiplier=0)
            nc.gpsimd.iota(c.iota_tile_i[:], [[1, P]], base=0, channel_multiplier=0).then_inc(made, 1)
            pool.wait_ge(made, 1)
            nc.gpsimd.affine_select(out=c.ident[:], in_=c.ident[:], compare_op=ALU.not_equal, fill=1.0,
                                    base=0, pattern=[[-1, 128]], channel_multiplier=1)
            nc.gpsimd.tensor_copy(c.iota_tile[:], c.iota_tile_i[:]).then_inc(made, 1)


def layer_norm(p, c, name, x, xn, xn_T, xn_dram=None):
    nc = p.nc
    with ExitStack() as scope:
        stats = p.sb(f"{name}_stats", [P, TILES * 6], scope=scope)
        mean = p.sb(f"{name}_mean", [P, TILES], scope=scope)
        var = p.sb(f"{name}_var", [P, TILES], scope=scope)
        half = p.sb(f"{name}_half", [P, TILES], scope=scope)
        std = p.sb(f"{name}_std", [P, TILES], scope=scope)
        turned = p.ps(f"{name}_turned", [128, 4, 512], scope=scope)
        chain = Chain(p.sem(f"{name}_chain"))
        var_ready, std_ready = p.sem(f"{name}_var_ready"), p.sem(f"{name}_std_ready")
        normed, transposed, copied = p.sem(f"{name}_normed"), p.sem(f"{name}_transposed"), p.sem(f"{name}_copied")
        stored, measured = p.sem(f"{name}_stored"), p.sem(f"{name}_measured")
        s = stats[:].rearrange("p (t k) -> p k t", k=6)
        with nc.Block() as block:
            @block.vector
            def _(dve):
                with dve.Fori(0, TILES) as t:
                    nc.vector.bn_stats(stats[:, bass.ds(t * 6, 6)], row(x, t)).then_inc(measured, 1)
                dve.wait_ge(measured, TILES)
                chain.wait(dve)
                nc.vector.tensor_tensor(half[:], s[:, 1, :], s[:, 4, :], ALU.subtract)
                nc.vector.tensor_tensor(mean[:], s[:, 1, :], s[:, 4, :], ALU.add)
                chain.tick(nc.vector.tensor_tensor(var[:], s[:, 2, :], s[:, 5, :], ALU.add))
                chain.wait(dve)
                nc.vector.tensor_scalar(mean[:], mean[:], 0.5, None, ALU.mult)
                chain.tick(nc.vector.scalar_tensor_tensor(half[:], half[:], 0.25, half[:], ALU.mult, ALU.mult))
                chain.wait(dve)
                chain.tick(nc.vector.scalar_tensor_tensor(var[:], var[:], 1.0 / DIM, half[:], ALU.mult, ALU.add))
                chain.wait(dve)
                nc.vector.tensor_scalar(var[:], var[:], LN_EPS, None, ALU.add).then_inc(var_ready, 1)
                dve.wait_ge(std_ready, 1)
                inverse_root(dve, nc, chain, std, var, half)
                with dve.Fori(0, TILES) as t:
                    nc.vector.tensor_scalar(xn[:, bass.ds(t, 1), 0:DIM].rearrange("p a d -> p (a d)"), row(x, t),
                                            mean[:, bass.ds(t, 1)], std[:, bass.ds(t, 1)],
                                            ALU.subtract, ALU.mult).then_inc(normed, 1)

            @block.tensor
            def _(pe):
                for t in range(TILES):
                    pe.wait_ge(normed, t + 1)
                    if t >= 4:
                        pe.wait_ge(copied, t - 3)
                    for k in range(KB):
                        last = nc.tensor.transpose(turned[:, t % 4, k * P:(k + 1) * P],
                                                   xn[:, t, k * 128:(k + 1) * 128], c.ident[:P, :P])
                    last.then_inc(transposed, 1)

            @block.scalar
            def _(act):
                act.wait_ge(var_ready, 1)
                nc.scalar.activation(std[:], var[:], ACT.Sqrt).then_inc(std_ready, 1)
                with act.Fori(0, TILES) as t:
                    act.wait_ge(transposed, t + 1)
                    nc.scalar.activation(xn_T[:, :, bass.ds(t * P, P)],
                                         turned[:, bass.ds(t % 4, 1), 0:KB * P].rearrange("p a (k n) -> p (a k) n", k=KB),
                                         ACT.Copy).then_inc(copied, 1)

            @block.sync
            def _(sp):
                if xn_dram is not None:
                    sp.wait_ge(normed, TILES)
                    sp.dma_start(xn_dram.rearrange("(t p) d -> p t d", p=P), xn[:, :, 0:DIM]).then_inc(stored, 16)
                    sp.wait_ge(stored, 16)


def edge_ranges(p, name, A, SUB):
    nc = p.nc
    BLOCKS = EDGE_TILES // SUB
    ROWS_IN_RANGES, PER_ROW = RANGE_ROWS, BLOCKS // RANGE_ROWS
    ranges = p.sb(f"{name}_ranges", [1, 3 * TILES], I32)
    low_dram = nc.dram_tensor(f"{name}_low_dram", [BLOCKS], F32).ap()
    high_dram = nc.dram_tensor(f"{name}_high_dram", [BLOCKS], F32).ap()
    ranges_dram = nc.dram_tensor(f"{name}_ranges_dram", [TILES, 3], I32).ap()
    with ExitStack() as scope:
        dst = p.sb(f"{name}_dst_by_block", [ROWS_IN_RANGES, PER_ROW, SUB * P], I32, scope)
        low = p.sb(f"{name}_block_low", [ROWS_IN_RANGES, PER_ROW], F32, scope)
        high = p.sb(f"{name}_block_high", [ROWS_IN_RANGES, PER_ROW], F32, scope)
        lows = p.sb(f"{name}_lows", [TILES, BLOCKS], F32, scope)
        highs = p.sb(f"{name}_highs", [TILES, BLOCKS], F32, scope)
        up_i = p.sb(f"{name}_up_i", [TILES, BLOCKS], I32, scope)
        up = p.sb(f"{name}_up", [TILES, BLOCKS], F32, scope)
        down = p.sb(f"{name}_down", [TILES, BLOCKS], F32, scope)
        start_i = p.sb(f"{name}_tile_start_i", [TILES, 1], I32, scope)
        start = p.sb(f"{name}_tile_start", [TILES, 1], F32, scope)
        end = p.sb(f"{name}_tile_end", [TILES, 1], F32, scope)
        earlier = p.sb(f"{name}_earlier", [TILES, TILES], F32, scope)
        first = p.sb(f"{name}_first", [TILES, 1], F32, scope)
        stop = p.sb(f"{name}_stop", [TILES, 1], F32, scope)
        found = p.sb(f"{name}_found", [TILES, 3], F32, scope)
        found_i = p.sb(f"{name}_found_i", [TILES, 3], I32, scope)
        base = p.ps(f"{name}_base", [TILES, 1], F32, scope)
        loaded, reduced, stored = p.sem(f"{name}_r_loaded"), p.sem(f"{name}_r_reduced"), p.sem(f"{name}_r_stored")
        made, counted, summed = p.sem(f"{name}_r_made"), p.sem(f"{name}_r_counted"), p.sem(f"{name}_r_summed")
        ready, kept = p.sem(f"{name}_r_ready"), p.sem(f"{name}_r_kept")
        chain = Chain(p.sem(f"{name}_r_chain"))
        with nc.Block() as block:
            @block.sync
            def _(sp):
                sp.dma_start(dst[:], A["dst_blocks"].rearrange("p (b e) -> p b e", b=PER_ROW)).then_inc(loaded, 16)
                sp.wait_ge(reduced, 1)
                sp.dma_start(low_dram.rearrange("(p b) -> p b", b=PER_ROW), low[:]).then_inc(stored, 16)
                sp.dma_start(high_dram.rearrange("(p b) -> p b", b=PER_ROW), high[:]).then_inc(stored, 16)
                sp.wait_ge(stored, 32)
                sp.dma_start(lows[:], low_dram.partition_broadcast(TILES)).then_inc(loaded, 16)
                sp.dma_start(highs[:], high_dram.partition_broadcast(TILES)).then_inc(loaded, 16)
                sp.wait_ge(ready, 1)
                sp.dma_start(ranges_dram, found_i[:]).then_inc(stored, 16)
                sp.wait_ge(stored, 48)
                sp.dma_start(ranges[:], ranges_dram.rearrange("t k -> (t k)").unsqueeze(0)).then_inc(kept, 16)
                sp.wait_ge(kept, 16)

            @block.gpsimd
            def _(pool):
                nc.gpsimd.iota(up_i[:], [[1, BLOCKS]], base=1, channel_multiplier=0)
                nc.gpsimd.iota(start_i[:], [[0, 1]], base=0, channel_multiplier=P)
                nc.gpsimd.memset(earlier[:], 1.0).then_inc(made, 1)
                pool.wait_ge(made, 1)
                nc.gpsimd.affine_select(out=earlier[:], in_=earlier[:], compare_op=ALU.is_gt, fill=0.0,
                                        base=0, pattern=[[1, TILES]], channel_multiplier=-1).then_inc(made, 1)

            @block.vector
            def _(dve):
                dve.wait_ge(loaded, 16)
                nc.vector.tensor_reduce(low[:], dst[:], AX.X, ALU.min)
                nc.vector.tensor_reduce(high[:], dst[:], AX.X, ALU.max).then_inc(reduced, 1)
                dve.wait_ge(made, 2)
                nc.vector.tensor_copy(up[:], up_i[:])
                chain.tick(nc.vector.tensor_copy(start[:], start_i[:]))
                chain.wait(dve)
                nc.vector.tensor_scalar(down[:], up[:], -1.0, float(BLOCKS + 1), ALU.mult, ALU.add)
                chain.tick(nc.vector.tensor_scalar(end[:], start[:], float(P - 1), None, ALU.add))
                dve.wait_ge(loaded, 48)
                chain.wait(dve)
                nc.vector.scalar_tensor_tensor(highs[:], highs[:], start[:], down[:], ALU.is_ge, ALU.mult)
                chain.tick(nc.vector.scalar_tensor_tensor(lows[:], lows[:], end[:], up[:], ALU.is_le, ALU.mult))
                chain.wait(dve)
                nc.vector.tensor_reduce(first[:], highs[:], AX.X, ALU.max)
                chain.tick(nc.vector.tensor_reduce(stop[:], lows[:], AX.X, ALU.max))
                chain.wait(dve)
                chain.tick(nc.vector.tensor_scalar(first[:], first[:], -1.0, float(BLOCKS), ALU.mult, ALU.add))
                chain.wait(dve)
                chain.tick(nc.vector.tensor_scalar(found[:, 0:1], first[:], float(BLOCKS - 1), None, ALU.min))
                chain.wait(dve)
                chain.tick(nc.vector.tensor_tensor(found[:, 1:2], stop[:], found[:, 0:1], ALU.subtract))
                chain.wait(dve)
                nc.vector.tensor_scalar(found[:, 1:2], found[:, 1:2], 1.0, None, ALU.max).then_inc(counted, 1)
                dve.wait_ge(summed, 1)
                chain.tick(nc.vector.tensor_copy(found[:, 2:3], base[:]))
                chain.wait(dve)
                nc.vector.tensor_copy(found_i[:], found[:]).then_inc(ready, 1)

            @block.tensor
            def _(pe):
                pe.wait_ge(made, 2)
                pe.wait_ge(counted, 1)
                nc.tensor.matmul(base[:], earlier[:], found[:, 1:2], start=True, stop=True).then_inc(summed, 1)
    return ranges


def load_range(engine, ranges, t, SUB):
    BLOCKS = EDGE_TILES // SUB
    return (engine.value_load(ranges[0:1, bass.ds(t * 3, 1)], min_val=0, max_val=BLOCKS - 1),
            engine.value_load(ranges[0:1, bass.ds(t * 3 + 1, 1)], min_val=1, max_val=BLOCKS),
            engine.value_load(ranges[0:1, bass.ds(t * 3 + 2, 1)], min_val=0, max_val=BLOCKS * TILES))


def neighbour_means(p, c, ranges, SUB, xn, src, dst, mean_in, sum_out, in_degree):
    nc = p.nc
    W = DIM + 1
    BLOCKS = EDGE_TILES // SUB
    with ExitStack() as scope:
        sb = lambda name, shape, dtype=F32: p.sb(name, shape, dtype, scope)
        hot_src = sb("hot_src", [P, SUB, NODES], BF16)
        hot_dst = sb("hot_dst", [P, SUB, P], BF16)
        adj = sb("adj", [P, GROUP, NODES])
        adj_T = sb("adj_T", [P, TILES, P])
        dst_f = sb("dst_f", [P, EDGES // P])
        src_f = sb("src_f", [P, EDGES // P])
        degree = sb("degree", [P, 1])
        degrees = sb("degrees", [P, TILES, 1])
        rows = p.ps("adj_rows", [P, CHUNKS, 512], scope=scope)
        turned = p.ps("adj_turned", [P, 2, 512], scope=scope)
        sum_in = p.ps("sum_in", [P, 512], scope=scope)
        hot_ready = [p.sem(f"nm_hot_ready{s}") for s in range(SUB)]
        hot_used = [p.sem(f"nm_hot_used{s}") for s in range(SUB)]
        rows_copied = p.sem("nm_rows_copied")
        turn_ready, turn_copied = p.sem("nm_turn_ready"), p.sem("nm_turn_copied")
        in_ready, in_copied = p.sem("nm_in_ready"), p.sem("nm_in_copied")
        out_ready, out_added = p.sem("nm_out_ready"), p.sem("nm_out_added")
        chain = Chain(p.sem("nm_chain"))
        deg_chain = p.sem("nm_degree")
        BATCH = 4
        BATCHES = TILES // BATCH

        with nc.Block() as block:
            @block.vector
            def _(dve):
                nc.vector.tensor_copy(src_f[:], src[:])
                nc.vector.tensor_copy(dst_f[:], dst[:])
                chain.tick(nc.vector.memset(sum_out[:], 0.0))
                chain.wait(dve)
                dve.sem_inc(in_copied, 1)
                dve.sem_inc(out_added, 1)

                def build(t):
                    lo, n, before = load_range(dve, ranges, t, SUB)
                    with dve.Fori(0, n) as i:
                        for s in range(SUB):
                            col = (lo + i).with_bounds(min_val=0, max_val=BLOCKS - 1) * SUB + s
                            dve.wait_ge(hot_used[s], before + i + 1)
                            nc.vector.tensor_scalar(hot_src[:, s, :], c.iota_node_i[:], src_f[:, bass.ds(col, 1)],
                                                    None, ALU.is_equal)
                            nc.vector.tensor_scalar(hot_dst[:, s, :], c.iota_node_i[:, bass.ds(t * P, P)],
                                                    dst_f[:, bass.ds(col, 1)], None,
                                                    ALU.is_equal).then_inc(hot_ready[s], 1)

                def finish_in(t, g, tt):
                    dve.wait_ge(in_ready, t + 1)
                    nc.vector.tensor_copy(in_degree[:, bass.ds(t, 1)], sum_in[:, DIM:W])
                    nc.vector.tensor_scalar(degree[:], sum_in[:, DIM:W], 1.0, None, ALU.max).then_inc(deg_chain, 1)
                    dve.wait_ge(deg_chain, t * 2 + 1)
                    nc.vector.reciprocal(degree[:], degree[:]).then_inc(deg_chain, 1)
                    dve.wait_ge(deg_chain, t * 2 + 2)
                    nc.vector.tensor_scalar(mean_in[:, bass.ds(t, 1), :].rearrange("p a d -> p (a d)"),
                                            sum_in[:, 0:DIM], degree[:], None, ALU.mult).then_inc(in_copied, 1)

                with dve.Fori(0, TILES // GROUP) as g:
                    build(g * GROUP)
                    for tt in range(GROUP):
                        if tt + 1 < GROUP:
                            build(g * GROUP + tt + 1)
                        finish_in(g * GROUP + tt, g, tt)
                    for s in range(TILES):
                        dve.wait_ge(out_ready, g * TILES + s + 1)
                        nc.vector.tensor_tensor(sum_out[:, s, :], rows[:, s % CHUNKS, 0:W], sum_out[:, s, :],
                                                ALU.add).then_inc(out_added, 1)
                dve.wait_ge(out_added, TILES * TILES // GROUP + 1)
                chain.tick(nc.vector.tensor_scalar(degrees[:], sum_out[:, :, DIM:W], 1.0, None, ALU.max))
                chain.wait(dve)
                chain.tick(nc.vector.reciprocal(degrees[:], degrees[:]))
                chain.wait(dve)
                nc.vector.tensor_tensor(sum_out[:, :, 0:DIM], sum_out[:, :, 0:DIM],
                                        degrees[:].broadcast_to([P, TILES, DIM]), ALU.mult)

            @block.tensor
            def _(pe):
                def build(t):
                    lo, n, before = load_range(pe, ranges, t, SUB)
                    pe.wait_ge(rows_copied, t + 1)
                    for q in range(CHUNKS):
                        nc.tensor.matmul(rows[:, q, 0:2], c.zero[:], c.zero[:, 0:2], start=True, stop=False,
                                         skip_group_check=True)
                    with pe.Fori(0, n) as i:
                        for s in range(SUB):
                            pe.wait_ge(hot_ready[s], before + i + 1)
                            for q in range(CHUNKS):
                                last = nc.tensor.matmul(rows[:, q, 0:CHUNK], hot_dst[:, s, :],
                                                        hot_src[:, s, q * CHUNK:(q + 1) * CHUNK],
                                                        start=False, stop=(s == SUB - 1), skip_group_check=True)
                            last.then_inc(hot_used[s], 1)

                def turn(t, tt, b):
                    n = t * BATCHES + b
                    pe.wait_ge(turn_copied, n + 2 if b == 0 else n + 1)
                    for j in range(BATCH):
                        s = b * BATCH + j
                        last = nc.tensor.transpose(turned[:, b % 2, j * P:(j + 1) * P],
                                                   adj[:, tt, s * P:(s + 1) * P], c.ident[:P, :P])
                    last.then_inc(turn_ready, 1)

                def sum_sources(t, tt):
                    pe.wait_ge(rows_copied, t + 2)
                    pe.wait_ge(in_copied, t + 1)
                    turn(t, tt, 0)
                    for b in range(BATCHES):
                        if b + 1 < BATCHES:
                            turn(t, tt, b + 1)
                        pe.wait_ge(turn_copied, t * BATCHES + b + 3)
                        for s in range(b * BATCH, (b + 1) * BATCH):
                            last = nc.tensor.matmul(sum_in[:, 0:W], adj_T[:, s, :], xn[:, s, :],
                                                    start=(s == 0), stop=(s == TILES - 1))
                    last.then_inc(in_ready, 1)

                for s in range(SUB):
                    pe.sem_inc(hot_used[s], 1)
                with pe.Fori(0, TILES // GROUP) as g:
                    build(g * GROUP)
                    for tt in range(GROUP):
                        if tt + 1 < GROUP:
                            build(g * GROUP + tt + 1)
                        sum_sources(g * GROUP + tt, tt)
                    pe.wait_ge(rows_copied, g * GROUP + GROUP + 1)
                    for s in range(TILES):
                        if s >= CHUNKS:
                            pe.wait_ge(out_added, g * TILES + s - CHUNKS + 2)
                        for tt in range(GROUP):
                            last = nc.tensor.matmul(rows[:, s % CHUNKS, 0:W], adj[:, tt, s * P:(s + 1) * P],
                                                    xn[:, bass.ds(g * GROUP + tt, 1), :],
                                                    start=(tt == 0), stop=(tt == GROUP - 1))
                        last.then_inc(out_ready, 1)
                    pe.wait_ge(out_added, g * TILES + TILES + 1)

            @block.scalar
            def _(act):
                def keep_rows(t, tt):
                    lo, n, before = load_range(act, ranges, t, SUB)
                    act.wait_ge(hot_used[SUB - 1], before + n + 1)
                    if tt == 0:
                        act.wait_ge(out_added, (t - tt) * (TILES // GROUP) + 1)
                    nc.scalar.activation(adj[:, tt, :].rearrange("p (q n) -> p q n", q=CHUNKS), rows[:, :, 0:CHUNK],
                                         ACT.Copy).then_inc(rows_copied, 1)

                def keep_turned(t):
                    for b in range(BATCHES):
                        act.wait_ge(turn_ready, t * BATCHES + b + 1)
                        act.wait_ge(in_copied, t + 1)
                        nc.scalar.activation(adj_T[:, b * BATCH:(b + 1) * BATCH, :],
                                             turned[:, b % 2, 0:BATCH * P].rearrange("p (j n) -> p j n", j=BATCH),
                                             ACT.Copy).then_inc(turn_copied, 1)

                act.sem_inc(rows_copied, 1)
                act.sem_inc(turn_copied, 2)
                with act.Fori(0, TILES // GROUP) as g:
                    keep_rows(g * GROUP, 0)
                    for tt in range(GROUP):
                        if tt + 1 < GROUP:
                            keep_rows(g * GROUP + tt + 1, tt + 1)
                        keep_turned(g * GROUP + tt)


def linear_attention(p, c, A, xn_T, mixer):
    nc = p.nc
    GROUPS = 2 * HEADS0
    with ExitStack() as scope:
        sb = lambda name, shape, dtype=F32: p.sb("la_" + name, shape, dtype, scope)
        w_kv = sb("w_kv", [128, KB, 2 * DIM])
        w_q = sb("w_q", [128, KB, DIM])
        w_o = sb("w_o", [128, KB, DIM])
        gain = sb("gain", [P, 2, HEAD0])
        shift = sb("shift", [P, 2, HEAD0])
        kv = sb("kv", [P, TILES, 2 * DIM])
        square = sb("square", [P, 2, 2 * DIM])
        total = sb("total", [P, GROUPS])
        var = sb("var", [P, TILES * GROUPS])
        std = sb("std", [P, TILES * GROUPS])
        work = sb("work", [P, TILES * GROUPS])
        heads_vk = sb("heads_vk", [128, KB, 128])
        kv_wo = sb("kv_wo", [128, KB, DIM])
        projected = p.ps("la_projected", [P, 2, 512], scope=scope)
        vk = p.ps("la_vk", [128, KB, 512], scope=scope)
        product = p.ps("la_product", [128, KB, 512], scope=scope)
        loaded, projected_ready, centred = p.sem("la_loaded"), p.sem("la_projected_ready"), p.sem("la_centred")
        squared, summed = p.sem("la_squared"), p.sem("la_summed")
        var_ready, std_ready, scaled, shifted = (p.sem("la_var_ready"), p.sem("la_std_ready"), p.sem("la_scaled"),
                                                 p.sem("la_shifted"))
        gained, vk_ready, heads_ready = p.sem("la_gained"), p.sem("la_vk_ready"), p.sem("la_heads_ready")
        kv_wo_ready, kv_wo_kept, mixer_ready = p.sem("la_kv_wo_ready"), p.sem("la_kv_wo_kept"), p.sem("la_mixer_ready")
        zeroed, totalled = p.sem("la_zeroed"), p.sem("la_totalled")
        chain = Chain(p.sem("la_chain"))
        by_head = lambda x: x.rearrange("p (h d) -> p h d", d=HEAD0)
        with nc.Block() as block:
            @block.sync
            def _(sp):
                sp.dma_start(w_kv[:, :, 0:DIM], A["wk_T"].rearrange("(k p) n -> p k n", p=128)).then_inc(loaded, 16)
                sp.dma_start(w_kv[:, :, DIM:], A["wv_T"].rearrange("(k p) n -> p k n", p=128)).then_inc(loaded, 16)
                sp.dma_start(w_q[:], A["wq"].rearrange("(k p) n -> p k n", p=128)).then_inc(loaded, 16)
                sp.dma_start(w_o[:], A["wo_T"].rearrange("(k p) n -> p k n", p=128)).then_inc(loaded, 16)
                for n, (g, b) in enumerate((("ln_k_g", "ln_k_b"), ("ln_v_g", "ln_v_b"))):
                    sp.dma_start(gain[:, n, :], A[g].partition_broadcast(P)).then_inc(loaded, 16)
                    sp.dma_start(shift[:, n, :], A[b].partition_broadcast(P)).then_inc(loaded, 16)
                sp.wait_ge(loaded, 8 * 16)

            @block.tensor
            def _(pe):
                pe.wait_ge(loaded, 8 * 16)
                for t in range(TILES):
                    if t >= 2:
                        pe.wait_ge(centred, t - 1)
                    for k in range(KB):
                        last = nc.tensor.matmul(projected[:, t % 2, :], xn_T[:, k, t * P:(t + 1) * P], w_kv[:, k, :],
                                                start=(k == 0), stop=(k == KB - 1))
                    last.then_inc(projected_ready, 1)
                for t in range(TILES):
                    pe.wait_ge(shifted, t + 1)
                    for b in range(KB):
                        last = nc.tensor.matmul(vk[:, b, 0:128], kv[:, t, DIM + b * 128:DIM + (b + 1) * 128],
                                                kv[:, t, b * 128:(b + 1) * 128], start=(t == 0), stop=(t == TILES - 1))
                last.then_inc(vk_ready, 1)
                pe.wait_ge(heads_ready, 1)
                for b in range(KB):
                    last = nc.tensor.matmul(product[:, b, 0:DIM], heads_vk[:, b, :], w_o[:, b, :], start=True, stop=True)
                last.then_inc(kv_wo_ready, 1)
                pe.wait_ge(kv_wo_kept, 1)
                for m in range(KB):
                    for b in range(KB):
                        last = nc.tensor.matmul(product[:, m, 0:DIM], w_q[:, b, m * 128:(m + 1) * 128], kv_wo[:, b, :],
                                                start=(b == 0), stop=(b == KB - 1))
                last.then_inc(mixer_ready, 1)

            @block.vector
            def _(dve):
                nc.vector.memset(heads_vk[:], 0.0).then_inc(zeroed, 1)
                with dve.Fori(0, TILES) as t:
                    tile = by_head(projected[:, bass.ds(t % 2, 1), :].rearrange("p a d -> p (a d)"))
                    dve.wait_ge(projected_ready, t + 1)
                    nc.vector.tensor_reduce(total[:], tile, AX.X, ALU.add).then_inc(totalled, 1)
                    dve.wait_ge(totalled, t + 1)
                    nc.vector.scalar_tensor_tensor(by_head(row(kv, t)), total[:].unsqueeze(2).broadcast_to([P, GROUPS, HEAD0]),
                                                   -1.0 / HEAD0, tile, ALU.mult, ALU.add).then_inc(centred, 1)
                    dve.wait_ge(squared, t + 1)
                    nc.vector.tensor_reduce(var[:, bass.ds(t * GROUPS, GROUPS)],
                                            by_head(square[:, bass.ds(t % 2, 1), :].rearrange("p a d -> p (a d)")),
                                            AX.X, ALU.add).then_inc(summed, 1)
                dve.wait_ge(summed, TILES)
                nc.vector.tensor_scalar(var[:], var[:], 1.0 / HEAD0, LN_EPS, ALU.mult, ALU.add).then_inc(var_ready, 1)
                dve.wait_ge(std_ready, 1)
                inverse_root(dve, nc, chain, std, var, work)
                with dve.Fori(0, TILES) as t:
                    nc.vector.tensor_tensor(by_head(row(kv, t)), by_head(row(kv, t)),
                                            std[:, bass.ds(t * GROUPS, GROUPS)].unsqueeze(2).broadcast_to([P, GROUPS, HEAD0]),
                                            ALU.mult).then_inc(scaled, 1)

            @block.gpsimd
            def _(pool):
                pool.wait_ge(loaded, 8 * 16)
                for t in range(TILES):
                    tile = row(kv, t).rearrange("p (n h d) -> p n h d", n=2, d=HEAD0)
                    pool.wait_ge(scaled, t + 1)
                    nc.gpsimd.tensor_tensor(tile, tile, gain[:].unsqueeze(2).broadcast_to([P, 2, HEADS0, HEAD0]),
                                            ALU.mult).then_inc(gained, 1)
                    pool.wait_ge(gained, t + 1)
                    nc.gpsimd.tensor_tensor(tile, tile, shift[:].unsqueeze(2).broadcast_to([P, 2, HEADS0, HEAD0]),
                                            ALU.add).then_inc(shifted, 1)

            @block.scalar
            def _(act):
                with act.Fori(0, TILES) as t:
                    act.wait_ge(centred, t + 1)
                    nc.scalar.activation(square[:, bass.ds(t % 2, 1), :].rearrange("p a d -> p (a d)"), row(kv, t),
                                         ACT.Square).then_inc(squared, 1)
                act.wait_ge(var_ready, 1)
                nc.scalar.activation(std[:], var[:], ACT.Sqrt).then_inc(std_ready, 1)
                act.wait_ge(vk_ready, 1)
                act.wait_ge(zeroed, 1)
                for b in range(KB):
                    for h in range(128 // HEAD0):
                        d = slice(h * HEAD0, (h + 1) * HEAD0)
                        last = nc.scalar.activation(heads_vk[d, b, d], vk[d, b, d], ACT.Copy, scale=1.0 / NODES)
                last.then_inc(heads_ready, 1)
                act.wait_ge(kv_wo_ready, 1)
                nc.scalar.activation(kv_wo[:], product[:, :, 0:DIM], ACT.Copy).then_inc(kv_wo_kept, 1)
                act.wait_ge(mixer_ready, 1)
                nc.scalar.activation(mixer[:], product[:, :, 0:DIM], ACT.Copy)


def sage_and_mix(p, c, A, x, xn_T, mean_in, mean_out, mixer):
    nc = p.nc
    HALF = DIM // 2
    with ExitStack() as scope:
        sb = lambda name, shape, dtype=F32: p.sb("sg_" + name, shape, dtype, scope)
        w_r = sb("w_r", [128, KB, DIM])
        w_l = sb("w_l", [128, 2, KB, HALF])
        bias, gamma, beta, bo = (sb(n, [P, DIM]) for n in ("bias", "gamma", "beta", "bo"))
        means_T = sb("means_T", [128, 2, 2 * KB * P])
        h = mean_in
        square = sb("square", [P, 2, DIM])
        average, var, std, work = (sb(n, [P, DIM]) for n in ("average", "var", "std", "work"))
        turned = p.ps("sg_turned", [128, 2, 512], scope=scope)
        projected = p.ps("sg_projected", [P, 2, 512], scope=scope)
        sums = p.ps("sg_sums", [P, 2, 512], scope=scope)
        mixed = p.ps("sg_mixed", [P, 2, 512], scope=scope)
        loaded, turn_ready, turn_copied = p.sem("sg_loaded"), p.sem("sg_turn_ready"), p.sem("sg_turn_copied")
        projected_ready, h_ready = p.sem("sg_projected_ready"), p.sem("sg_h_ready")
        sum_ready, centred, squared, square_summed = (p.sem("sg_sum_ready"), p.sem("sg_centred"), p.sem("sg_squared"),
                                                      p.sem("sg_square_summed"))
        var_ready, std_ready = p.sem("sg_var_ready"), p.sem("sg_std_ready")
        scaled, shifted, mixed_ready, added, finished = (p.sem("sg_scaled"), p.sem("sg_shifted"), p.sem("sg_mixed_ready"),
                                                         p.sem("sg_added"), p.sem("sg_finished"))
        chain = Chain(p.sem("sg_chain"))
        LOADS = 9
        with nc.Block() as block:
            @block.sync
            def _(sp):
                by_block = lambda a: a.rearrange("(k p) n -> p k n", p=128)
                for d, (l, r, b) in enumerate((("W_l_f_T", "W_r_f_T", "b_l_f"), ("W_l_b_T", "W_r_b_T", "b_l_b"))):
                    at = slice(d * HALF, (d + 1) * HALF)
                    sp.dma_start(w_r[:, :, at], by_block(A[r])).then_inc(loaded, 16)
                    sp.dma_start(w_l[:, d, :, :], by_block(A[l])).then_inc(loaded, 16)
                    sp.dma_start(bias[:, at], A[b].partition_broadcast(P)).then_inc(loaded, 16)
                for to, name in ((gamma, "bn_gamma"), (beta, "bn_beta"), (bo, "bo")):
                    sp.dma_start(to[:], A[name].partition_broadcast(P)).then_inc(loaded, 16)
                sp.wait_ge(loaded, LOADS * 16)

            @block.tensor
            def _(pe):
                def turn(t):
                    if t >= 2:
                        pe.wait_ge(turn_copied, t - 1)
                    for d, means in enumerate((mean_in, mean_out)):
                        for k in range(KB):
                            n = d * KB + k
                            last = nc.tensor.transpose(turned[:, t % 2, n * P:(n + 1) * P],
                                                       means[:, t, k * 128:(k + 1) * 128], c.ident[:P, :P])
                    last.then_inc(turn_ready, 1)

                pe.wait_ge(loaded, LOADS * 16)
                turn(0)
                for t in range(TILES):
                    if t + 1 < TILES:
                        turn(t + 1)
                    if t >= 2:
                        pe.wait_ge(h_ready, t - 1)
                    for k in range(KB):
                        nc.tensor.matmul(projected[:, t % 2, 0:DIM], xn_T[:, k, t * P:(t + 1) * P], w_r[:, k, :],
                                         start=(k == 0), stop=False, skip_group_check=True)
                    pe.wait_ge(turn_copied, t + 1)
                    for d in range(2):
                        for k in range(KB):
                            n = d * KB + k
                            last = nc.tensor.matmul(projected[:, t % 2, d * HALF:(d + 1) * HALF],
                                                    means_T[:, t % 2, n * P:(n + 1) * P], w_l[:, d, k, :],
                                                    start=False, stop=(k == KB - 1), skip_group_check=True)
                    last.then_inc(projected_ready, 1)
                for t in range(TILES):
                    pe.wait_ge(h_ready, t + 1)
                    last = nc.tensor.matmul(sums[:, 0, 0:DIM], c.ones[:P, :P], h[:, t, :],
                                            start=(t == 0), stop=(t == TILES - 1))
                last.then_inc(sum_ready, 1)
                for t in range(TILES):
                    pe.wait_ge(squared, t + 1)
                    last = nc.tensor.matmul(sums[:, 1, 0:DIM], c.ones[:P, :P], square[:, t % 2, :],
                                            start=(t == 0), stop=(t == TILES - 1))
                    last.then_inc(square_summed, 1)
                for t in range(TILES):
                    if t >= 2:
                        pe.wait_ge(added, t - 1)
                    for k in range(KB):
                        last = nc.tensor.matmul(mixed[:, t % 2, 0:DIM], xn_T[:, k, t * P:(t + 1) * P], mixer[:, k, :],
                                                start=(k == 0), stop=(k == KB - 1))
                    last.then_inc(mixed_ready, 1)

            @block.scalar
            def _(act):
                with act.Fori(0, TILES) as t:
                    act.wait_ge(turn_ready, t + 1)
                    nc.scalar.activation(means_T[:, bass.ds(t % 2, 1), :].rearrange("p a d -> p (a d)"),
                                         turned[:, bass.ds(t % 2, 1), 0:2 * KB * P].rearrange("p a d -> p (a d)"),
                                         ACT.Copy).then_inc(turn_copied, 1)
                act.sem_inc(square_summed, 2)
                with act.Fori(0, TILES) as t:
                    act.wait_ge(centred, t + 1)
                    act.wait_ge(square_summed, t + 1)
                    nc.scalar.activation(square[:, bass.ds(t % 2, 1), :].rearrange("p a d -> p (a d)"), row(h, t),
                                         ACT.Square).then_inc(squared, 1)
                act.wait_ge(var_ready, 1)
                nc.scalar.activation(std[:], var[:], ACT.Sqrt).then_inc(std_ready, 1)

            @block.vector
            def _(dve):
                dve.wait_ge(loaded, LOADS * 16)
                with dve.Fori(0, TILES) as t:
                    dve.wait_ge(projected_ready, t + 1)
                    nc.vector.tensor_tensor(row(h, t), projected[:, bass.ds(t % 2, 1), 0:DIM].rearrange("p a d -> p (a d)"),
                                            bias[:], ALU.add).then_inc(h_ready, 1)
                dve.wait_ge(sum_ready, 1)
                chain.tick(nc.vector.tensor_scalar(average[:], sums[:, 0, 0:DIM], 1.0 / NODES, None, ALU.mult))
                chain.wait(dve)
                with dve.Fori(0, TILES) as t:
                    nc.vector.tensor_tensor(row(h, t), row(h, t), average[:], ALU.subtract).then_inc(centred, 1)
                dve.wait_ge(square_summed, TILES + 2)
                chain.tick(nc.vector.tensor_scalar(var[:], sums[:, 1, 0:DIM], 1.0 / NODES, LN_EPS, ALU.mult, ALU.add))
                chain.wait(dve)
                nc.vector.engine_nop().then_inc(var_ready, 1)
                dve.wait_ge(std_ready, 1)
                inverse_root(dve, nc, chain, std, var, work)
                chain.tick(nc.vector.tensor_tensor(std[:], std[:], gamma[:], ALU.mult))
                chain.wait(dve)
                dve.wait_ge(centred, TILES)
                with dve.Fori(0, TILES) as t:
                    nc.vector.tensor_tensor(row(h, t), row(h, t), std[:], ALU.mult).then_inc(scaled, 1)
                with dve.Fori(0, TILES) as t:
                    dve.wait_ge(mixed_ready, t + 1)
                    dve.wait_ge(finished, t + 1)
                    nc.vector.tensor_tensor(row(x, t), mixed[:, bass.ds(t % 2, 1), 0:DIM].rearrange("p a d -> p (a d)"),
                                            row(x, t), ALU.add).then_inc(added, 1)
                    dve.wait_ge(shifted, t + 1)
                    dve.wait_ge(added, t + 1)
                    nc.vector.scalar_tensor_tensor(row(x, t), row(h, t), 0.0, row(x, t), ALU.max, ALU.add)

            @block.gpsimd
            def _(pool):
                pool.wait_ge(loaded, LOADS * 16)
                with pool.Fori(0, TILES) as t:
                    nc.gpsimd.tensor_tensor(row(x, t), row(x, t), bo[:], ALU.add).then_inc(finished, 1)
                for t in range(TILES):
                    pool.wait_ge(scaled, t + 1)
                    nc.gpsimd.tensor_tensor(row(h, t), row(h, t), beta[:], ALU.add).then_inc(shifted, 1)


def gate(p, c, scope, name, logits_ready, logits, bias, top, weight, gated, block_vector, block_scalar):
    nc = p.nc
    sb = lambda n, shape, dtype=F32: p.sb(f"{name}_{n}", shape, dtype, scope)
    raw, prob = sb("raw", [P, TILES, EXPERTS]), sb("prob", [P, TILES, EXPERTS])
    part = sb("part", [P, TILES, EXPERTS])
    best, total = sb("best", [P, TILES]), sb("total", [P, TILES])
    most = sb("most", [P, TILES, EXPERTS])
    which = sb("which", [P, TILES, EXPERTS], mybir.dt.uint32)
    which_f = sb("which_f", [P, TILES, EXPERTS])
    number_i, number = sb("number_i", [P, EXPERTS], I32), sb("number", [P, EXPERTS])
    shares = sb("shares", [P, TILES, 2])
    shifted, exped, numbered = p.sem(f"{name}_shifted"), p.sem(f"{name}_exped"), p.sem(f"{name}_numbered")
    chain = Chain(p.sem(f"{name}_chain"))
    over = lambda a: a.unsqueeze(2).broadcast_to([P, TILES, EXPERTS])

    def pool_steps(pool):
        nc.gpsimd.iota(number_i[:], [[1, EXPERTS]], base=0, channel_multiplier=0).then_inc(numbered, 1)

    def scalar_steps(act):
        act.wait_ge(shifted, 1)
        nc.scalar.activation(prob[:], raw[:], ACT.Exp).then_inc(exped, 1)

    def vector_steps(dve):
        dve.wait_ge(numbered, 1)
        nc.vector.tensor_copy(number[:], number_i[:])
        dve.wait_ge(logits_ready, TILES)
        if bias is None:
            chain.tick(nc.vector.tensor_copy(raw[:], logits))
        else:
            chain.tick(nc.vector.tensor_tensor(raw[:], logits, bias[:].unsqueeze(1).broadcast_to([P, TILES, EXPERTS]),
                                               ALU.add))
        chain.wait(dve)
        chain.tick(nc.vector.tensor_reduce(best[:], raw[:], AX.X, ALU.max))
        chain.wait(dve)
        nc.vector.tensor_tensor(raw[:], raw[:], over(best[:]), ALU.subtract).then_inc(shifted, 1)
        dve.wait_ge(exped, 1)
        chain.tick(nc.vector.tensor_reduce(total[:], prob[:], AX.X, ALU.add))
        chain.wait(dve)
        chain.tick(nc.vector.reciprocal(total[:], total[:]))
        chain.wait(dve)
        chain.tick(nc.vector.tensor_tensor(prob[:], prob[:], over(total[:]), ALU.mult))
        chain.wait(dve)
        for t in range(TILES):
            last = nc.vector.max(most[:, t, :], prob[:, t, :])
        chain.tick(last)
        chain.wait(dve)
        for t in range(TILES):
            last = nc.vector.max_index(which[:, t, :], most[:, t, :], prob[:, t, :])
        chain.tick(last)
        chain.wait(dve)
        chain.tick(nc.vector.tensor_copy(which_f[:], which[:]))
        if top == 2:
            chain.tick(nc.vector.tensor_tensor(total[:], most[:, :, 0], most[:, :, 1], ALU.add))
            chain.wait(dve)
            chain.tick(nc.vector.tensor_scalar(total[:], total[:], 1e-12, None, ALU.max))
            chain.wait(dve)
            chain.tick(nc.vector.reciprocal(total[:], total[:]))
            chain.wait(dve)
            chain.tick(nc.vector.tensor_tensor(shares[:], most[:, :, 0:2], total[:].unsqueeze(2).broadcast_to([P, TILES, 2]),
                                               ALU.mult))
        else:
            chain.tick(nc.vector.tensor_copy(shares[:], most[:, :, 0:2]))
        chain.wait(dve)
        for n in range(top):
            to = weight if n == 0 else part
            chain.tick(nc.vector.tensor_tensor(to[:], number[:].unsqueeze(1).broadcast_to([P, TILES, EXPERTS]),
                                               over(which_f[:, :, n]), ALU.is_equal))
            chain.wait(dve)
            chain.tick(nc.vector.tensor_tensor(to[:], to[:], over(shares[:, :, n]), ALU.mult))
            chain.wait(dve)
        if top == 2:
            chain.tick(nc.vector.tensor_tensor(weight[:], weight[:], part[:], ALU.add))
            chain.wait(dve)
        nc.vector.engine_nop().then_inc(gated, 1)

    return pool_steps, scalar_steps, vector_steps


def mixture(p, c, A, x, xn, xn_T):
    nc = p.nc
    with ExitStack() as scope:
        sb = lambda name, shape, dtype=F32: p.sb("mx_" + name, shape, dtype, scope)
        router = sb("router", [128, KB, EXPERTS])
        share = sb("share", [P, TILES, EXPERTS])
        share_T = sb("share_T", [EXPERTS, NODES])
        b1 = sb("b1", [128, EXPERTS * KB])
        b2 = sb("b2", [EXPERTS, DIM])
        w1 = sb("w1", [128, 2, KB, DIM])
        w2 = sb("w2", [128, 2, KB, DIM])
        hidden = sb("hidden", [128, 2, KB, CHUNK])
        logits = p.ps("mx_logits", [P, TILES, EXPERTS], scope=scope)
        turned = p.ps("mx_turned", [EXPERTS, 512], scope=scope)
        up = p.ps("mx_up", [128, 2, 512], scope=scope)
        down = p.ps("mx_down", [P, 4, 512], scope=scope)
        loaded, logits_ready, gated = p.sem("mx_loaded"), p.sem("mx_logits_ready"), p.sem("mx_gated")
        turn_ready, turn_copied = p.sem("mx_turn_ready"), p.sem("mx_turn_copied")
        w_loaded = [p.sem(f"mx_w_loaded{u}") for u in range(2)]
        up_ready, hidden_ready, down_ready, added = (p.sem("mx_up_ready"), p.sem("mx_hidden_ready"),
                                                     p.sem("mx_down_ready"), p.sem("mx_added"))
        based = p.sem("mx_based")
        pool_gate, scalar_gate, vector_gate = gate(p, c, scope, "mg", logits_ready, logits[:], None, 2, share, gated,
                                                   None, None)
        by_block = lambda a: a.rearrange("(k p) n -> p k n", p=128)
        with nc.Block() as block:
            @block.sync
            def _(sp):
                sp.dma_start(router[:], by_block(A["router_T"])).then_inc(loaded, 16)
                sp.dma_start(b1[:], A["ffn0_b1_T"]).then_inc(loaded, 16)
                sp.dma_start(b2[:], A["ffn0_b2"]).then_inc(loaded, 16)
                for e in range(EXPERTS):
                    if e >= 2:
                        sp.wait_ge(down_ready, (e - 1) * TILES)
                    sp.dma_start(w1[:, e % 2, :, :], by_block(A["ffn0_w1"][e])).then_inc(w_loaded[e % 2], 16)
                    sp.dma_start(w2[:, e % 2, :, :], by_block(A["ffn0_w2"][e])).then_inc(w_loaded[e % 2], 16)
                sp.wait_ge(loaded, 48)

            @block.gpsimd
            def _(pool):
                pool_gate(pool)
                with pool.Fori(0, TILES) as t:
                    nc.gpsimd.tensor_tensor(row(x, t), row(x, t), xn[:, bass.ds(t, 1), 0:DIM].rearrange("p a d -> p (a d)"),
                                            ALU.add).then_inc(based, 1)

            @block.tensor
            def _(pe):
                pe.wait_ge(loaded, 48)
                for t in range(TILES):
                    for k in range(KB):
                        last = nc.tensor.matmul(logits[:, t, :], xn_T[:, k, t * P:(t + 1) * P], router[:, k, :],
                                                start=(k == 0), stop=(k == KB - 1))
                    last.then_inc(logits_ready, 1)

                def raise_up(e, q):
                    n = e * CHUNKS + q
                    pe.wait_ge(w_loaded[e % 2], 32 * (e // 2 + 1))
                    for m in range(KB):
                        i = n * KB + m
                        if i >= 2:
                            pe.wait_ge(hidden_ready, i - 1)
                        for k in range(KB):
                            last = nc.tensor.matmul(up[:, m, 0:CHUNK], w1[:, e % 2, k, m * 128:(m + 1) * 128],
                                                    xn_T[:, k, q * CHUNK:(q + 1) * CHUNK], start=(k == 0),
                                                    stop=(k == KB - 1))
                        last.then_inc(up_ready, 1)

                def bring_down(e, q):
                    n = e * CHUNKS + q
                    pe.wait_ge(hidden_ready, (n + 1) * KB)
                    for j in range(4):
                        i = n * 4 + j
                        if i >= 4:
                            pe.wait_ge(added, i - 3)
                        for k in range(KB):
                            last = nc.tensor.matmul(down[:, i % 4, 0:DIM], hidden[:, n % 2, k, j * P:(j + 1) * P],
                                                    w2[:, e % 2, k, :], start=(k == 0), stop=(k == KB - 1))
                        last.then_inc(down_ready, 1)

                steps = [(e, q) for e in range(EXPERTS) for q in range(CHUNKS)]
                raise_up(*steps[0])
                for n, step in enumerate(steps):
                    if n + 1 < len(steps):
                        raise_up(*steps[n + 1])
                    bring_down(*step)
                pe.wait_ge(gated, 1)
                for q in range(CHUNKS):
                    if q >= 1:
                        pe.wait_ge(turn_copied, q)
                    for j in range(4):
                        last = nc.tensor.transpose(turned[:, j * P:(j + 1) * P], share[:, q * 4 + j, :], c.ident[:P, :P])
                    last.then_inc(turn_ready, 1)
                for t in range(TILES):
                    i = len(steps) * 4 + t
                    pe.wait_ge(turn_copied, t // 4 + 1)
                    pe.wait_ge(added, i - 3)
                    nc.tensor.matmul(down[:, i % 4, 0:DIM], share_T[:, t * P:(t + 1) * P], b2[:], start=True,
                                     stop=True).then_inc(down_ready, 1)

            @block.scalar
            def _(act):
                scalar_gate(act)
                act.wait_ge(loaded, 48)
                for e in range(EXPERTS):
                    for q in range(CHUNKS):
                        n = e * CHUNKS + q
                        if n >= 2:
                            act.wait_ge(down_ready, (n - 1) * 4)
                        for m in range(KB):
                            act.wait_ge(up_ready, n * KB + m + 1)
                            nc.scalar.activation(hidden[:, n % 2, m, :], up[:, m, 0:CHUNK], ACT.Gelu,
                                                 bias=b1[:, e * KB + m:e * KB + m + 1]).then_inc(hidden_ready, 1)
                for q in range(CHUNKS):
                    act.wait_ge(turn_ready, q + 1)
                    nc.scalar.activation(share_T[:, q * CHUNK:(q + 1) * CHUNK], turned[:, 0:CHUNK],
                                         ACT.Copy).then_inc(turn_copied, 1)

            @block.vector
            def _(dve):
                vector_gate(dve)
                dve.wait_ge(based, TILES)
                with dve.Fori(0, EXPERTS) as e:
                    for t in range(TILES):
                        dve.wait_ge(down_ready, e * TILES + t + 1)
                        nc.vector.scalar_tensor_tensor(x[:, t, :], down[:, t % 4, 0:DIM], share[:, t, bass.ds(e, 1)],
                                                       x[:, t, :], ALU.mult, ALU.add).then_inc(added, 1)
                with dve.Fori(0, TILES) as t:
                    dve.wait_ge(down_ready, t + EXPERTS * TILES + 1)
                    nc.vector.tensor_tensor(row(x, t), down[:, bass.ds(t % 4, 1), 0:DIM].rearrange("p a d -> p (a d)"),
                                            row(x, t), ALU.add).then_inc(added, 1)


def to_nodes_first(p, c, A, xn_T, weight, bias, table):
    nc = p.nc
    with ExitStack() as scope:
        w = p.sb("nf_w", [128, KB, DIM], scope=scope)
        b = p.sb("nf_b", [P, DIM], scope=scope)
        rows = p.sb("nf_rows", [P, TILES, DIM], scope=scope)
        projected = p.ps("nf_projected", [P, 4, 512], scope=scope)
        loaded, ready, kept, stored = p.sem("nf_loaded"), p.sem("nf_ready"), p.sem("nf_kept"), p.sem("nf_stored")
        with nc.Block() as block:
            @block.sync
            def _(sp):
                sp.dma_start(w[:], weight.rearrange("(k p) n -> p k n", p=128)).then_inc(loaded, 16)
                sp.dma_start(b[:], bias.partition_broadcast(P)).then_inc(loaded, 16)
                sp.wait_ge(kept, TILES)
                sp.dma_start(table.rearrange("(t p) d -> p t d", p=P), rows[:]).then_inc(stored, 16)
                sp.wait_ge(stored, 16)

            @block.tensor
            def _(pe):
                pe.wait_ge(loaded, 32)
                for t in range(TILES):
                    if t >= 4:
                        pe.wait_ge(kept, t - 3)
                    for k in range(KB):
                        last = nc.tensor.matmul(projected[:, t % 4, 0:DIM], xn_T[:, k, t * P:(t + 1) * P], w[:, k, :],
                                                start=(k == 0), stop=(k == KB - 1))
                    last.then_inc(ready, 1)

            @block.vector
            def _(dve):
                dve.wait_ge(loaded, 32)
                with dve.Fori(0, TILES) as t:
                    dve.wait_ge(ready, t + 1)
                    nc.vector.tensor_tensor(row(rows, t), projected[:, bass.ds(t % 4, 1), 0:DIM].rearrange("p a d -> p (a d)"),
                                            b[:], ALU.add).then_inc(kept, 1)


def edge_messages(p, c, ranges, SUB, A, src, dst, table, hidden_sum):
    nc = p.nc
    BLOCKS = EDGE_TILES // SUB
    with ExitStack() as scope:
        sb = lambda name, shape, dtype=F32: p.sb("em_" + name, shape, dtype, scope)
        w1 = sb("w1", [128, KB, DIM])
        attr = [sb(f"attr{s}", [128, KB, P]) for s in range(SUB)]
        which = [sb(f"which{s}", [P, 1], I32) for s in range(SUB)]
        gathered = [sb(f"gathered{s}", [P, DIM]) for s in range(SUB)]
        pre = sb("pre", [P, SUB, DIM])
        hidden = sb("hidden", [P, SUB, DIM])
        hot = sb("hot", [P, SUB, P])
        dst_f = sb("dst_f", [P, EDGE_TILES])
        projected = p.ps("em_projected", [P, SUB, 512], scope=scope)
        total = p.ps("em_total", [P, 512], scope=scope)
        w_loaded, dst_ready = p.sem("em_w_loaded"), p.sem("em_dst_ready")
        attr_loaded = [p.sem(f"em_attr_loaded{s}") for s in range(SUB)]
        copied = [p.sem(f"em_copied{s}") for s in range(SUB)]
        got = [p.sem(f"em_got{s}") for s in range(SUB)]
        projected_ready = [p.sem(f"em_projected_ready{s}") for s in range(SUB)]
        pre_ready = [p.sem(f"em_pre_ready{s}") for s in range(SUB)]
        hidden_ready = [p.sem(f"em_hidden_ready{s}") for s in range(SUB)]
        hot_ready = [p.sem(f"em_hot_ready{s}") for s in range(SUB)]
        summed = [p.sem(f"em_summed{s}") for s in range(SUB)]
        kept, passed = p.sem("em_kept"), p.sem("em_passed")
        edge_tile = lambda lo, i, s: (lo + i).with_bounds(min_val=0, max_val=BLOCKS - 1) * SUB + s
        with nc.Block() as block:
            @block.sync
            def _(sp):
                sp.dma_start(w1[:], A["gnn1_W1"].rearrange("(k p) n -> p k n", p=128)).then_inc(w_loaded, 16)
                for s in range(SUB):
                    sp.sem_inc(projected_ready[s], 1)
                with sp.Fori(0, TILES) as t:
                    lo, n, before = load_range(sp, ranges, t, SUB)
                    with sp.Fori(0, n) as i:
                        for s in range(SUB):
                            sp.wait_ge(projected_ready[s], before + i + 1)
                            sp.dma_start(attr[s][:], A["edge_attr_T"][bass.ds(edge_tile(lo, i, s), 1)]
                                         .rearrange("a p k e -> p (a k) e")).then_inc(attr_loaded[s], 16)

            @block.gpsimd
            def _(pool):
                for s in range(SUB):
                    pool.sem_inc(pre_ready[s], 1)
                with pool.Fori(0, TILES) as t:
                    lo, n, before = load_range(pool, ranges, t, SUB)
                    with pool.Fori(0, n) as i:
                        for s in range(SUB):
                            pool.wait_ge(pre_ready[s], before + i + 1)
                            nc.gpsimd.tensor_copy(which[s][:], src[:, bass.ds(edge_tile(lo, i, s), 1)]).then_inc(copied[s], 1)
                            pool.wait_ge(copied[s], before + i + 1)
                            pool.sem_inc(passed, 1)
                            nc.gpsimd.indirect_dma_start(
                                out=gathered[s][:], out_offset=None, in_=table,
                                in_offset=bass.IndirectOffsetOnAxis(ap=which[s][:].bitcast(mybir.dt.uint32), axis=0)).then_inc(got[s], 16)

            @block.tensor
            def _(pe):
                def project(before, i, s):
                    pe.wait_ge(attr_loaded[s], (before + i + 1) * 16)
                    pe.wait_ge(pre_ready[s], before + i + 1)
                    for k in range(KB):
                        last = nc.tensor.matmul(projected[:, s, 0:DIM], attr[s][:, k, :], w1[:, k, :],
                                                start=(k == 0), stop=(k == KB - 1))
                    last.then_inc(projected_ready[s], 1)

                def add_up(before, i, s):
                    pe.wait_ge(hidden_ready[s], before + i + 1)
                    pe.wait_ge(hot_ready[s], before + i + 1)
                    nc.tensor.matmul(total[:, 0:DIM], hot[:, s, :], hidden[:, s, :], start=False, stop=True,
                                     skip_group_check=True).then_inc(summed[s], 1)

                pe.wait_ge(w_loaded, 16)
                for s in range(SUB):
                    pe.sem_inc(summed[s], 1)
                with pe.Fori(0, TILES) as t:
                    lo, n, before = load_range(pe, ranges, t, SUB)
                    pe.wait_ge(kept, t + 1)
                    nc.tensor.matmul(total[:, 0:2], c.zero[:], c.zero[:, 0:2], start=True, stop=False, skip_group_check=True)
                    with pe.Fori(0, n) as i:
                        project(before, i, 0)
                        for s in range(SUB):
                            if s + 1 < SUB:
                                project(before, i, s + 1)
                            if s >= 1:
                                add_up(before, i, s - 1)
                        add_up(before, i, SUB - 1)

            @block.vector
            def _(dve):
                nc.vector.tensor_copy(dst_f[:], dst[:]).then_inc(dst_ready, 1)
                dve.wait_ge(dst_ready, 1)
                dve.sem_inc(kept, 1)
                with dve.Fori(0, TILES) as t:
                    lo, n, before = load_range(dve, ranges, t, SUB)
                    with dve.Fori(0, n) as i:
                        for s in range(SUB):
                            dve.wait_ge(summed[s], before + i + 1)
                            nc.vector.tensor_scalar(hot[:, s, :], c.iota_node_i[:, bass.ds(t * P, P)],
                                                    dst_f[:, bass.ds(edge_tile(lo, i, s), 1)], None,
                                                    ALU.is_equal).then_inc(hot_ready[s], 1)
                        for s in range(SUB):
                            dve.wait_ge(projected_ready[s], before + i + 2)
                            dve.wait_ge(got[s], (before + i + 1) * 16)
                            nc.vector.tensor_tensor(pre[:, s, :], projected[:, s, 0:DIM], gathered[s][:],
                                                    ALU.add).then_inc(pre_ready[s], 1)
                    dve.wait_ge(summed[SUB - 1], before + n + 1)
                    nc.vector.tensor_copy(row(hidden_sum, t), total[:, 0:DIM]).then_inc(kept, 1)

            @block.scalar
            def _(act):
                with act.Fori(0, TILES) as t:
                    lo, n, before = load_range(act, ranges, t, SUB)
                    with act.Fori(0, n) as i:
                        for s in range(SUB):
                            act.wait_ge(pre_ready[s], before + i + 2)
                            nc.scalar.activation(hidden[:, s, :], pre[:, s, :], ACT.Relu).then_inc(hidden_ready[s], 1)


def softmax_attention(p, c, A, x, xn, xn_T, hidden_sum, in_degree):
    nc = p.nc
    with ExitStack() as scope:
        sb = lambda name, shape, dtype=F32: p.sb("at_" + name, shape, dtype, scope)
        w = sb("w", [128, KB, 3 * DIM])
        w_out = sb("w_out", [128, KB, DIM])
        w2 = sb("w2", [128, KB, DIM])
        b2, gamma = sb("b2", [P, DIM]), sb("gamma", [P, DIM])
        q, k, v = (sb(n, [P, TILES, DIM]) for n in "qkv")
        q_T = sb("q_T", [128, KB, NODES])
        peak = sb("peak", [P, DIM])
        peak_col = sb("peak_col", [128, KB])
        q_peak, q_sum = sb("q_peak", [P, HEADS1]), sb("q_sum", [P, HEADS1])
        heads_vk = sb("heads_vk", [128, KB, 128])
        k_share = sb("k_share", [128, KB])
        kv_wo = sb("kv_wo", [128, KB, DIM])
        sum_T = sb("sum_T", [128, 2, KB * P])
        stats = sb("stats", [P, TILES * 6])
        mean, var, std, half = (sb(n, [P, TILES]) for n in ("mean", "var", "std", "half"))
        out = k
        loaded = p.sem("at_loaded")
        chain = Chain(p.sem("at_chain"))
        sem = lambda n: p.sem("at_" + n)
        by_head = lambda a: a.rearrange("p (h d) -> p h d", d=HEAD1)
        spread = lambda a: a[:].unsqueeze(2).broadcast_to([P, HEADS1, HEAD1])
        LOADS = 5

        with ExitStack() as first:
            q_bank = p.ps("at_q_bank", [P, 2, 512], scope=first)
            kv_bank = p.ps("at_kv_bank", [P, 2, 512], scope=first)
            turned = p.ps("at_turned", [128, 2, 512], scope=first)
            peaks = p.ps("at_peaks", [128, KB, 512], scope=first)
            qkkv_ready, kv_read = sem("qkkv_ready"), sem("kv_read")
            q_less, q_exped, q_added, q_inverted, q_ready = sem("q_less"), sem("q_exped"), sem("q_added"), sem("q_inverted"), sem("q_ready")
            q_peaked, turn_ready, turn_copied, peaked = sem("q_peaked"), sem("turn_ready"), sem("turn_copied"), sem("peaked")
            passed, peak_turned, peak_found, peak_spread, k_less = sem("passed"), sem("peak_turned"), sem("peak_found"), sem("peak_spread"), sem("k_less")
            with nc.Block() as block:
                @block.sync
                def _(sp):
                    by_block = lambda a: a.rearrange("(k p) n -> p k n", p=128)
                    sp.dma_start(w[:], by_block(A["Wqkv"])).then_inc(loaded, 16)
                    sp.dma_start(w_out[:], by_block(A["Wout"])).then_inc(loaded, 16)
                    sp.dma_start(w2[:], by_block(A["gnn1_W2"])).then_inc(loaded, 16)
                    sp.dma_start(b2[:], A["gnn1_b2"].partition_broadcast(P)).then_inc(loaded, 16)
                    sp.dma_start(gamma[:], A["mix1_gamma"].partition_broadcast(P)).then_inc(loaded, 16)
                    sp.wait_ge(loaded, LOADS * 16)

                @block.tensor
                def _(pe):
                    def turn(t):
                        pe.wait_ge(q_ready, t + 1)
                        if t >= 2:
                            pe.wait_ge(turn_copied, t - 1)
                        for b in range(KB):
                            last = nc.tensor.transpose(turned[:, t % 2, b * P:(b + 1) * P], q[:, t, b * 128:(b + 1) * 128],
                                                       c.ident[:P, :P])
                        last.then_inc(turn_ready, 1)

                    pe.wait_ge(loaded, LOADS * 16)
                    for t in range(TILES):
                        if t >= 2:
                            pe.wait_ge(q_less, t - 1)
                            pe.wait_ge(kv_read, 2 * (t - 1))
                        for b in range(KB):
                            nc.tensor.matmul(q_bank[:, t % 2, 0:DIM], xn_T[:, b, t * P:(t + 1) * P], w[:, b, 0:DIM],
                                             start=(b == 0), stop=(b == KB - 1))
                        for b in range(KB):
                            last = nc.tensor.matmul(kv_bank[:, t % 2, :], xn_T[:, b, t * P:(t + 1) * P], w[:, b, DIM:],
                                                    start=(b == 0), stop=(b == KB - 1))
                        last.then_inc(qkkv_ready, 1)
                    for t in range(TILES):
                        turn(t)
                    pe.wait_ge(peaked, TILES + 1)
                    for b in range(KB):
                        last = nc.tensor.transpose(peaks[:, b, 0:P], peak[:, b * 128:(b + 1) * 128], c.ident[:P, :P])
                    last.then_inc(peak_turned, 1)
                    pe.wait_ge(peak_found, 1)
                    for b in range(KB):
                        last = nc.tensor.matmul(peaks[:P, b, 128:256], peak_col[:, b:b + 1].broadcast_to([128, P]), c.ident[:],
                                                start=True, stop=True)
                    last.then_inc(peak_spread, 1)

                @block.scalar
                def _(act):
                    with act.Fori(0, TILES) as t:
                        act.wait_ge(qkkv_ready, t + 1)
                        nc.scalar.activation(row(k, t), kv_bank[:, bass.ds(t % 2, 1), 0:DIM].rearrange("p a d -> p (a d)"),
                                             ACT.Copy).then_inc(kv_read, 1)
                        nc.scalar.activation(row(v, t), kv_bank[:, bass.ds(t % 2, 1), DIM:].rearrange("p a d -> p (a d)"),
                                             ACT.Copy).then_inc(kv_read, 1)
                        act.wait_ge(q_less, t + 1)
                        nc.scalar.activation(row(q, t), row(q, t), ACT.Exp).then_inc(q_exped, 1)
                    with act.Fori(0, TILES) as t:
                        act.wait_ge(turn_ready, t + 1)
                        nc.scalar.activation(q_T[:, :, bass.ds(t * P, P)],
                                             turned[:, bass.ds(t % 2, 1), 0:KB * P].rearrange("p a (k n) -> p (a k) n", k=KB),
                                             ACT.Copy).then_inc(turn_copied, 1)

                @block.vector
                def _(dve):
                    nc.vector.memset(peak[:], -3.0e38).then_inc(peaked, 1)
                    with dve.Fori(0, TILES) as t:
                        dve.wait_ge(qkkv_ready, t + 1)
                        heads = by_head(q_bank[:, bass.ds(t % 2, 1), 0:DIM].rearrange("p a d -> p (a d)"))
                        nc.vector.tensor_reduce(q_peak[:], heads, AX.X, ALU.max).then_inc(q_peaked, 1)
                        dve.wait_ge(q_peaked, t + 1)
                        nc.vector.tensor_tensor(by_head(row(q, t)), heads, spread(q_peak), ALU.subtract).then_inc(q_less, 1)
                        dve.wait_ge(peaked, t + 1)
                        dve.wait_ge(kv_read, t * 2 + 1)
                        nc.vector.tensor_tensor(peak[:], row(k, t), peak[:], ALU.max).then_inc(peaked, 1)
                        dve.wait_ge(q_exped, t + 1)
                        dve.sem_inc(passed, 1)
                        nc.vector.tensor_reduce(q_sum[:], by_head(row(q, t)), AX.X, ALU.add).then_inc(q_added, 1)
                        dve.wait_ge(q_added, t + 1)
                        nc.vector.reciprocal(q_sum[:], q_sum[:]).then_inc(q_inverted, 1)
                        dve.wait_ge(q_inverted, t + 1)
                        nc.vector.tensor_tensor(by_head(row(q, t)), by_head(row(q, t)), spread(q_sum), ALU.mult).then_inc(q_ready, 1)
                    dve.wait_ge(peak_turned, 1)
                    nc.vector.tensor_reduce(peak_col[:], peaks[:, :, 0:P], AX.X, ALU.max).then_inc(peak_found, 1)
                    dve.wait_ge(peak_spread, 1)
                    chain.tick(nc.vector.tensor_copy(peak[:].rearrange("p (b d) -> p b d", b=KB), peaks[:P, :, 128:256]))
                    chain.wait(dve)
                    dve.wait_ge(kv_read, 2 * TILES)
                    with dve.Fori(0, TILES) as t:
                        nc.vector.tensor_tensor(row(k, t), row(k, t), peak[:], ALU.subtract)

        with ExitStack() as second:
            vk = p.ps("at_vk", [128, KB, 512], scope=second)
            k_sum = p.ps("at_k_sum", [128, KB, 512], scope=second)
            outs = p.ps("at_outs", [P, 2, 512], scope=second)
            turned = p.ps("at_turned2", [128, 2, 512], scope=second)
            zeroed, k_exped, vk_ready, heads_ready = sem("zeroed"), sem("k_exped"), sem("vk_ready"), sem("heads_ready")
            k_inverted, kv_wo_ready, kv_wo_kept = sem("k_inverted"), sem("kv_wo_ready"), sem("kv_wo_kept")
            out_ready, out_kept, measured = sem("out_ready"), sem("out_kept"), sem("measured")
            var_ready, std_ready, normed, based, degreed = sem("var_ready"), sem("std_ready"), sem("normed"), sem("based"), sem("degreed")
            sum_turned, sum_copied, message_ready, added = sem("sum_turned"), sem("sum_copied"), sem("message_ready"), sem("added")
            gained = sem("gained")
            s6 = stats[:].rearrange("p (t k) -> p k t", k=6)
            with nc.Block() as block:
                @block.scalar
                def _(act):
                    with act.Fori(0, TILES) as t:
                        nc.scalar.activation(row(k, t), row(k, t), ACT.Exp).then_inc(k_exped, 1)
                    act.wait_ge(vk_ready, 1)
                    act.wait_ge(zeroed, 1)
                    for b in range(KB):
                        for h in range(128 // HEAD1):
                            d = slice(h * HEAD1, (h + 1) * HEAD1)
                            last = nc.scalar.activation(heads_vk[d, b, d], vk[d, b, d], ACT.Copy)
                    last.then_inc(heads_ready, 1)
                    with act.Fori(0, TILES) as t:
                        act.wait_ge(sum_turned, t + 1)
                        nc.scalar.activation(sum_T[:, bass.ds(t % 2, 1), :].rearrange("p a d -> p (a d)"),
                                             turned[:, bass.ds(t % 2, 1), 0:KB * P].rearrange("p a d -> p (a d)"),
                                             ACT.Copy).then_inc(sum_copied, 1)
                    act.wait_ge(var_ready, 1)
                    nc.scalar.activation(std[:], var[:], ACT.Sqrt).then_inc(std_ready, 1)

                @block.tensor
                def _(pe):
                    for t in range(TILES):
                        pe.wait_ge(k_exped, t + 1)
                        for b in range(KB):
                            f = slice(b * 128, (b + 1) * 128)
                            nc.tensor.matmul(vk[:, b, 0:128], v[:, t, f], k[:, t, f], start=(t == 0), stop=(t == TILES - 1))
                            last = nc.tensor.matmul(k_sum[:, b, 0:1], k[:, t, f], c.ones[:P, 0:1], start=(t == 0),
                                                    stop=(t == TILES - 1))
                    last.then_inc(vk_ready, 1)
                    pe.wait_ge(heads_ready, 1)
                    for b in range(KB):
                        last = nc.tensor.matmul(vk[:, b, 0:DIM], heads_vk[:, b, :],
                                                w_out[:, b, :], start=True, stop=True)
                    last.then_inc(kv_wo_ready, 1)
                    pe.wait_ge(kv_wo_kept, 1)
                    for t in range(TILES):
                        if t >= 2:
                            pe.wait_ge(out_kept, t - 1)
                        for b in range(KB):
                            last = nc.tensor.matmul(outs[:, t % 2, 0:DIM], q_T[:, b, t * P:(t + 1) * P], kv_wo[:, b, :],
                                                    start=(b == 0), stop=(b == KB - 1))
                        last.then_inc(out_ready, 1)

                    def turn(t):
                        if t >= 2:
                            pe.wait_ge(sum_copied, t - 1)
                        for b in range(KB):
                            last = nc.tensor.transpose(turned[:, t % 2, b * P:(b + 1) * P],
                                                       hidden_sum[:, t, b * 128:(b + 1) * 128], c.ident[:P, :P])
                        last.then_inc(sum_turned, 1)

                    pe.wait_ge(out_kept, TILES)
                    turn(0)
                    for t in range(TILES):
                        if t + 1 < TILES:
                            turn(t + 1)
                        pe.wait_ge(sum_copied, t + 1)
                        if t >= 2:
                            pe.wait_ge(added, t - 1)
                        for b in range(KB):
                            last = nc.tensor.matmul(outs[:, t % 2, 0:DIM], sum_T[:, t % 2, b * P:(b + 1) * P], w2[:, b, :],
                                                    start=(b == 0), stop=(b == KB - 1))
                        last.then_inc(message_ready, 1)

                @block.gpsimd
                def _(pool):
                    with pool.Fori(0, TILES) as t:
                        nc.gpsimd.tensor_tensor(row(x, t), row(x, t), xn[:, bass.ds(t, 1), 0:DIM].rearrange("p a d -> p (a d)"),
                                                ALU.add).then_inc(based, 1)
                    for t in range(TILES):
                        pool.wait_ge(normed, t + 1)
                        nc.gpsimd.tensor_tensor(row(out, t), row(out, t), gamma[:], ALU.mult).then_inc(gained, 1)

                @block.vector
                def _(dve):
                    nc.vector.memset(heads_vk[:], 0.0).then_inc(zeroed, 1)
                    dve.wait_ge(based, TILES)
                    with dve.Fori(0, TILES) as t:
                        nc.vector.scalar_tensor_tensor(row(x, t), b2[:], in_degree[:, bass.ds(t, 1)], row(x, t),
                                                       ALU.mult, ALU.add).then_inc(degreed, 1)
                    dve.wait_ge(vk_ready, 1)
                    nc.vector.reciprocal(k_share[:].unsqueeze(2), k_sum[:, :, 0:1]).then_inc(k_inverted, 1)
                    dve.wait_ge(k_inverted, 1)
                    dve.wait_ge(kv_wo_ready, 1)
                    for b in range(KB):
                        last = nc.vector.tensor_scalar(kv_wo[:, b, :], vk[:, b, 0:DIM], k_share[:, b:b + 1], HEAD1 ** -0.5,
                                                       ALU.mult, ALU.mult)
                    last.then_inc(kv_wo_kept, 1)
                    with dve.Fori(0, TILES) as t:
                        dve.wait_ge(out_ready, t + 1)
                        nc.vector.tensor_copy(row(out, t), outs[:, bass.ds(t % 2, 1), 0:DIM].rearrange("p a d -> p (a d)")).then_inc(out_kept, 1)
                        dve.wait_ge(out_kept, t + 1)
                        nc.vector.bn_stats(stats[:, bass.ds(t * 6, 6)], row(out, t)).then_inc(measured, 1)
                    dve.wait_ge(measured, TILES)
                    nc.vector.tensor_tensor(half[:], s6[:, 1, :], s6[:, 4, :], ALU.subtract)
                    nc.vector.tensor_tensor(mean[:], s6[:, 1, :], s6[:, 4, :], ALU.add)
                    chain.tick(nc.vector.tensor_tensor(var[:], s6[:, 2, :], s6[:, 5, :], ALU.add))
                    chain.wait(dve)
                    nc.vector.tensor_scalar(mean[:], mean[:], 0.5, None, ALU.mult)
                    chain.tick(nc.vector.scalar_tensor_tensor(half[:], half[:], 0.25, half[:], ALU.mult, ALU.mult))
                    chain.wait(dve)
                    chain.tick(nc.vector.scalar_tensor_tensor(var[:], var[:], 1.0 / DIM, half[:], ALU.mult, ALU.add))
                    chain.wait(dve)
                    nc.vector.tensor_scalar(var[:], var[:], LN_EPS, None, ALU.add).then_inc(var_ready, 1)
                    dve.wait_ge(degreed, TILES)
                    with dve.Fori(0, TILES) as t:
                        dve.wait_ge(message_ready, t + 1)
                        nc.vector.tensor_tensor(row(x, t), outs[:, bass.ds(t % 2, 1), 0:DIM].rearrange("p a d -> p (a d)"),
                                                row(x, t), ALU.add).then_inc(added, 1)
                    dve.wait_ge(std_ready, 1)
                    inverse_root(dve, nc, chain, std, var, half)
                    with dve.Fori(0, TILES) as t:
                        nc.vector.tensor_scalar(row(out, t), row(out, t), mean[:, bass.ds(t, 1)], std[:, bass.ds(t, 1)],
                                                ALU.subtract, ALU.mult).then_inc(normed, 1)
                    dve.wait_ge(added, TILES)
                    with dve.Fori(0, TILES) as t:
                        dve.wait_ge(gained, t + 1)
                        nc.vector.tensor_tensor(row(x, t), row(out, t), row(x, t), ALU.add)


def layer1(p, c, A, x, xn, xn_T, ranges, SUB, src, dst, in_degree):
    table = p.nc.dram_tensor("edge_table", [NODES, DIM], F32).ap()
    layer_norm(p, c, "ln2", x, xn, xn_T)
    to_nodes_first(p, c, A, xn_T, A["gnn1_W1"], A["gnn1_b1"], table)
    with ExitStack() as scope:
        hidden_sum = p.sb("hidden_sum", [P, TILES, DIM], scope=scope)
        edge_messages(p, c, ranges, SUB, A, src, dst, table, hidden_sum)
        softmax_attention(p, c, A, x, xn, xn_T, hidden_sum, in_degree)


def one_expert(p, c, A, x, xn_T):
    nc = p.nc
    HB = HIDDEN // 128
    with ExitStack() as scope:
        sb = lambda name, shape, dtype=F32: p.sb("oe_" + name, shape, dtype, scope)
        hidden = sb("hidden", [128, HB, NODES])
        w1 = sb("w1", [128, KB, HIDDEN])
        wg = sb("wg", [128, HB, EXPERTS])
        b1 = sb("b1", [128, HB])
        bg = sb("bg", [P, EXPERTS])
        bd = sb("bd", [EXPERTS, DIM])
        wd = sb("wd", [128, 2, HB, DIM])
        share = sb("share", [P, TILES, EXPERTS])
        share_T = sb("share_T", [EXPERTS, NODES])
        logits = p.ps("oe_logits", [P, TILES, EXPERTS], scope=scope)
        turned = p.ps("oe_turned", [EXPERTS, 512], scope=scope)
        up = p.ps("oe_up", [128, 2, 512], scope=scope)
        down = p.ps("oe_down", [P, 4, 512], scope=scope)
        sem = lambda n: p.sem("oe_" + n)
        loaded, up_ready, hidden_ready, logits_ready, gated = (sem("loaded"), sem("up_ready"), sem("hidden_ready"),
                                                               sem("logits_ready"), sem("gated"))
        turn_ready, turn_copied, down_ready, added = sem("turn_ready"), sem("turn_copied"), sem("down_ready"), sem("added")
        wd_loaded = [sem(f"wd_loaded{u}") for u in range(2)]
        pool_gate, scalar_gate, vector_gate = gate(p, c, scope, "og", logits_ready, logits[:], bg, 1, share, gated, None, None)
        by_block = lambda a: a.rearrange("(k p) n -> p k n", p=128)
        LOADS = 5
        with nc.Block() as block:
            @block.sync
            def _(sp):
                sp.dma_start(w1[:], by_block(A["ffn1_W1"])).then_inc(loaded, 16)
                sp.dma_start(wg[:], by_block(A["ffn1_Wg"])).then_inc(loaded, 16)
                sp.dma_start(b1[:], A["ffn1_b1_T"]).then_inc(loaded, 16)
                sp.dma_start(bg[:], A["ffn1_bg"].partition_broadcast(P)).then_inc(loaded, 16)
                sp.dma_start(bd[:], A["ffn1_bd"]).then_inc(loaded, 16)
                for e in range(EXPERTS):
                    if e >= 2:
                        sp.wait_ge(down_ready, (e - 1) * TILES)
                    sp.dma_start(wd[:, e % 2, :, :], by_block(A["ffn1_Wd"][e])).then_inc(wd_loaded[e % 2], 16)
                sp.wait_ge(loaded, LOADS * 16)

            @block.gpsimd
            def _(pool):
                pool_gate(pool)

            @block.tensor
            def _(pe):
                pe.wait_ge(loaded, LOADS * 16)
                for q in range(CHUNKS):
                    for m in range(HB):
                        i = q * HB + m
                        if i >= 2:
                            pe.wait_ge(hidden_ready, i - 1)
                        for k in range(KB):
                            last = nc.tensor.matmul(up[:, i % 2, 0:CHUNK], w1[:, k, m * 128:(m + 1) * 128],
                                                    xn_T[:, k, q * CHUNK:(q + 1) * CHUNK], start=(k == 0), stop=(k == KB - 1))
                        last.then_inc(up_ready, 1)
                for t in range(TILES):
                    pe.wait_ge(hidden_ready, (t // 4 + 1) * HB)
                    for m in range(HB):
                        last = nc.tensor.matmul(logits[:, t, :], hidden[:, m, t * P:(t + 1) * P], wg[:, m, :],
                                                start=(m == 0), stop=(m == HB - 1))
                    last.then_inc(logits_ready, 1)
                for e in range(EXPERTS):
                    pe.wait_ge(wd_loaded[e % 2], 16 * (e // 2 + 1))
                    for t in range(TILES):
                        i = e * TILES + t
                        if i >= 4:
                            pe.wait_ge(added, i - 3)
                        for m in range(HB):
                            last = nc.tensor.matmul(down[:, i % 4, 0:DIM], hidden[:, m, t * P:(t + 1) * P], wd[:, e % 2, m, :],
                                                    start=(m == 0), stop=(m == HB - 1))
                        last.then_inc(down_ready, 1)
                pe.wait_ge(gated, 1)
                for q in range(CHUNKS):
                    if q >= 1:
                        pe.wait_ge(turn_copied, q)
                    for j in range(4):
                        last = nc.tensor.transpose(turned[:, j * P:(j + 1) * P], share[:, q * 4 + j, :], c.ident[:P, :P])
                    last.then_inc(turn_ready, 1)
                for t in range(TILES):
                    i = EXPERTS * TILES + t
                    pe.wait_ge(turn_copied, t // 4 + 1)
                    pe.wait_ge(added, i - 3)
                    nc.tensor.matmul(down[:, i % 4, 0:DIM], share_T[:, t * P:(t + 1) * P], bd[:], start=True,
                                     stop=True).then_inc(down_ready, 1)

            @block.scalar
            def _(act):
                act.wait_ge(loaded, LOADS * 16)
                for q in range(CHUNKS):
                    for m in range(HB):
                        i = q * HB + m
                        act.wait_ge(up_ready, i + 1)
                        nc.scalar.activation(hidden[:, m, q * CHUNK:(q + 1) * CHUNK], up[:, i % 2, 0:CHUNK], ACT.Gelu,
                                             bias=b1[:, m:m + 1]).then_inc(hidden_ready, 1)
                scalar_gate(act)
                for q in range(CHUNKS):
                    act.wait_ge(turn_ready, q + 1)
                    nc.scalar.activation(share_T[:, q * CHUNK:(q + 1) * CHUNK], turned[:, 0:CHUNK],
                                         ACT.Copy).then_inc(turn_copied, 1)

            @block.vector
            def _(dve):
                dve.wait_ge(loaded, LOADS * 16)
                vector_gate(dve)
                with dve.Fori(0, EXPERTS) as e:
                    for t in range(TILES):
                        dve.wait_ge(down_ready, e * TILES + t + 1)
                        nc.vector.scalar_tensor_tensor(x[:, t, :], down[:, t % 4, 0:DIM], share[:, t, bass.ds(e, 1)],
                                                       x[:, t, :], ALU.mult, ALU.add).then_inc(added, 1)
                with dve.Fori(0, TILES) as t:
                    dve.wait_ge(down_ready, t + EXPERTS * TILES + 1)
                    nc.vector.tensor_tensor(row(x, t), down[:, bass.ds(t % 4, 1), 0:DIM].rearrange("p a d -> p (a d)"),
                                            row(x, t), ALU.add).then_inc(added, 1)


class Names:
    pass


def gps_layers(nc, A, out, upto=99):
    with ExitStack() as ctx:
        p, c = Program(nc, ctx), Names()
        constants(p, c)
        x = p.sb("x", [P, TILES, DIM])
        xn = p.sb("xn", [P, TILES, DIM + 1])
        xn_T = p.sb("xn_T", [128, KB, NODES])
        src = p.sb("src_cols", [P, EDGE_TILES], I32)
        dst = p.sb("dst_cols", [P, EDGE_TILES], I32)
        in_degree = p.sb("in_degree", [P, TILES])
        c.zero = p.sb("zero", [1, P], BF16)
        loaded = p.sem("x_loaded")
        with nc.Block() as block:
            @block.vector
            def _(dve):
                nc.vector.memset(c.zero[:], 0.0)
                nc.vector.memset(xn[:, :, DIM:DIM + 1], 1.0)

            @block.sync
            def _(sp):
                sp.dma_start(x[:], A["x"].rearrange("(t p) d -> p t d", p=P)).then_inc(loaded, 16)
                sp.dma_start(src[:], A["src_cols"]).then_inc(loaded, 16)
                sp.dma_start(dst[:], A["dst_cols"]).then_inc(loaded, 16)
                sp.wait_ge(loaded, 48)
        ranges0 = edge_ranges(p, "two", A, 2)
        ranges1 = edge_ranges(p, "four", A, 4)
        with ExitStack() as layer0:
            mean_in = p.sb("mean_in", [P, TILES, DIM], scope=layer0)
            mean_out = p.sb("mean_out", [P, TILES, DIM + 1], scope=layer0)
            mixer = p.sb("mixer", [128, KB, DIM], scope=layer0)
            layer_norm(p, c, "ln0", x, xn, xn_T)
            neighbour_means(p, c, ranges0, 2, xn, src, dst, mean_in, mean_out, in_degree)
            if upto >= 1:
                linear_attention(p, c, A, xn_T, mixer)
                sage_and_mix(p, c, A, x, xn_T, mean_in, mean_out, mixer)
        if upto >= 2:
            layer_norm(p, c, "ln1", x, xn, xn_T)
            mixture(p, c, A, x, xn, xn_T)
        if upto >= 3:
            p.clear_semaphores()
            layer1(p, c, A, x, xn, xn_T, ranges1, 4, src, dst, in_degree)
        if upto >= 4:
            layer_norm(p, c, "ln3", x, xn, xn_T)
            one_expert(p, c, A, x, xn_T)
        done = p.sem("done")
        with nc.Block() as block:
            @block.sync
            def _(sp):
                sp.dma_start(out.rearrange("(t p) d -> p t d", p=P), x[:]).then_inc(done, 16)
                sp.wait_ge(done, 16)


def laid_out(i):
    import numpy as np
    turn = lambda a: np.ascontiguousarray(np.asarray(a).T)
    keep = lambda a: np.ascontiguousarray(np.asarray(a))
    a = {
        "x": keep(i["x"]),
        "src_cols": turn(keep(i["src"]).reshape(EDGE_TILES, P)),
        "dst_cols": turn(keep(i["dst"]).reshape(EDGE_TILES, P)),
        "dst_blocks": keep(i["dst"]).reshape(RANGE_ROWS, -1),
        "edge_attr_T": np.ascontiguousarray(keep(i["edge_attr_256"]).reshape(EDGE_TILES, P, KB, 128).transpose(0, 3, 2, 1)),
        "wk_T": turn(i["L0_mix_wk"]), "wv_T": turn(i["L0_mix_wv"]), "wq": keep(i["L0_mix_wq"]), "wo_T": turn(i["L0_mix_wo"]),
        "ln_k_g": keep(i["L0_mix_ln_k_g"]), "ln_k_b": keep(i["L0_mix_ln_k_b"]),
        "ln_v_g": keep(i["L0_mix_ln_v_g"]), "ln_v_b": keep(i["L0_mix_ln_v_b"]),
        "W_l_f_T": turn(i["L0_gnn_W_l_f"]), "W_r_f_T": turn(i["L0_gnn_W_r_f"]), "b_l_f": keep(i["L0_gnn_b_l_f"]),
        "W_l_b_T": turn(i["L0_gnn_W_l_b"]), "W_r_b_T": turn(i["L0_gnn_W_r_b"]), "b_l_b": keep(i["L0_gnn_b_l_b"]),
        "bn_gamma": keep(i["L0_gnn_gamma"]), "bn_beta": keep(i["L0_gnn_beta"]), "bo": keep(i["L0_mix_bo"]),
        "router_T": turn(i["L0_ffn_router_w"]),
        "ffn0_b1_T": turn(keep(i["L0_ffn_b1"]).reshape(EXPERTS * KB, 128)),
        "ffn0_w1": keep(i["L0_ffn_w1"]), "ffn0_w2": keep(i["L0_ffn_w2"]), "ffn0_b2": keep(i["L0_ffn_b2"]),
        "gnn1_W1": keep(i["L1_gnn_W1"]), "gnn1_b1": keep(i["L1_gnn_b1"]),
        "gnn1_W2": keep(i["L1_gnn_W2"]), "gnn1_b2": keep(i["L1_gnn_b2"]),
        "Wqkv": keep(i["L1_mix_Wqkv"]), "Wout": keep(i["L1_mix_Wout"]), "mix1_gamma": keep(i["L1_mix_gamma"]),
        "ffn1_W1": keep(i["L1_ffn_W1"]), "ffn1_b1_T": turn(keep(i["L1_ffn_b1"]).reshape(HIDDEN // 128, 128)),
        "ffn1_Wg": keep(i["L1_ffn_Wg"]), "ffn1_bg": keep(i["L1_ffn_bg"]),
        "ffn1_Wd": keep(i["L1_ffn_Wd"]), "ffn1_bd": keep(i["L1_ffn_bd"]),
    }
    return a


def kernel(**inputs):
    import concourse.bacc as bacc
    from concourse.bass_utils import run_bass_kernel_spmd

    arrays = laid_out(inputs)
    nc = bacc.Bacc("TRN2", target_bir_lowering=False, num_devices=1)
    A = {n: nc.dram_tensor(f"in_{n}", a.shape, mybir.dt.from_np(a.dtype), kind="ExternalInput").ap()
         for n, a in arrays.items()}
    out = nc.dram_tensor("out", [NODES, DIM], F32, kind="ExternalOutput").ap()
    gps_layers(nc, A, out)
    result = run_bass_kernel_spmd(nc, [{f"in_{n}": a for n, a in arrays.items()}], core_ids=[0])
    return result.results[0]["out"]
```

```python
from contextlib import ExitStack, nullcontext

import concourse.bass as bass
from concourse import mybir

F32 = mybir.dt.float32
F16 = mybir.dt.float16
BF16 = mybir.dt.bfloat16
I32 = mybir.dt.int32
I16 = mybir.dt.int16
ALU = mybir.AluOpType
ACT = mybir.ActivationFunctionType
AX = mybir.AxisListType

NODES, DIM, EDGES = 2500, 256, 40000
P = 125
TILES = NODES // P
KB = DIM // 128
CHUNK = 4 * P
CHUNKS = NODES // CHUNK
EDGE_TILES = EDGES // P
RANGE_ROWS = 80
HEADS0, HEADS1, EXPERTS, HIDDEN = 4, 8, 8, 1024
ROW = 2 * DIM + 3
SHARE, NUMBER = 2 * DIM + 1, 2 * DIM + 2
HEAD0, HEAD1 = DIM // HEADS0, DIM // HEADS1
CROWD = 2048
LN_EPS = 1e-5


class Chain:

    def __init__(self, sem):
        self.sem, self.n = sem, 0

    def tick(self, instruction):
        self.n += 1
        instruction.then_inc(self.sem, 1)

    def wait(self, engine):
        engine.wait_ge(self.sem, self.n)


class Program:

    def __init__(self, nc, ctx):
        self.nc, self.ctx = nc, ctx
        self.used, self.free = [], []

    def sb(self, name, shape, dtype=F32, scope=None):
        return (scope or self.ctx).enter_context(self.nc.sbuf_tensor(name, shape, dtype))

    def ps(self, name, shape, dtype=F32, scope=None):
        return (scope or self.ctx).enter_context(self.nc.psum_tensor(name, shape, dtype))

    def sem(self, name):
        sem = self.free.pop() if self.free else self.ctx.enter_context(self.nc.semaphore(name))
        self.used.append(sem)
        return sem

    def clear_semaphores(self):
        done, self.used = self.used, []
        with self.nc.Block() as block:
            for n, engine in enumerate((block.sync, block.gpsimd, block.scalar, block.vector, block.tensor)):
                @engine
                def _(e, share=done[n::5]):
                    for sem in share:
                        e.sem_clear(sem)
        self.free = done + self.free


def row(x, t):
    return x[:, bass.ds(t, 1), :].rearrange("p a d -> p (a d)")


def inverse_root(dve, nc, chain, root, value, work):
    chain.tick(nc.vector.reciprocal(root[:], root[:]))
    chain.wait(dve)
    chain.tick(nc.vector.tensor_tensor(work[:], root[:], root[:], ALU.mult))
    chain.wait(dve)
    chain.tick(nc.vector.scalar_tensor_tensor(work[:], work[:], -0.5, value[:], ALU.mult, ALU.mult))
    chain.wait(dve)
    chain.tick(nc.vector.scalar_tensor_tensor(root[:], work[:], 1.5, root[:], ALU.add, ALU.mult))
    chain.wait(dve)


def constants(p, c, scope):
    nc = p.nc
    c.iota_node_i = p.sb("iota_node_i", [P, NODES], I16, scope)
    made = p.sem("constants_made")
    with nc.Block() as block:
        @block.gpsimd
        def _(pool):
            nc.gpsimd.memset(c.ident[:], 0.0)
            nc.gpsimd.memset(c.ones[:], 1.0)
            nc.gpsimd.iota(c.iota_node_i[:], [[1, NODES]], base=0, channel_multiplier=0).then_inc(made, 1)
            pool.wait_ge(made, 1)
            nc.gpsimd.affine_select(out=c.ident[:], in_=c.ident[:], compare_op=ALU.not_equal, fill=1.0,
                                    base=0, pattern=[[-1, 128]], channel_multiplier=1).then_inc(made, 1)


def layer_norm(p, c, name, x, xn, xn_T, xn_dram=None):
    nc = p.nc
    with ExitStack() as scope:
        stats = p.sb(f"{name}_stats", [P, TILES * 6], scope=scope)
        mean = p.sb(f"{name}_mean", [P, TILES], scope=scope)
        var = p.sb(f"{name}_var", [P, TILES], scope=scope)
        half = p.sb(f"{name}_half", [P, TILES], scope=scope)
        std = p.sb(f"{name}_std", [P, TILES], scope=scope)
        turned = p.ps(f"{name}_turned", [128, 4, 512], scope=scope)
        chain = Chain(p.sem(f"{name}_chain"))
        var_ready, std_ready = p.sem(f"{name}_var_ready"), p.sem(f"{name}_std_ready")
        normed, transposed, copied = p.sem(f"{name}_normed"), p.sem(f"{name}_transposed"), p.sem(f"{name}_copied")
        stored, measured = p.sem(f"{name}_stored"), p.sem(f"{name}_measured")
        s = stats[:].rearrange("p (t k) -> p k t", k=6)
        with nc.Block() as block:
            @block.vector
            def _(dve):
                with dve.Fori(0, TILES) as t:
                    nc.vector.bn_stats(stats[:, bass.ds(t * 6, 6)], row(x, t)).then_inc(measured, 1)
                dve.wait_ge(measured, TILES)
                chain.wait(dve)
                nc.vector.tensor_tensor(half[:], s[:, 1, :], s[:, 4, :], ALU.subtract)
                nc.vector.tensor_tensor(mean[:], s[:, 1, :], s[:, 4, :], ALU.add)
                chain.tick(nc.vector.tensor_tensor(var[:], s[:, 2, :], s[:, 5, :], ALU.add))
                chain.wait(dve)
                nc.vector.tensor_scalar(mean[:], mean[:], 0.5, None, ALU.mult)
                chain.tick(nc.vector.scalar_tensor_tensor(half[:], half[:], 0.25, half[:], ALU.mult, ALU.mult))
                chain.wait(dve)
                chain.tick(nc.vector.scalar_tensor_tensor(var[:], var[:], 1.0 / DIM, half[:], ALU.mult, ALU.add))
                chain.wait(dve)
                nc.vector.tensor_scalar(var[:], var[:], LN_EPS, None, ALU.add).then_inc(var_ready, 1)
                dve.wait_ge(std_ready, 1)
                inverse_root(dve, nc, chain, std, var, half)
                with dve.Fori(0, TILES) as t:
                    nc.vector.tensor_scalar(xn[:, bass.ds(t, 1), 0:DIM].rearrange("p a d -> p (a d)"), row(x, t),
                                            mean[:, bass.ds(t, 1)], std[:, bass.ds(t, 1)],
                                            ALU.subtract, ALU.mult).then_inc(normed, 1)

            @block.tensor
            def _(pe):
                for t in range(TILES):
                    pe.wait_ge(normed, t + 1)
                    if t >= 4:
                        pe.wait_ge(copied, t - 3)
                    for k in range(KB):
                        last = nc.tensor.transpose(turned[:, t % 4, k * P:(k + 1) * P],
                                                   xn[:, t, k * 128:(k + 1) * 128], c.ident[:P, :P])
                    last.then_inc(transposed, 1)

            @block.scalar
            def _(act):
                act.wait_ge(var_ready, 1)
                nc.scalar.activation(std[:], var[:], ACT.Sqrt).then_inc(std_ready, 1)
                with act.Fori(0, TILES) as t:
                    act.wait_ge(transposed, t + 1)
                    nc.scalar.activation(xn_T[:, :, bass.ds(t * P, P)],
                                         turned[:, bass.ds(t % 4, 1), 0:KB * P].rearrange("p a (k n) -> p (a k) n", k=KB),
                                         ACT.Copy).then_inc(copied, 1)

            @block.sync
            def _(sp):
                if xn_dram is not None:
                    sp.wait_ge(normed, TILES)
                    sp.dma_start(xn_dram.rearrange("(t p) d -> p t d", p=P), xn[:, :, 0:DIM]).then_inc(stored, 16)
                    sp.wait_ge(stored, 16)


def edge_ranges(p, name, A, SUB, outer):
    nc = p.nc
    BLOCKS = EDGE_TILES // SUB
    ROWS_IN_RANGES, PER_ROW = RANGE_ROWS, BLOCKS // RANGE_ROWS
    ranges = p.sb(f"{name}_ranges", [1, 3 * TILES], I32, outer)
    low_dram = nc.dram_tensor(f"{name}_low_dram", [BLOCKS], F32).ap()
    high_dram = nc.dram_tensor(f"{name}_high_dram", [BLOCKS], F32).ap()
    ranges_dram = nc.dram_tensor(f"{name}_ranges_dram", [TILES, 3], I32).ap()
    with ExitStack() as scope:
        dst = p.sb(f"{name}_dst_by_block", [ROWS_IN_RANGES, PER_ROW, SUB * P], I32, scope)
        low = p.sb(f"{name}_block_low", [ROWS_IN_RANGES, PER_ROW], F32, scope)
        high = p.sb(f"{name}_block_high", [ROWS_IN_RANGES, PER_ROW], F32, scope)
        lows = p.sb(f"{name}_lows", [TILES, BLOCKS], F32, scope)
        highs = p.sb(f"{name}_highs", [TILES, BLOCKS], F32, scope)
        up_i = p.sb(f"{name}_up_i", [TILES, BLOCKS], I32, scope)
        up = p.sb(f"{name}_up", [TILES, BLOCKS], F32, scope)
        down = p.sb(f"{name}_down", [TILES, BLOCKS], F32, scope)
        start_i = p.sb(f"{name}_tile_start_i", [TILES, 1], I32, scope)
        start = p.sb(f"{name}_tile_start", [TILES, 1], F32, scope)
        end = p.sb(f"{name}_tile_end", [TILES, 1], F32, scope)
        earlier = p.sb(f"{name}_earlier", [TILES, TILES], F32, scope)
        first = p.sb(f"{name}_first", [TILES, 1], F32, scope)
        stop = p.sb(f"{name}_stop", [TILES, 1], F32, scope)
        found = p.sb(f"{name}_found", [TILES, 3], F32, scope)
        found_i = p.sb(f"{name}_found_i", [TILES, 3], I32, scope)
        base = p.ps(f"{name}_base", [TILES, 1], F32, scope)
        loaded, reduced, stored = p.sem(f"{name}_r_loaded"), p.sem(f"{name}_r_reduced"), p.sem(f"{name}_r_stored")
        made, counted, summed = p.sem(f"{name}_r_made"), p.sem(f"{name}_r_counted"), p.sem(f"{name}_r_summed")
        ready, kept = p.sem(f"{name}_r_ready"), p.sem(f"{name}_r_kept")
        chain = Chain(p.sem(f"{name}_r_chain"))
        with nc.Block() as block:
            @block.sync
            def _(sp):
                sp.dma_start(dst[:], A["dst_blocks"].rearrange("p (b e) -> p b e", b=PER_ROW)).then_inc(loaded, 16)
                sp.wait_ge(reduced, 1)
                sp.dma_start(low_dram.rearrange("(p b) -> p b", b=PER_ROW), low[:]).then_inc(stored, 16)
                sp.dma_start(high_dram.rearrange("(p b) -> p b", b=PER_ROW), high[:]).then_inc(stored, 16)
                sp.wait_ge(stored, 32)
                sp.dma_start(lows[:], low_dram.partition_broadcast(TILES)).then_inc(loaded, 16)
                sp.dma_start(highs[:], high_dram.partition_broadcast(TILES)).then_inc(loaded, 16)
                sp.wait_ge(ready, 1)
                sp.dma_start(ranges_dram, found_i[:]).then_inc(stored, 16)
                sp.wait_ge(stored, 48)
                sp.dma_start(ranges[:], ranges_dram.rearrange("t k -> (t k)").unsqueeze(0)).then_inc(kept, 16)
                sp.wait_ge(kept, 16)

            @block.gpsimd
            def _(pool):
                nc.gpsimd.iota(up_i[:], [[1, BLOCKS]], base=1, channel_multiplier=0)
                nc.gpsimd.iota(start_i[:], [[0, 1]], base=0, channel_multiplier=P)
                nc.gpsimd.memset(earlier[:], 1.0).then_inc(made, 1)
                pool.wait_ge(made, 1)
                nc.gpsimd.affine_select(out=earlier[:], in_=earlier[:], compare_op=ALU.is_gt, fill=0.0,
                                        base=0, pattern=[[1, TILES]], channel_multiplier=-1).then_inc(made, 1)

            @block.vector
            def _(dve):
                dve.wait_ge(loaded, 16)
                nc.vector.tensor_reduce(low[:], dst[:], AX.X, ALU.min)
                nc.vector.tensor_reduce(high[:], dst[:], AX.X, ALU.max).then_inc(reduced, 1)
                dve.wait_ge(made, 2)
                nc.vector.tensor_copy(up[:], up_i[:])
                chain.tick(nc.vector.tensor_copy(start[:], start_i[:]))
                chain.wait(dve)
                nc.vector.tensor_scalar(down[:], up[:], -1.0, float(BLOCKS + 1), ALU.mult, ALU.add)
                chain.tick(nc.vector.tensor_scalar(end[:], start[:], float(P - 1), None, ALU.add))
                dve.wait_ge(loaded, 48)
                chain.wait(dve)
                nc.vector.scalar_tensor_tensor(highs[:], highs[:], start[:], down[:], ALU.is_ge, ALU.mult)
                chain.tick(nc.vector.scalar_tensor_tensor(lows[:], lows[:], end[:], up[:], ALU.is_le, ALU.mult))
                chain.wait(dve)
                nc.vector.tensor_reduce(first[:], highs[:], AX.X, ALU.max)
                chain.tick(nc.vector.tensor_reduce(stop[:], lows[:], AX.X, ALU.max))
                chain.wait(dve)
                chain.tick(nc.vector.tensor_scalar(first[:], first[:], -1.0, float(BLOCKS), ALU.mult, ALU.add))
                chain.wait(dve)
                chain.tick(nc.vector.tensor_scalar(found[:, 0:1], first[:], float(BLOCKS - 1), None, ALU.min))
                chain.wait(dve)
                chain.tick(nc.vector.tensor_tensor(found[:, 1:2], stop[:], found[:, 0:1], ALU.subtract))
                chain.wait(dve)
                nc.vector.tensor_scalar(found[:, 1:2], found[:, 1:2], 1.0, None, ALU.max).then_inc(counted, 1)
                dve.wait_ge(summed, 1)
                chain.tick(nc.vector.tensor_copy(found[:, 2:3], base[:]))
                chain.wait(dve)
                nc.vector.tensor_copy(found_i[:], found[:]).then_inc(ready, 1)

            @block.tensor
            def _(pe):
                pe.wait_ge(made, 2)
                pe.wait_ge(counted, 1)
                nc.tensor.matmul(base[:], earlier[:], found[:, 1:2], start=True, stop=True).then_inc(summed, 1)
    return ranges


def load_range(engine, ranges, t, SUB):
    BLOCKS = EDGE_TILES // SUB
    return (engine.value_load(ranges[0:1, bass.ds(t * 3, 1)], min_val=0, max_val=BLOCKS - 1),
            engine.value_load(ranges[0:1, bass.ds(t * 3 + 1, 1)], min_val=1, max_val=BLOCKS),
            engine.value_load(ranges[0:1, bass.ds(t * 3 + 2, 1)], min_val=0, max_val=BLOCKS * TILES))


def only_if(engine, flag):
    return nullcontext() if flag is None else engine.If(engine.value_load(flag[0:1, 0:1], min_val=0, max_val=1) == 1)


def neighbour_sums(p, c, name, dtype, GROUP, ranges, SUB, xn, src, dst, sum_in, sum_out, flag=None):
    nc = p.nc
    W = DIM + 1
    BLOCKS = EDGE_TILES // SUB
    GROUPS = TILES // GROUP
    BATCH = 5 if dtype is F16 else 4
    BATCHES = TILES // BATCH
    with ExitStack() as scope:
        sb = lambda n, shape, dtype=F32: p.sb(f"{name}_{n}", shape, dtype, scope)
        sem = lambda n: p.sem(f"{name}_{n}")
        hot_src = sb("hot_src", [P, 2 * SUB, NODES], BF16)
        hot_dst = sb("hot_dst", [P, 2 * SUB, P], BF16)
        adj = sb("adj", [P, GROUP, NODES], dtype)
        adj_T = sb("adj_T", [P, TILES, P], dtype)
        dst_f = sb("dst_f", [P, EDGE_TILES])
        src_f = sb("src_f", [P, EDGE_TILES])
        if dtype is F16:
            parts = [sb("high", [P, TILES, W], F16), sb("low", [P, TILES, W], F16)]
            ident = sb("ident", [P, P], F16)
        else:
            parts, ident = [xn], c.ident
        rows = p.ps(f"{name}_rows", [P, CHUNKS, 512], scope=scope)
        turned = p.ps(f"{name}_turned", [P, 2, 1024 if dtype is F16 else 512], dtype, scope)
        bank_in = p.ps(f"{name}_bank_in", [P, 512], scope=scope)
        hot_ready = [sem(f"hot_ready{s}") for s in range(SUB)]
        hot_used = [sem(f"hot_used{s}") for s in range(SUB)]
        rows_copied, turn_ready, turn_copied = sem("rows_copied"), sem("turn_ready"), sem("turn_copied")
        in_ready, in_copied, out_ready, out_added = sem("in_ready"), sem("in_copied"), sem("out_ready"), sem("out_added")
        high_ready, parts_ready, floats_ready = sem("high_ready"), sem("parts_ready"), sem("floats_ready")
        buffer = lambda before, i, s: bass.ds(((before + i) % 2).with_bounds(min_val=0, max_val=1) * SUB + s, 1)
        flat = lambda a: a.rearrange("p a n -> p (a n)")
        with nc.Block() as block:
            @block.gpsimd
            def _(pool):
                with only_if(pool, flag):
                    if dtype is F16:
                        pool.wait_ge(high_ready, 1)
                        nc.gpsimd.tensor_tensor(parts[1][:], xn[:], parts[0][:], ALU.subtract).then_inc(parts_ready, 1)

            @block.vector
            def _(dve):
                def build(t):
                    lo, n, before = load_range(dve, ranges, t, SUB)
                    with dve.Fori(0, n) as i:
                        for s in range(SUB):
                            col = (lo + i).with_bounds(min_val=0, max_val=BLOCKS - 1) * SUB + s
                            dve.wait_ge(hot_used[s], before + i + 1)
                            nc.vector.tensor_scalar(flat(hot_src[:, buffer(before, i, s), :]), c.iota_node_i[:],
                                                    src_f[:, bass.ds(col, 1)], None, ALU.is_equal)
                            nc.vector.tensor_scalar(flat(hot_dst[:, buffer(before, i, s), :]), c.iota_node_i[:, bass.ds(t * P, P)],
                                                    dst_f[:, bass.ds(col, 1)], None,
                                                    ALU.is_equal).then_inc(hot_ready[s], 1)

                def keep_turned(t):
                    for b in range(BATCHES):
                        dve.wait_ge(turn_ready, t * BATCHES + b + 1)
                        nc.vector.tensor_copy(adj_T[:, b * BATCH:(b + 1) * BATCH, :],
                                              turned[:, b % 2, 0:BATCH * 128].rearrange("p (j n) -> p j n", j=BATCH)[:, :, 0:P]
                                              ).then_inc(turn_copied, 1)

                with only_if(dve, flag):
                    nc.vector.tensor_copy(src_f[:], src[:])
                    nc.vector.tensor_copy(dst_f[:], dst[:])
                    nc.vector.memset(sum_out[:], 0.0).then_inc(floats_ready, 1)
                    dve.wait_ge(floats_ready, 1)
                    dve.sem_inc(turn_copied, 2)
                    dve.sem_inc(out_added, 1)
                    with dve.Fori(0, GROUPS) as g:
                        build(g * GROUP)
                        for tt in range(GROUP):
                            if tt + 1 < GROUP:
                                build(g * GROUP + tt + 1)
                            keep_turned(g * GROUP + tt)
                        for s in range(TILES):
                            dve.wait_ge(out_ready, g * TILES + s + 1)
                            nc.vector.tensor_tensor(sum_out[:, s, :], rows[:, s % CHUNKS, 0:W], sum_out[:, s, :],
                                                    ALU.add).then_inc(out_added, 1)

            @block.tensor
            def _(pe):
                def build(t):
                    lo, n, before = load_range(pe, ranges, t, SUB)
                    pe.wait_ge(rows_copied, t + 1)
                    for q in range(CHUNKS):
                        nc.tensor.matmul(rows[:, q, 0:2], c.zero[:], c.zero[:, 0:2], start=True, stop=False,
                                         skip_group_check=True)
                    with pe.Fori(0, n) as i:
                        for s in range(SUB):
                            pe.wait_ge(hot_ready[s], before + i + 1)
                            for q in range(CHUNKS):
                                last = nc.tensor.matmul(rows[:, q, 0:CHUNK], flat(hot_dst[:, buffer(before, i, s), :]),
                                                        flat(hot_src[:, buffer(before, i, s), q * CHUNK:(q + 1) * CHUNK]),
                                                        start=False, stop=(s == SUB - 1), skip_group_check=True)
                            last.then_inc(hot_used[s], 1)

                def turn(t, tt, b):
                    pe.wait_ge(turn_copied, t * BATCHES + b + 1)
                    for j in range(BATCH):
                        s = b * BATCH + j
                        last = nc.tensor.transpose(turned[:, b % 2, j * 128:j * 128 + P],
                                                   adj[:, tt, s * P:(s + 1) * P], ident[:P, :P])
                    last.then_inc(turn_ready, 1)

                def sum_sources(t, tt):
                    pe.wait_ge(rows_copied, t + 2)
                    turn(t, tt, 0)
                    pe.wait_ge(in_copied, t + 1)
                    for b in range(BATCHES):
                        if b + 1 < BATCHES:
                            turn(t, tt, b + 1)
                        pe.wait_ge(turn_copied, t * BATCHES + b + 3)
                        for s in range(b * BATCH, (b + 1) * BATCH):
                            for part in parts:
                                last = nc.tensor.matmul(bank_in[:, 0:W], adj_T[:, s, :], part[:, s, :],
                                                        start=(s == 0 and part is parts[0]),
                                                        stop=(s == TILES - 1 and part is parts[-1]))
                    last.then_inc(in_ready, 1)

                with only_if(pe, flag):
                    for s in range(SUB):
                        pe.sem_inc(hot_used[s], 2)
                    with pe.Fori(0, GROUPS) as g:
                        build(g * GROUP)
                        if dtype is F16:
                            pe.wait_ge(parts_ready, 1)
                        for tt in range(GROUP):
                            if tt + 1 < GROUP:
                                build(g * GROUP + tt + 1)
                            sum_sources(g * GROUP + tt, tt)
                        pe.wait_ge(rows_copied, g * GROUP + GROUP + 1)
                        for s in range(TILES):
                            if s >= CHUNKS:
                                pe.wait_ge(out_added, g * TILES + s - CHUNKS + 2)
                            for tt in range(GROUP):
                                for part in parts:
                                    last = nc.tensor.matmul(rows[:, s % CHUNKS, 0:W], adj[:, tt, s * P:(s + 1) * P],
                                                            flat(part[:, bass.ds(g * GROUP + tt, 1), :]),
                                                            start=(tt == 0 and part is parts[0]),
                                                            stop=(tt == GROUP - 1 and part is parts[-1]))
                            last.then_inc(out_ready, 1)
                        pe.wait_ge(out_added, g * TILES + TILES + 1)

            @block.scalar
            def _(act):
                def keep_rows(t, tt):
                    lo, n, before = load_range(act, ranges, t, SUB)
                    act.wait_ge(hot_used[SUB - 1], before + n + 2)
                    if tt == 0:
                        act.wait_ge(out_added, (t - tt) * (TILES // GROUP) + 1)
                    nc.scalar.activation(adj[:, tt, :].rearrange("p (q n) -> p q n", q=CHUNKS), rows[:, :, 0:CHUNK],
                                         ACT.Copy).then_inc(rows_copied, 1)

                def keep_sum(t):
                    act.wait_ge(in_ready, t + 1)
                    nc.scalar.activation(row(sum_in, t), bank_in[:, 0:W], ACT.Copy).then_inc(in_copied, 1)

                with only_if(act, flag):
                    if dtype is F16:
                        nc.scalar.activation(ident[:], c.ident[:P, :P], ACT.Copy)
                        nc.scalar.activation(parts[0][:], xn[:], ACT.Copy).then_inc(high_ready, 1)
                    act.sem_inc(rows_copied, 1)
                    act.sem_inc(in_copied, 1)
                    with act.Fori(0, GROUPS) as g:
                        keep_rows(g * GROUP, 0)
                        for tt in range(GROUP):
                            if tt + 1 < GROUP:
                                keep_rows(g * GROUP + tt + 1, tt + 1)
                            keep_sum(g * GROUP + tt)


def neighbour_means(p, c, ranges, SUB, xn, src, dst, mean_in, mean_out, in_degree):
    nc = p.nc
    W = DIM + 1
    neighbour_sums(p, c, "nm", F16, 5, ranges, SUB, xn, src, dst, mean_in, mean_out)
    with ExitStack() as scope:
        most = p.sb("nm_most", [P, 1], scope=scope)
        most_of_all = p.sb("nm_most_of_all", [1, 1], scope=scope)
        crowded = p.sb("nm_crowded", [1, 1], I32, scope)
        chain, most_ready, most_turned = Chain(p.sem("nm_most_chain")), p.sem("nm_most_ready"), p.sem("nm_most_turned")
        with nc.psum_tensor("nm_most_T", [1, P], F32) as most_T, nc.Block() as block:
            @block.vector
            def _(dve):
                nc.vector.tensor_reduce(most[:], mean_in[:, :, DIM], AX.X, ALU.max).then_inc(most_ready, 1)
                dve.wait_ge(most_turned, 1)
                chain.tick(nc.vector.tensor_reduce(most_of_all[:], most_T[:], AX.X, ALU.max))
                chain.wait(dve)
                nc.vector.tensor_scalar(crowded[:], most_of_all[:], float(CROWD), None, ALU.is_ge)

            @block.tensor
            def _(pe):
                pe.wait_ge(most_ready, 1)
                nc.tensor.transpose(most_T[:], most[:], c.ident[:P, :P]).then_inc(most_turned, 1)
        neighbour_sums(p, c, "ns", F32, 2, ranges, SUB, xn, src, dst, mean_in, mean_out, crowded)
        degrees = p.sb("nm_degrees", [P, 2, TILES, 1], scope=scope)
        chain = Chain(p.sem("nm_chain"))
        with nc.Block() as block:
            @block.vector
            def _(dve):
                nc.vector.tensor_copy(in_degree[:].unsqueeze(2), mean_in[:, :, DIM:W])
                for d, sums in enumerate((mean_in, mean_out)):
                    chain.tick(nc.vector.tensor_scalar(degrees[:, d], sums[:, :, DIM:W], 1.0, None, ALU.max))
                chain.wait(dve)
                chain.tick(nc.vector.reciprocal(degrees[:], degrees[:]))
                chain.wait(dve)
                for d, sums in enumerate((mean_in, mean_out)):
                    nc.vector.tensor_tensor(sums[:, :, 0:DIM], sums[:, :, 0:DIM],
                                            degrees[:, d].broadcast_to([P, TILES, DIM]), ALU.mult)


def linear_attention(p, c, A, xn_T, mixer):
    nc = p.nc
    GROUPS = 2 * HEADS0
    with ExitStack() as scope:
        sb = lambda name, shape, dtype=F32: p.sb("la_" + name, shape, dtype, scope)
        w_kv = sb("w_kv", [128, KB, 2 * DIM])
        w_q = sb("w_q", [128, KB, DIM])
        w_o = sb("w_o", [128, KB, DIM])
        gain = sb("gain", [P, 2, HEAD0])
        shift = sb("shift", [P, 2, HEAD0])
        kv = sb("kv", [P, TILES, 2 * DIM])
        square = sb("square", [P, 2, 2 * DIM])
        total = sb("total", [P, GROUPS])
        var = sb("var", [P, TILES * GROUPS])
        std = sb("std", [P, TILES * GROUPS])
        work = sb("work", [P, TILES * GROUPS])
        heads_vk = sb("heads_vk", [128, KB, 128])
        kv_wo = sb("kv_wo", [128, KB, DIM])
        projected = p.ps("la_projected", [P, 2, 512], scope=scope)
        vk = p.ps("la_vk", [128, KB, 512], scope=scope)
        product = p.ps("la_product", [128, KB, 512], scope=scope)
        loaded, projected_ready, centred = p.sem("la_loaded"), p.sem("la_projected_ready"), p.sem("la_centred")
        squared, summed = p.sem("la_squared"), p.sem("la_summed")
        var_ready, std_ready, scaled, shifted = (p.sem("la_var_ready"), p.sem("la_std_ready"), p.sem("la_scaled"),
                                                 p.sem("la_shifted"))
        gained, vk_ready, heads_ready = p.sem("la_gained"), p.sem("la_vk_ready"), p.sem("la_heads_ready")
        kv_wo_ready, kv_wo_kept, mixer_ready = p.sem("la_kv_wo_ready"), p.sem("la_kv_wo_kept"), p.sem("la_mixer_ready")
        zeroed, totalled = p.sem("la_zeroed"), p.sem("la_totalled")
        chain = Chain(p.sem("la_chain"))
        by_head = lambda x: x.rearrange("p (h d) -> p h d", d=HEAD0)
        with nc.Block() as block:
            @block.sync
            def _(sp):
                sp.dma_start(w_kv[:, :, 0:DIM], A["wk_T"].rearrange("(k p) n -> p k n", p=128)).then_inc(loaded, 16)
                sp.dma_start(w_kv[:, :, DIM:], A["wv_T"].rearrange("(k p) n -> p k n", p=128)).then_inc(loaded, 16)
                sp.dma_start(w_q[:], A["wq"].rearrange("(k p) n -> p k n", p=128)).then_inc(loaded, 16)
                sp.dma_start(w_o[:], A["wo_T"].rearrange("(k p) n -> p k n", p=128)).then_inc(loaded, 16)
                for n, (g, b) in enumerate((("ln_k_g", "ln_k_b"), ("ln_v_g", "ln_v_b"))):
                    sp.dma_start(gain[:, n, :], A[g].partition_broadcast(P)).then_inc(loaded, 16)
                    sp.dma_start(shift[:, n, :], A[b].partition_broadcast(P)).then_inc(loaded, 16)
                sp.wait_ge(loaded, 8 * 16)

            @block.tensor
            def _(pe):
                pe.wait_ge(loaded, 8 * 16)
                for t in range(TILES):
                    if t >= 2:
                        pe.wait_ge(centred, t - 1)
                    for k in range(KB):
                        last = nc.tensor.matmul(projected[:, t % 2, :], xn_T[:, k, t * P:(t + 1) * P], w_kv[:, k, :],
                                                start=(k == 0), stop=(k == KB - 1))
                    last.then_inc(projected_ready, 1)
                for t in range(TILES):
                    pe.wait_ge(shifted, t + 1)
                    for b in range(KB):
                        last = nc.tensor.matmul(vk[:, b, 0:128], kv[:, t, DIM + b * 128:DIM + (b + 1) * 128],
                                                kv[:, t, b * 128:(b + 1) * 128], start=(t == 0), stop=(t == TILES - 1))
                last.then_inc(vk_ready, 1)
                pe.wait_ge(heads_ready, 1)
                for b in range(KB):
                    last = nc.tensor.matmul(product[:, b, 0:DIM], heads_vk[:, b, :], w_o[:, b, :], start=True, stop=True)
                last.then_inc(kv_wo_ready, 1)
                pe.wait_ge(kv_wo_kept, 1)
                for m in range(KB):
                    for b in range(KB):
                        last = nc.tensor.matmul(product[:, m, 0:DIM], w_q[:, b, m * 128:(m + 1) * 128], kv_wo[:, b, :],
                                                start=(b == 0), stop=(b == KB - 1))
                last.then_inc(mixer_ready, 1)

            @block.vector
            def _(dve):
                nc.vector.memset(heads_vk[:], 0.0).then_inc(zeroed, 1)
                with dve.Fori(0, TILES) as t:
                    tile = by_head(projected[:, bass.ds(t % 2, 1), :].rearrange("p a d -> p (a d)"))
                    dve.wait_ge(projected_ready, t + 1)
                    nc.vector.tensor_reduce(total[:], tile, AX.X, ALU.add).then_inc(totalled, 1)
                    dve.wait_ge(totalled, t + 1)
                    nc.vector.scalar_tensor_tensor(by_head(row(kv, t)), total[:].unsqueeze(2).broadcast_to([P, GROUPS, HEAD0]),
                                                   -1.0 / HEAD0, tile, ALU.mult, ALU.add).then_inc(centred, 1)
                    dve.wait_ge(squared, t + 1)
                    nc.vector.tensor_reduce(var[:, bass.ds(t * GROUPS, GROUPS)],
                                            by_head(square[:, bass.ds(t % 2, 1), :].rearrange("p a d -> p (a d)")),
                                            AX.X, ALU.add).then_inc(summed, 1)
                dve.wait_ge(summed, TILES)
                nc.vector.tensor_scalar(var[:], var[:], 1.0 / HEAD0, LN_EPS, ALU.mult, ALU.add).then_inc(var_ready, 1)
                dve.wait_ge(std_ready, 1)
                inverse_root(dve, nc, chain, std, var, work)
                with dve.Fori(0, TILES) as t:
                    nc.vector.tensor_tensor(by_head(row(kv, t)), by_head(row(kv, t)),
                                            std[:, bass.ds(t * GROUPS, GROUPS)].unsqueeze(2).broadcast_to([P, GROUPS, HEAD0]),
                                            ALU.mult).then_inc(scaled, 1)

            @block.gpsimd
            def _(pool):
                pool.wait_ge(loaded, 8 * 16)
                for t in range(TILES):
                    tile = row(kv, t).rearrange("p (n h d) -> p n h d", n=2, d=HEAD0)
                    pool.wait_ge(scaled, t + 1)
                    nc.gpsimd.tensor_tensor(tile, tile, gain[:].unsqueeze(2).broadcast_to([P, 2, HEADS0, HEAD0]),
                                            ALU.mult).then_inc(gained, 1)
                    pool.wait_ge(gained, t + 1)
                    nc.gpsimd.tensor_tensor(tile, tile, shift[:].unsqueeze(2).broadcast_to([P, 2, HEADS0, HEAD0]),
                                            ALU.add).then_inc(shifted, 1)

            @block.scalar
            def _(act):
                with act.Fori(0, TILES) as t:
                    act.wait_ge(centred, t + 1)
                    nc.scalar.activation(square[:, bass.ds(t % 2, 1), :].rearrange("p a d -> p (a d)"), row(kv, t),
                                         ACT.Square).then_inc(squared, 1)
                act.wait_ge(var_ready, 1)
                nc.scalar.activation(std[:], var[:], ACT.Sqrt).then_inc(std_ready, 1)
                act.wait_ge(vk_ready, 1)
                act.wait_ge(zeroed, 1)
                for b in range(KB):
                    for h in range(128 // HEAD0):
                        d = slice(h * HEAD0, (h + 1) * HEAD0)
                        last = nc.scalar.activation(heads_vk[d, b, d], vk[d, b, d], ACT.Copy, scale=1.0 / NODES)
                last.then_inc(heads_ready, 1)
                act.wait_ge(kv_wo_ready, 1)
                nc.scalar.activation(kv_wo[:], product[:, :, 0:DIM], ACT.Copy).then_inc(kv_wo_kept, 1)
                act.wait_ge(mixer_ready, 1)
                nc.scalar.activation(mixer[:], product[:, :, 0:DIM], ACT.Copy)


def sage_and_mix(p, c, A, x, xn_T, mean_in, mean_out, mixer):
    nc = p.nc
    HALF = DIM // 2
    with ExitStack() as scope:
        sb = lambda name, shape, dtype=F32: p.sb("sg_" + name, shape, dtype, scope)
        w_r = sb("w_r", [128, KB, DIM])
        w_l = sb("w_l", [128, 2, KB, HALF])
        bias, gamma, beta, bo = (sb(n, [P, DIM]) for n in ("bias", "gamma", "beta", "bo"))
        means_T = sb("means_T", [128, 2, 2 * KB * P])
        h = mean_in
        square = sb("square", [P, 2, DIM])
        average, var, std, work = (sb(n, [P, DIM]) for n in ("average", "var", "std", "work"))
        turned = p.ps("sg_turned", [128, 2, 512], scope=scope)
        projected = p.ps("sg_projected", [P, 2, 512], scope=scope)
        sums = p.ps("sg_sums", [P, 2, 512], scope=scope)
        mixed = p.ps("sg_mixed", [P, 2, 512], scope=scope)
        loaded, turn_ready, turn_copied = p.sem("sg_loaded"), p.sem("sg_turn_ready"), p.sem("sg_turn_copied")
        projected_ready, h_ready = p.sem("sg_projected_ready"), p.sem("sg_h_ready")
        sum_ready, centred, squared, square_summed = (p.sem("sg_sum_ready"), p.sem("sg_centred"), p.sem("sg_squared"),
                                                      p.sem("sg_square_summed"))
        var_ready, std_ready = p.sem("sg_var_ready"), p.sem("sg_std_ready")
        scaled, shifted, mixed_ready, added, finished = (p.sem("sg_scaled"), p.sem("sg_shifted"), p.sem("sg_mixed_ready"),
                                                         p.sem("sg_added"), p.sem("sg_finished"))
        chain = Chain(p.sem("sg_chain"))
        LOADS = 9
        with nc.Block() as block:
            @block.sync
            def _(sp):
                by_block = lambda a: a.rearrange("(k p) n -> p k n", p=128)
                for d, (l, r, b) in enumerate((("W_l_f_T", "W_r_f_T", "b_l_f"), ("W_l_b_T", "W_r_b_T", "b_l_b"))):
                    at = slice(d * HALF, (d + 1) * HALF)
                    sp.dma_start(w_r[:, :, at], by_block(A[r])).then_inc(loaded, 16)
                    sp.dma_start(w_l[:, d, :, :], by_block(A[l])).then_inc(loaded, 16)
                    sp.dma_start(bias[:, at], A[b].partition_broadcast(P)).then_inc(loaded, 16)
                for to, name in ((gamma, "bn_gamma"), (beta, "bn_beta"), (bo, "bo")):
                    sp.dma_start(to[:], A[name].partition_broadcast(P)).then_inc(loaded, 16)
                sp.wait_ge(loaded, LOADS * 16)

            @block.tensor
            def _(pe):
                def turn(t):
                    if t >= 2:
                        pe.wait_ge(turn_copied, t - 1)
                    for d, means in enumerate((mean_in, mean_out)):
                        for k in range(KB):
                            n = d * KB + k
                            last = nc.tensor.transpose(turned[:, t % 2, n * P:(n + 1) * P],
                                                       means[:, t, k * 128:(k + 1) * 128], c.ident[:P, :P])
                    last.then_inc(turn_ready, 1)

                pe.wait_ge(loaded, LOADS * 16)
                turn(0)
                for t in range(TILES):
                    if t + 1 < TILES:
                        turn(t + 1)
                    if t >= 2:
                        pe.wait_ge(h_ready, t - 1)
                    for k in range(KB):
                        nc.tensor.matmul(projected[:, t % 2, 0:DIM], xn_T[:, k, t * P:(t + 1) * P], w_r[:, k, :],
                                         start=(k == 0), stop=False, skip_group_check=True)
                    pe.wait_ge(turn_copied, t + 1)
                    for d in range(2):
                        for k in range(KB):
                            n = d * KB + k
                            last = nc.tensor.matmul(projected[:, t % 2, d * HALF:(d + 1) * HALF],
                                                    means_T[:, t % 2, n * P:(n + 1) * P], w_l[:, d, k, :],
                                                    start=False, stop=(k == KB - 1), skip_group_check=True)
                    last.then_inc(projected_ready, 1)
                for t in range(TILES):
                    pe.wait_ge(h_ready, t + 1)
                    last = nc.tensor.matmul(sums[:, 0, 0:DIM], c.ones[:P, :P], h[:, t, :],
                                            start=(t == 0), stop=(t == TILES - 1))
                last.then_inc(sum_ready, 1)
                for t in range(TILES):
                    pe.wait_ge(squared, t + 1)
                    last = nc.tensor.matmul(sums[:, 1, 0:DIM], c.ones[:P, :P], square[:, t % 2, :],
                                            start=(t == 0), stop=(t == TILES - 1))
                    last.then_inc(square_summed, 1)
                for t in range(TILES):
                    if t >= 2:
                        pe.wait_ge(added, t - 1)
                    for k in range(KB):
                        last = nc.tensor.matmul(mixed[:, t % 2, 0:DIM], xn_T[:, k, t * P:(t + 1) * P], mixer[:, k, :],
                                                start=(k == 0), stop=(k == KB - 1))
                    last.then_inc(mixed_ready, 1)

            @block.scalar
            def _(act):
                with act.Fori(0, TILES) as t:
                    act.wait_ge(turn_ready, t + 1)
                    nc.scalar.activation(means_T[:, bass.ds(t % 2, 1), :].rearrange("p a d -> p (a d)"),
                                         turned[:, bass.ds(t % 2, 1), 0:2 * KB * P].rearrange("p a d -> p (a d)"),
                                         ACT.Copy).then_inc(turn_copied, 1)
                act.sem_inc(square_summed, 2)
                with act.Fori(0, TILES) as t:
                    act.wait_ge(centred, t + 1)
                    act.wait_ge(square_summed, t + 1)
                    nc.scalar.activation(square[:, bass.ds(t % 2, 1), :].rearrange("p a d -> p (a d)"), row(h, t),
                                         ACT.Square).then_inc(squared, 1)
                act.wait_ge(var_ready, 1)
                nc.scalar.activation(std[:], var[:], ACT.Sqrt).then_inc(std_ready, 1)

            @block.vector
            def _(dve):
                dve.wait_ge(loaded, LOADS * 16)
                with dve.Fori(0, TILES) as t:
                    dve.wait_ge(projected_ready, t + 1)
                    nc.vector.tensor_tensor(row(h, t), projected[:, bass.ds(t % 2, 1), 0:DIM].rearrange("p a d -> p (a d)"),
                                            bias[:], ALU.add).then_inc(h_ready, 1)
                dve.wait_ge(sum_ready, 1)
                chain.tick(nc.vector.tensor_scalar(average[:], sums[:, 0, 0:DIM], 1.0 / NODES, None, ALU.mult))
                chain.wait(dve)
                with dve.Fori(0, TILES) as t:
                    nc.vector.tensor_tensor(row(h, t), row(h, t), average[:], ALU.subtract).then_inc(centred, 1)
                dve.wait_ge(square_summed, TILES + 2)
                chain.tick(nc.vector.tensor_scalar(var[:], sums[:, 1, 0:DIM], 1.0 / NODES, LN_EPS, ALU.mult, ALU.add))
                chain.wait(dve)
                nc.vector.engine_nop().then_inc(var_ready, 1)
                dve.wait_ge(std_ready, 1)
                inverse_root(dve, nc, chain, std, var, work)
                chain.tick(nc.vector.tensor_tensor(std[:], std[:], gamma[:], ALU.mult))
                chain.wait(dve)
                dve.wait_ge(centred, TILES)
                with dve.Fori(0, TILES) as t:
                    nc.vector.tensor_tensor(row(h, t), row(h, t), std[:], ALU.mult).then_inc(scaled, 1)
                with dve.Fori(0, TILES) as t:
                    dve.wait_ge(mixed_ready, t + 1)
                    dve.wait_ge(finished, t + 1)
                    nc.vector.tensor_tensor(row(x, t), mixed[:, bass.ds(t % 2, 1), 0:DIM].rearrange("p a d -> p (a d)"),
                                            row(x, t), ALU.add).then_inc(added, 1)
                    dve.wait_ge(shifted, t + 1)
                    dve.wait_ge(added, t + 1)
                    nc.vector.scalar_tensor_tensor(row(x, t), row(h, t), 0.0, row(x, t), ALU.max, ALU.add)

            @block.gpsimd
            def _(pool):
                pool.wait_ge(loaded, LOADS * 16)
                with pool.Fori(0, TILES) as t:
                    nc.gpsimd.tensor_tensor(row(x, t), row(x, t), bo[:], ALU.add).then_inc(finished, 1)
                for t in range(TILES):
                    pool.wait_ge(scaled, t + 1)
                    nc.gpsimd.tensor_tensor(row(h, t), row(h, t), beta[:], ALU.add).then_inc(shifted, 1)


class Gate:

    def __init__(self, p, scope, name, top, bias=None):
        self.nc, self.top, self.bias = p.nc, top, bias
        sb = lambda n, shape, dtype=F32: p.sb(f"{name}_{n}", shape, dtype, scope)
        self.raw, self.prob = sb("raw", [P, TILES, EXPERTS]), sb("prob", [P, TILES, EXPERTS])
        self.order_i, self.order = sb("order_i", [P, EXPERTS], I32), sb("order", [P, EXPERTS])
        self.peak, self.total, self.place = sb("peak", [P, TILES]), sb("total", [P, TILES]), sb("place", [P, TILES])
        self.chosen = [sb(f"chosen{n}", [P, TILES, EXPERTS]) for n in range(top)]
        self.best = [sb(f"best{n}", [P, TILES]) for n in range(top)]
        self.shifted, self.exped, self.numbered = (p.sem(f"{name}_shifted"), p.sem(f"{name}_exped"),
                                                   p.sem(f"{name}_numbered"))
        self.chain = Chain(p.sem(f"{name}_chain"))

    def pool_steps(self, pool):
        self.nc.gpsimd.iota(self.order_i[:], [[-1, EXPERTS]], base=EXPERTS, channel_multiplier=0).then_inc(self.numbered, 1)

    def scalar_steps(self, act):
        act.wait_ge(self.shifted, 1)
        self.nc.scalar.activation(self.prob[:], self.raw[:], ACT.Exp).then_inc(self.exped, 1)

    def vector_steps(self, dve, logits, ready, count):
        nc, chain = self.nc, self.chain
        over = lambda a: a[:].unsqueeze(2).broadcast_to([P, TILES, EXPERTS])
        across = lambda a: a[:].unsqueeze(1).broadcast_to([P, TILES, EXPERTS])

        def then(instruction):
            chain.tick(instruction)
            chain.wait(dve)

        dve.wait_ge(self.numbered, 1)
        nc.vector.tensor_copy(self.order[:], self.order_i[:])
        dve.wait_ge(ready, count)
        if self.bias is None:
            then(nc.vector.tensor_copy(self.raw[:], logits))
        else:
            then(nc.vector.tensor_tensor(self.raw[:], logits, across(self.bias), ALU.add))
        then(nc.vector.tensor_reduce(self.peak[:], self.raw[:], AX.X, ALU.max))
        nc.vector.tensor_tensor(self.raw[:], self.raw[:], over(self.peak), ALU.subtract).then_inc(self.shifted, 1)
        dve.wait_ge(self.exped, 1)
        then(nc.vector.tensor_reduce(self.total[:], self.prob[:], AX.X, ALU.add))
        then(nc.vector.reciprocal(self.total[:], self.total[:]))
        then(nc.vector.tensor_tensor(self.prob[:], self.prob[:], over(self.total), ALU.mult))
        for n in range(self.top):
            then(nc.vector.tensor_reduce(self.best[n][:], self.prob[:], AX.X, ALU.max))
            then(nc.vector.tensor_tensor(self.raw[:], self.prob[:], over(self.best[n]), ALU.is_equal))
            then(nc.vector.tensor_tensor(self.raw[:], self.raw[:], across(self.order), ALU.mult))
            then(nc.vector.tensor_reduce(self.place[:], self.raw[:], AX.X, ALU.max))
            then(nc.vector.tensor_tensor(self.chosen[n][:], self.raw[:], over(self.place), ALU.is_equal))
            if n + 1 < self.top:
                then(nc.vector.scalar_tensor_tensor(self.prob[:], self.chosen[n][:], -2.0, self.prob[:], ALU.mult, ALU.add))


class Dispatch:

    def __init__(self, p, c, scope, name, top):
        self.nc, self.c, self.top = p.nc, c, top
        self.tiles = (top * NODES + EXPERTS * (P - 1)) // P
        sb = lambda n, shape, dtype=F32: p.sb(f"{name}_{n}", shape, dtype, scope)
        W = TILES * EXPERTS
        self.width = W
        self.earlier = sb("earlier", [P, P])
        self.tile_start_i, self.tile_start = sb("tile_start_i", [P, top * TILES], I32), sb("tile_start", [P, top * TILES])
        self.tile_i, self.tile = sb("tile_i", [1, self.tiles], I32), sb("tile", [1, self.tiles])
        self.counts = [sb(f"counts{i}", [P, top * TILES, EXPERTS]) for i in range(2)]
        self.place = sb("place", [P, TILES, EXPERTS])
        self.size = sb("size", [P, EXPERTS])
        self.full = sb("full", [P, EXPERTS, top * TILES])
        self.first = [sb(f"first{i}", [P, EXPERTS]) for i in range(2)]
        self.own = sb("own", [1, self.tiles, EXPERTS - 1])
        self.owner_f, self.owner = sb("owner_f", [1, self.tiles]), sb("owner", [1, self.tiles], I32)
        self.slot_f = sb("slot_f", [P, TILES])
        self.slot = [sb(f"slot{n}", [P, TILES], I32) for n in range(top)]
        self.before = p.ps(f"{name}_before", [P, top, W], scope=scope)
        self.number = p.ps(f"{name}_number", [P, top, W], scope=scope)
        self.made, self.counted, self.ready = p.sem(f"{name}_made"), p.sem(f"{name}_counted"), p.sem(f"{name}_ready")
        self.chosen_ready = p.sem(f"{name}_chosen_ready")
        self.chain = Chain(p.sem(f"{name}_chain"))

    def pool_steps(self, pool):
        nc = self.nc
        nc.gpsimd.memset(self.earlier[:], 1.0)
        nc.gpsimd.iota(self.tile_start_i[:], [[P, self.top * TILES]], base=0, channel_multiplier=0)
        nc.gpsimd.iota(self.tile_i[:], [[1, self.tiles]], base=0, channel_multiplier=0).then_inc(self.made, 1)
        pool.wait_ge(self.made, 1)
        nc.gpsimd.affine_select(out=self.earlier[:], in_=self.earlier[:], compare_op=ALU.is_gt, fill=0.0, base=0,
                                pattern=[[1, P]], channel_multiplier=-1).then_inc(self.made, 1)

    def tensor_steps(self, pe, gate):
        nc = self.nc
        pe.wait_ge(self.made, 2)
        pe.wait_ge(self.chosen_ready, 1)
        for n in range(self.top):
            chosen = gate.chosen[n][:].rearrange("p t e -> p (t e)")
            nc.tensor.matmul(self.before[:, n, :], self.earlier[:], chosen, start=True, stop=True)
            last = nc.tensor.matmul(self.number[:, n, :], self.c.ones[:P, :P], chosen, start=True, stop=True)
        last.then_inc(self.counted, 1)

    def vector_steps(self, dve, gate):
        nc, chain, top = self.nc, self.chain, self.top

        def then(instruction):
            chain.tick(instruction)
            chain.wait(dve)

        nc.vector.engine_nop().then_inc(self.chosen_ready, 1)
        dve.wait_ge(self.made, 2)
        nc.vector.tensor_copy(self.tile[:], self.tile_i[:])
        then(nc.vector.tensor_copy(self.tile_start[:], self.tile_start_i[:]))
        dve.wait_ge(self.counted, 1)
        now, new = self.counts
        then(nc.vector.tensor_copy(now[:].rearrange("p (n t) e -> p n (t e)", n=top), self.number[:]))
        step = 1
        while step < top * TILES:
            nc.vector.tensor_copy(new[:, 0:step, :], now[:, 0:step, :])
            then(nc.vector.tensor_tensor(new[:, step:, :], now[:, step:, :], now[:, :top * TILES - step, :], ALU.add))
            now, new, step = new, now, 2 * step
        then(nc.vector.tensor_copy(self.size[:], now[:, top * TILES - 1, :]))
        then(nc.vector.tensor_tensor(self.full[:], self.size[:].unsqueeze(2).broadcast_to([P, EXPERTS, top * TILES]),
                                     self.tile_start[:].unsqueeze(1).broadcast_to([P, EXPERTS, top * TILES]), ALU.is_gt))
        a, b = self.first
        then(nc.vector.tensor_reduce(self.size[:], self.full[:], AX.X, ALU.add))
        then(nc.vector.tensor_copy(a[:], self.size[:]))
        step = 1
        while step < EXPERTS:
            nc.vector.tensor_copy(b[:, 0:step], a[:, 0:step])
            then(nc.vector.tensor_tensor(b[:, step:], a[:, step:], a[:, :EXPERTS - step], ALU.add))
            a, b, step = b, a, 2 * step
        then(nc.vector.tensor_tensor(b[:], a[:], self.size[:], ALU.subtract))
        then(nc.vector.tensor_tensor(self.own[:], self.tile[:].unsqueeze(2).broadcast_to([1, self.tiles, EXPERTS - 1]),
                                     b[0:1, 1:].unsqueeze(1).broadcast_to([1, self.tiles, EXPERTS - 1]), ALU.is_ge))
        then(nc.vector.tensor_reduce(self.owner_f[:], self.own[:], AX.X, ALU.add))
        nc.vector.tensor_copy(self.owner[:], self.owner_f[:])
        for n in range(top):
            mine = slice(n * TILES, (n + 1) * TILES)
            then(nc.vector.tensor_tensor(self.place[:], now[:, mine, :], self.number[:, n, :].rearrange("p (t e) -> p t e", e=EXPERTS),
                                         ALU.subtract))
            then(nc.vector.tensor_tensor(self.place[:], self.place[:], self.before[:, n, :].rearrange("p (t e) -> p t e", e=EXPERTS),
                                         ALU.add))
            then(nc.vector.scalar_tensor_tensor(self.place[:], b[:].unsqueeze(1).broadcast_to([P, TILES, EXPERTS]), float(P),
                                                self.place[:], ALU.mult, ALU.add))
            then(nc.vector.tensor_tensor(self.place[:], self.place[:], gate.chosen[n][:], ALU.mult))
            then(nc.vector.tensor_reduce(self.slot_f[:], self.place[:], AX.X, ALU.add))
            then(nc.vector.tensor_copy(self.slot[n][:], self.slot_f[:]))
        nc.vector.engine_nop().then_inc(self.ready, 1)


def mixture(p, c, A, x, xn, xn_T):
    nc = p.nc
    with ExitStack() as scope:
        sb = lambda name, shape, dtype=F32: p.sb("mx_" + name, shape, dtype, scope)
        router = sb("router", [128, KB, EXPERTS])
        share = sb("share", [P, TILES, EXPERTS])
        share_T = sb("share_T", [EXPERTS, NODES])
        b1 = sb("b1", [128, EXPERTS * KB])
        b2 = sb("b2", [EXPERTS, DIM])
        w1 = sb("w1", [128, 2, KB, DIM])
        w2 = sb("w2", [128, 2, KB, DIM])
        hidden = sb("hidden", [128, 2, KB, CHUNK])
        logits = p.ps("mx_logits", [P, TILES, EXPERTS], scope=scope)
        turned = p.ps("mx_turned", [EXPERTS, 512], scope=scope)
        up = p.ps("mx_up", [128, 2, 512], scope=scope)
        down = p.ps("mx_down", [P, 4, 512], scope=scope)
        loaded, logits_ready, gated = p.sem("mx_loaded"), p.sem("mx_logits_ready"), p.sem("mx_gated")
        turn_ready, turn_copied = p.sem("mx_turn_ready"), p.sem("mx_turn_copied")
        w_loaded = [p.sem(f"mx_w_loaded{u}") for u in range(2)]
        up_ready, hidden_ready, down_ready, added = (p.sem("mx_up_ready"), p.sem("mx_hidden_ready"),
                                                     p.sem("mx_down_ready"), p.sem("mx_added"))
        based = p.sem("mx_based")
        gate = Gate(p, scope, "mg", 2)
        by_block = lambda a: a.rearrange("(k p) n -> p k n", p=128)
        with nc.Block() as block:
            @block.sync
            def _(sp):
                sp.dma_start(router[:], by_block(A["router_T"])).then_inc(loaded, 16)
                sp.dma_start(b1[:], A["ffn0_b1_T"]).then_inc(loaded, 16)
                sp.dma_start(b2[:], A["ffn0_b2"]).then_inc(loaded, 16)
                for e in range(EXPERTS):
                    if e >= 2:
                        sp.wait_ge(down_ready, (e - 1) * TILES)
                    sp.dma_start(w1[:, e % 2, :, :], by_block(A["ffn0_w1"][e])).then_inc(w_loaded[e % 2], 16)
                    sp.dma_start(w2[:, e % 2, :, :], by_block(A["ffn0_w2"][e])).then_inc(w_loaded[e % 2], 16)
                sp.wait_ge(loaded, 48)

            @block.gpsimd
            def _(pool):
                gate.pool_steps(pool)
                with pool.Fori(0, TILES) as t:
                    nc.gpsimd.tensor_tensor(row(x, t), row(x, t), xn[:, bass.ds(t, 1), 0:DIM].rearrange("p a d -> p (a d)"),
                                            ALU.add).then_inc(based, 1)

            @block.tensor
            def _(pe):
                pe.wait_ge(loaded, 48)
                for t in range(TILES):
                    for k in range(KB):
                        last = nc.tensor.matmul(logits[:, t, :], xn_T[:, k, t * P:(t + 1) * P], router[:, k, :],
                                                start=(k == 0), stop=(k == KB - 1))
                    last.then_inc(logits_ready, 1)

                def raise_up(e, q):
                    n = e * CHUNKS + q
                    pe.wait_ge(w_loaded[e % 2], 32 * (e // 2 + 1))
                    for m in range(KB):
                        i = n * KB + m
                        if i >= 2:
                            pe.wait_ge(hidden_ready, i - 1)
                        for k in range(KB):
                            last = nc.tensor.matmul(up[:, m, 0:CHUNK], w1[:, e % 2, k, m * 128:(m + 1) * 128],
                                                    xn_T[:, k, q * CHUNK:(q + 1) * CHUNK], start=(k == 0),
                                                    stop=(k == KB - 1))
                        last.then_inc(up_ready, 1)

                def bring_down(e, q):
                    n = e * CHUNKS + q
                    pe.wait_ge(hidden_ready, (n + 1) * KB)
                    for j in range(4):
                        i = n * 4 + j
                        if i >= 4:
                            pe.wait_ge(added, i - 3)
                        for k in range(KB):
                            last = nc.tensor.matmul(down[:, i % 4, 0:DIM], hidden[:, n % 2, k, j * P:(j + 1) * P],
                                                    w2[:, e % 2, k, :], start=(k == 0), stop=(k == KB - 1))
                        last.then_inc(down_ready, 1)

                steps = [(e, q) for e in range(EXPERTS) for q in range(CHUNKS)]
                raise_up(*steps[0])
                for n, step in enumerate(steps):
                    if n + 1 < len(steps):
                        raise_up(*steps[n + 1])
                    bring_down(*step)
                pe.wait_ge(gated, 1)
                for q in range(CHUNKS):
                    if q >= 1:
                        pe.wait_ge(turn_copied, q)
                    for j in range(4):
                        last = nc.tensor.transpose(turned[:, j * P:(j + 1) * P], share[:, q * 4 + j, :], c.ident[:P, :P])
                    last.then_inc(turn_ready, 1)
                for t in range(TILES):
                    i = len(steps) * 4 + t
                    pe.wait_ge(turn_copied, t // 4 + 1)
                    pe.wait_ge(added, i - 3)
                    nc.tensor.matmul(down[:, i % 4, 0:DIM], share_T[:, t * P:(t + 1) * P], b2[:], start=True,
                                     stop=True).then_inc(down_ready, 1)

            @block.scalar
            def _(act):
                gate.scalar_steps(act)
                act.wait_ge(loaded, 48)
                for e in range(EXPERTS):
                    for q in range(CHUNKS):
                        n = e * CHUNKS + q
                        if n >= 2:
                            act.wait_ge(down_ready, (n - 1) * 4)
                        for m in range(KB):
                            act.wait_ge(up_ready, n * KB + m + 1)
                            nc.scalar.activation(hidden[:, n % 2, m, :], up[:, m, 0:CHUNK], ACT.Gelu,
                                                 bias=b1[:, e * KB + m:e * KB + m + 1]).then_inc(hidden_ready, 1)
                for q in range(CHUNKS):
                    act.wait_ge(turn_ready, q + 1)
                    nc.scalar.activation(share_T[:, q * CHUNK:(q + 1) * CHUNK], turned[:, 0:CHUNK],
                                         ACT.Copy).then_inc(turn_copied, 1)

            @block.vector
            def _(dve):
                gate.vector_steps(dve, logits[:], logits_ready, TILES)
                chain = gate.chain
                chain.tick(nc.vector.tensor_tensor(gate.total[:], gate.best[0][:], gate.best[1][:], ALU.add))
                chain.wait(dve)
                chain.tick(nc.vector.tensor_scalar(gate.total[:], gate.total[:], 1e-12, None, ALU.max))
                chain.wait(dve)
                chain.tick(nc.vector.reciprocal(gate.total[:], gate.total[:]))
                chain.wait(dve)
                for n in range(2):
                    chain.tick(nc.vector.tensor_tensor(gate.best[n][:], gate.best[n][:], gate.total[:], ALU.mult))
                    chain.wait(dve)
                    chain.tick(nc.vector.tensor_tensor(gate.chosen[n][:], gate.chosen[n][:],
                                                       gate.best[n][:].unsqueeze(2).broadcast_to([P, TILES, EXPERTS]), ALU.mult))
                    chain.wait(dve)
                nc.vector.tensor_tensor(share[:], gate.chosen[0][:], gate.chosen[1][:], ALU.add).then_inc(gated, 1)
                dve.wait_ge(gated, 1)
                dve.wait_ge(based, TILES)
                with dve.Fori(0, EXPERTS) as e:
                    for t in range(TILES):
                        dve.wait_ge(down_ready, e * TILES + t + 1)
                        nc.vector.scalar_tensor_tensor(x[:, t, :], down[:, t % 4, 0:DIM], share[:, t, bass.ds(e, 1)],
                                                       x[:, t, :], ALU.mult, ALU.add).then_inc(added, 1)
                with dve.Fori(0, TILES) as t:
                    dve.wait_ge(down_ready, t + EXPERTS * TILES + 1)
                    nc.vector.tensor_tensor(row(x, t), down[:, bass.ds(t % 4, 1), 0:DIM].rearrange("p a d -> p (a d)"),
                                            row(x, t), ALU.add).then_inc(added, 1)


def to_nodes_first(p, c, A, xn_T, weight, bias, table):
    nc = p.nc
    with ExitStack() as scope:
        w = p.sb("nf_w", [128, KB, DIM], scope=scope)
        b = p.sb("nf_b", [P, DIM], scope=scope)
        rows = p.sb("nf_rows", [P, TILES, DIM], scope=scope)
        projected = p.ps("nf_projected", [P, 4, 512], scope=scope)
        loaded, ready, kept, stored = p.sem("nf_loaded"), p.sem("nf_ready"), p.sem("nf_kept"), p.sem("nf_stored")
        with nc.Block() as block:
            @block.sync
            def _(sp):
                sp.dma_start(w[:], weight.rearrange("(k p) n -> p k n", p=128)).then_inc(loaded, 16)
                sp.dma_start(b[:], bias.partition_broadcast(P)).then_inc(loaded, 16)
                sp.wait_ge(kept, TILES)
                sp.dma_start(table.rearrange("(t p) d -> p t d", p=P), rows[:]).then_inc(stored, 16)
                sp.wait_ge(stored, 16)

            @block.tensor
            def _(pe):
                pe.wait_ge(loaded, 32)
                for t in range(TILES):
                    if t >= 4:
                        pe.wait_ge(kept, t - 3)
                    for k in range(KB):
                        last = nc.tensor.matmul(projected[:, t % 4, 0:DIM], xn_T[:, k, t * P:(t + 1) * P], w[:, k, :],
                                                start=(k == 0), stop=(k == KB - 1))
                    last.then_inc(ready, 1)

            @block.vector
            def _(dve):
                dve.wait_ge(loaded, 32)
                with dve.Fori(0, TILES) as t:
                    dve.wait_ge(ready, t + 1)
                    nc.vector.tensor_tensor(row(rows, t), projected[:, bass.ds(t % 4, 1), 0:DIM].rearrange("p a d -> p (a d)"),
                                            b[:], ALU.add).then_inc(kept, 1)


def edge_messages(p, c, ranges, SUB, A, src, dst, table, hidden_sum):
    nc = p.nc
    BLOCKS = EDGE_TILES // SUB
    with ExitStack() as scope:
        sb = lambda name, shape, dtype=F32: p.sb("em_" + name, shape, dtype, scope)
        w1 = sb("w1", [128, KB, DIM])
        attr = [sb(f"attr{s}", [128, KB, P]) for s in range(SUB)]
        which = [sb(f"which{s}", [P, 1], I32) for s in range(SUB)]
        gathered = [sb(f"gathered{s}", [P, DIM]) for s in range(SUB)]
        pre = sb("pre", [P, SUB, DIM])
        hidden = sb("hidden", [P, SUB, DIM])
        hot = sb("hot", [P, SUB, P])
        dst_f = sb("dst_f", [P, EDGE_TILES])
        projected = p.ps("em_projected", [P, SUB, 512], scope=scope)
        total = p.ps("em_total", [P, 512], scope=scope)
        w_loaded, dst_ready = p.sem("em_w_loaded"), p.sem("em_dst_ready")
        attr_loaded = [p.sem(f"em_attr_loaded{s}") for s in range(SUB)]
        copied = [p.sem(f"em_copied{s}") for s in range(SUB)]
        got = [p.sem(f"em_got{s}") for s in range(SUB)]
        projected_ready = [p.sem(f"em_projected_ready{s}") for s in range(SUB)]
        pre_ready = [p.sem(f"em_pre_ready{s}") for s in range(SUB)]
        hidden_ready = [p.sem(f"em_hidden_ready{s}") for s in range(SUB)]
        hot_ready = [p.sem(f"em_hot_ready{s}") for s in range(SUB)]
        summed = [p.sem(f"em_summed{s}") for s in range(SUB)]
        kept, passed = p.sem("em_kept"), p.sem("em_passed")
        edge_tile = lambda lo, i, s: (lo + i).with_bounds(min_val=0, max_val=BLOCKS - 1) * SUB + s
        with nc.Block() as block:
            @block.sync
            def _(sp):
                sp.dma_start(w1[:], A["gnn1_W1"].rearrange("(k p) n -> p k n", p=128)).then_inc(w_loaded, 16)
                for s in range(SUB):
                    sp.sem_inc(projected_ready[s], 1)
                with sp.Fori(0, TILES) as t:
                    lo, n, before = load_range(sp, ranges, t, SUB)
                    with sp.Fori(0, n) as i:
                        for s in range(SUB):
                            sp.wait_ge(projected_ready[s], before + i + 1)
                            sp.dma_start(attr[s][:], A["edge_attr_T"][bass.ds(edge_tile(lo, i, s), 1)]
                                         .rearrange("a p k e -> p (a k) e")).then_inc(attr_loaded[s], 16)

            @block.gpsimd
            def _(pool):
                for s in range(SUB):
                    pool.sem_inc(pre_ready[s], 1)
                with pool.Fori(0, TILES) as t:
                    lo, n, before = load_range(pool, ranges, t, SUB)
                    with pool.Fori(0, n) as i:
                        for s in range(SUB):
                            pool.wait_ge(pre_ready[s], before + i + 1)
                            nc.gpsimd.tensor_copy(which[s][:], src[:, bass.ds(edge_tile(lo, i, s), 1)]).then_inc(copied[s], 1)
                            pool.wait_ge(copied[s], before + i + 1)
                            pool.sem_inc(passed, 1)
                            nc.gpsimd.indirect_dma_start(
                                out=gathered[s][:], out_offset=None, in_=table,
                                in_offset=bass.IndirectOffsetOnAxis(ap=which[s][:].bitcast(mybir.dt.uint32), axis=0)).then_inc(got[s], 16)

            @block.tensor
            def _(pe):
                def project(before, i, s):
                    pe.wait_ge(attr_loaded[s], (before + i + 1) * 16)
                    pe.wait_ge(pre_ready[s], before + i + 1)
                    for k in range(KB):
                        last = nc.tensor.matmul(projected[:, s, 0:DIM], attr[s][:, k, :], w1[:, k, :],
                                                start=(k == 0), stop=(k == KB - 1))
                    last.then_inc(projected_ready[s], 1)

                def add_up(before, i, s):
                    pe.wait_ge(hidden_ready[s], before + i + 1)
                    pe.wait_ge(hot_ready[s], before + i + 1)
                    nc.tensor.matmul(total[:, 0:DIM], hot[:, s, :], hidden[:, s, :], start=False, stop=True,
                                     skip_group_check=True).then_inc(summed[s], 1)

                pe.wait_ge(w_loaded, 16)
                for s in range(SUB):
                    pe.sem_inc(summed[s], 1)
                with pe.Fori(0, TILES) as t:
                    lo, n, before = load_range(pe, ranges, t, SUB)
                    pe.wait_ge(kept, t + 1)
                    nc.tensor.matmul(total[:, 0:2], c.zero[:], c.zero[:, 0:2], start=True, stop=False, skip_group_check=True)
                    with pe.Fori(0, n) as i:
                        project(before, i, 0)
                        for s in range(SUB):
                            if s + 1 < SUB:
                                project(before, i, s + 1)
                            if s >= 1:
                                add_up(before, i, s - 1)
                        add_up(before, i, SUB - 1)

            @block.vector
            def _(dve):
                nc.vector.tensor_copy(dst_f[:], dst[:]).then_inc(dst_ready, 1)
                dve.wait_ge(dst_ready, 1)
                dve.sem_inc(kept, 1)
                with dve.Fori(0, TILES) as t:
                    lo, n, before = load_range(dve, ranges, t, SUB)
                    with dve.Fori(0, n) as i:
                        for s in range(SUB):
                            dve.wait_ge(summed[s], before + i + 1)
                            nc.vector.tensor_scalar(hot[:, s, :], c.iota_node_i[:, bass.ds(t * P, P)],
                                                    dst_f[:, bass.ds(edge_tile(lo, i, s), 1)], None,
                                                    ALU.is_equal).then_inc(hot_ready[s], 1)
                        for s in range(SUB):
                            dve.wait_ge(projected_ready[s], before + i + 2)
                            dve.wait_ge(got[s], (before + i + 1) * 16)
                            nc.vector.tensor_tensor(pre[:, s, :], projected[:, s, 0:DIM], gathered[s][:],
                                                    ALU.add).then_inc(pre_ready[s], 1)
                    dve.wait_ge(summed[SUB - 1], before + n + 1)
                    nc.vector.tensor_copy(row(hidden_sum, t), total[:, 0:DIM]).then_inc(kept, 1)

            @block.scalar
            def _(act):
                with act.Fori(0, TILES) as t:
                    lo, n, before = load_range(act, ranges, t, SUB)
                    with act.Fori(0, n) as i:
                        for s in range(SUB):
                            act.wait_ge(pre_ready[s], before + i + 2)
                            nc.scalar.activation(hidden[:, s, :], pre[:, s, :], ACT.Relu).then_inc(hidden_ready[s], 1)


def softmax_attention(p, c, A, x, xn, xn_T, hidden_sum, in_degree):
    nc = p.nc
    with ExitStack() as scope:
        sb = lambda name, shape, dtype=F32: p.sb("at_" + name, shape, dtype, scope)
        w = sb("w", [128, KB, 3 * DIM])
        w_out = sb("w_out", [128, KB, DIM])
        w2 = sb("w2", [128, KB, DIM])
        b2, gamma = sb("b2", [P, DIM]), sb("gamma", [P, DIM])
        q, k, v = (sb(n, [P, TILES, DIM]) for n in "qkv")
        q_T = sb("q_T", [128, KB, NODES])
        peak = sb("peak", [P, DIM])
        peak_col = sb("peak_col", [128, KB])
        q_peak, q_sum = sb("q_peak", [P, HEADS1]), sb("q_sum", [P, HEADS1])
        heads_vk = sb("heads_vk", [128, KB, 128])
        k_share = sb("k_share", [128, KB])
        kv_wo = sb("kv_wo", [128, KB, DIM])
        sum_T = sb("sum_T", [128, 2, KB * P])
        stats = sb("stats", [P, TILES * 6])
        mean, var, std, half = (sb(n, [P, TILES]) for n in ("mean", "var", "std", "half"))
        out = k
        loaded = p.sem("at_loaded")
        chain = Chain(p.sem("at_chain"))
        sem = lambda n: p.sem("at_" + n)
        by_head = lambda a: a.rearrange("p (h d) -> p h d", d=HEAD1)
        spread = lambda a: a[:].unsqueeze(2).broadcast_to([P, HEADS1, HEAD1])
        LOADS = 5

        with ExitStack() as first:
            q_bank = p.ps("at_q_bank", [P, 2, 512], scope=first)
            kv_bank = p.ps("at_kv_bank", [P, 2, 512], scope=first)
            turned = p.ps("at_turned", [128, 2, 512], scope=first)
            peaks = p.ps("at_peaks", [128, KB, 512], scope=first)
            qkkv_ready, kv_read = sem("qkkv_ready"), sem("kv_read")
            q_less, q_exped, q_added, q_inverted, q_ready = sem("q_less"), sem("q_exped"), sem("q_added"), sem("q_inverted"), sem("q_ready")
            q_peaked, turn_ready, turn_copied, peaked = sem("q_peaked"), sem("turn_ready"), sem("turn_copied"), sem("peaked")
            passed, peak_turned, peak_found, peak_spread, k_less = sem("passed"), sem("peak_turned"), sem("peak_found"), sem("peak_spread"), sem("k_less")
            with nc.Block() as block:
                @block.sync
                def _(sp):
                    by_block = lambda a: a.rearrange("(k p) n -> p k n", p=128)
                    sp.dma_start(w[:], by_block(A["Wqkv"])).then_inc(loaded, 16)
                    sp.dma_start(w_out[:], by_block(A["Wout"])).then_inc(loaded, 16)
                    sp.dma_start(w2[:], by_block(A["gnn1_W2"])).then_inc(loaded, 16)
                    sp.dma_start(b2[:], A["gnn1_b2"].partition_broadcast(P)).then_inc(loaded, 16)
                    sp.dma_start(gamma[:], A["mix1_gamma"].partition_broadcast(P)).then_inc(loaded, 16)
                    sp.wait_ge(loaded, LOADS * 16)

                @block.tensor
                def _(pe):
                    def turn(t):
                        pe.wait_ge(q_ready, t + 1)
                        if t >= 2:
                            pe.wait_ge(turn_copied, t - 1)
                        for b in range(KB):
                            last = nc.tensor.transpose(turned[:, t % 2, b * P:(b + 1) * P], q[:, t, b * 128:(b + 1) * 128],
                                                       c.ident[:P, :P])
                        last.then_inc(turn_ready, 1)

                    pe.wait_ge(loaded, LOADS * 16)
                    for t in range(TILES):
                        if t >= 2:
                            pe.wait_ge(q_less, t - 1)
                            pe.wait_ge(kv_read, 2 * (t - 1))
                        for b in range(KB):
                            nc.tensor.matmul(q_bank[:, t % 2, 0:DIM], xn_T[:, b, t * P:(t + 1) * P], w[:, b, 0:DIM],
                                             start=(b == 0), stop=(b == KB - 1))
                        for b in range(KB):
                            last = nc.tensor.matmul(kv_bank[:, t % 2, :], xn_T[:, b, t * P:(t + 1) * P], w[:, b, DIM:],
                                                    start=(b == 0), stop=(b == KB - 1))
                        last.then_inc(qkkv_ready, 1)
                    for t in range(TILES):
                        turn(t)
                    pe.wait_ge(peaked, TILES + 1)
                    for b in range(KB):
                        last = nc.tensor.transpose(peaks[:, b, 0:P], peak[:, b * 128:(b + 1) * 128], c.ident[:P, :P])
                    last.then_inc(peak_turned, 1)
                    pe.wait_ge(peak_found, 1)
                    for b in range(KB):
                        last = nc.tensor.matmul(peaks[:P, b, 128:256], peak_col[:, b:b + 1].broadcast_to([128, P]), c.ident[:],
                                                start=True, stop=True)
                    last.then_inc(peak_spread, 1)

                @block.scalar
                def _(act):
                    with act.Fori(0, TILES) as t:
                        act.wait_ge(qkkv_ready, t + 1)
                        nc.scalar.activation(row(k, t), kv_bank[:, bass.ds(t % 2, 1), 0:DIM].rearrange("p a d -> p (a d)"),
                                             ACT.Copy).then_inc(kv_read, 1)
                        nc.scalar.activation(row(v, t), kv_bank[:, bass.ds(t % 2, 1), DIM:].rearrange("p a d -> p (a d)"),
                                             ACT.Copy).then_inc(kv_read, 1)
                        act.wait_ge(q_less, t + 1)
                        nc.scalar.activation(row(q, t), row(q, t), ACT.Exp).then_inc(q_exped, 1)
                    with act.Fori(0, TILES) as t:
                        act.wait_ge(turn_ready, t + 1)
                        nc.scalar.activation(q_T[:, :, bass.ds(t * P, P)],
                                             turned[:, bass.ds(t % 2, 1), 0:KB * P].rearrange("p a (k n) -> p (a k) n", k=KB),
                                             ACT.Copy).then_inc(turn_copied, 1)

                @block.vector
                def _(dve):
                    nc.vector.memset(peak[:], -3.0e38).then_inc(peaked, 1)
                    with dve.Fori(0, TILES) as t:
                        dve.wait_ge(qkkv_ready, t + 1)
                        heads = by_head(q_bank[:, bass.ds(t % 2, 1), 0:DIM].rearrange("p a d -> p (a d)"))
                        nc.vector.tensor_reduce(q_peak[:], heads, AX.X, ALU.max).then_inc(q_peaked, 1)
                        dve.wait_ge(q_peaked, t + 1)
                        nc.vector.tensor_tensor(by_head(row(q, t)), heads, spread(q_peak), ALU.subtract).then_inc(q_less, 1)
                        dve.wait_ge(peaked, t + 1)
                        dve.wait_ge(kv_read, t * 2 + 1)
                        nc.vector.tensor_tensor(peak[:], row(k, t), peak[:], ALU.max).then_inc(peaked, 1)
                        dve.wait_ge(q_exped, t + 1)
                        dve.sem_inc(passed, 1)
                        nc.vector.tensor_reduce(q_sum[:], by_head(row(q, t)), AX.X, ALU.add).then_inc(q_added, 1)
                        dve.wait_ge(q_added, t + 1)
                        nc.vector.reciprocal(q_sum[:], q_sum[:]).then_inc(q_inverted, 1)
                        dve.wait_ge(q_inverted, t + 1)
                        nc.vector.tensor_tensor(by_head(row(q, t)), by_head(row(q, t)), spread(q_sum), ALU.mult).then_inc(q_ready, 1)
                    dve.wait_ge(peak_turned, 1)
                    nc.vector.tensor_reduce(peak_col[:], peaks[:, :, 0:P], AX.X, ALU.max).then_inc(peak_found, 1)
                    dve.wait_ge(peak_spread, 1)
                    chain.tick(nc.vector.tensor_copy(peak[:].rearrange("p (b d) -> p b d", b=KB), peaks[:P, :, 128:256]))
                    chain.wait(dve)
                    dve.wait_ge(kv_read, 2 * TILES)
                    with dve.Fori(0, TILES) as t:
                        nc.vector.tensor_tensor(row(k, t), row(k, t), peak[:], ALU.subtract)

        with ExitStack() as second:
            vk = p.ps("at_vk", [128, KB, 512], scope=second)
            k_sum = p.ps("at_k_sum", [128, KB, 512], scope=second)
            outs = p.ps("at_outs", [P, 2, 512], scope=second)
            turned = p.ps("at_turned2", [128, 2, 512], scope=second)
            zeroed, k_exped, vk_ready, heads_ready = sem("zeroed"), sem("k_exped"), sem("vk_ready"), sem("heads_ready")
            k_inverted, kv_wo_ready, kv_wo_kept = sem("k_inverted"), sem("kv_wo_ready"), sem("kv_wo_kept")
            out_ready, out_kept, measured = sem("out_ready"), sem("out_kept"), sem("measured")
            var_ready, std_ready, normed, based, degreed = sem("var_ready"), sem("std_ready"), sem("normed"), sem("based"), sem("degreed")
            sum_turned, sum_copied, message_ready, added = sem("sum_turned"), sem("sum_copied"), sem("message_ready"), sem("added")
            gained = sem("gained")
            s6 = stats[:].rearrange("p (t k) -> p k t", k=6)
            with nc.Block() as block:
                @block.scalar
                def _(act):
                    with act.Fori(0, TILES) as t:
                        nc.scalar.activation(row(k, t), row(k, t), ACT.Exp).then_inc(k_exped, 1)
                    act.wait_ge(vk_ready, 1)
                    act.wait_ge(zeroed, 1)
                    for b in range(KB):
                        for h in range(128 // HEAD1):
                            d = slice(h * HEAD1, (h + 1) * HEAD1)
                            last = nc.scalar.activation(heads_vk[d, b, d], vk[d, b, d], ACT.Copy)
                    last.then_inc(heads_ready, 1)
                    with act.Fori(0, TILES) as t:
                        act.wait_ge(sum_turned, t + 1)
                        nc.scalar.activation(sum_T[:, bass.ds(t % 2, 1), :].rearrange("p a d -> p (a d)"),
                                             turned[:, bass.ds(t % 2, 1), 0:KB * P].rearrange("p a d -> p (a d)"),
                                             ACT.Copy).then_inc(sum_copied, 1)
                    act.wait_ge(var_ready, 1)
                    nc.scalar.activation(std[:], var[:], ACT.Sqrt).then_inc(std_ready, 1)

                @block.tensor
                def _(pe):
                    for t in range(TILES):
                        pe.wait_ge(k_exped, t + 1)
                        for b in range(KB):
                            f = slice(b * 128, (b + 1) * 128)
                            nc.tensor.matmul(vk[:, b, 0:128], v[:, t, f], k[:, t, f], start=(t == 0), stop=(t == TILES - 1))
                            last = nc.tensor.matmul(k_sum[:, b, 0:1], k[:, t, f], c.ones[:P, 0:1], start=(t == 0),
                                                    stop=(t == TILES - 1))
                    last.then_inc(vk_ready, 1)
                    pe.wait_ge(heads_ready, 1)
                    for b in range(KB):
                        last = nc.tensor.matmul(vk[:, b, 0:DIM], heads_vk[:, b, :],
                                                w_out[:, b, :], start=True, stop=True)
                    last.then_inc(kv_wo_ready, 1)
                    pe.wait_ge(kv_wo_kept, 1)
                    for t in range(TILES):
                        if t >= 2:
                            pe.wait_ge(out_kept, t - 1)
                        for b in range(KB):
                            last = nc.tensor.matmul(outs[:, t % 2, 0:DIM], q_T[:, b, t * P:(t + 1) * P], kv_wo[:, b, :],
                                                    start=(b == 0), stop=(b == KB - 1))
                        last.then_inc(out_ready, 1)

                    def turn(t):
                        if t >= 2:
                            pe.wait_ge(sum_copied, t - 1)
                        for b in range(KB):
                            last = nc.tensor.transpose(turned[:, t % 2, b * P:(b + 1) * P],
                                                       hidden_sum[:, t, b * 128:(b + 1) * 128], c.ident[:P, :P])
                        last.then_inc(sum_turned, 1)

                    pe.wait_ge(out_kept, TILES)
                    turn(0)
                    for t in range(TILES):
                        if t + 1 < TILES:
                            turn(t + 1)
                        pe.wait_ge(sum_copied, t + 1)
                        if t >= 2:
                            pe.wait_ge(added, t - 1)
                        for b in range(KB):
                            last = nc.tensor.matmul(outs[:, t % 2, 0:DIM], sum_T[:, t % 2, b * P:(b + 1) * P], w2[:, b, :],
                                                    start=(b == 0), stop=(b == KB - 1))
                        last.then_inc(message_ready, 1)

                @block.gpsimd
                def _(pool):
                    with pool.Fori(0, TILES) as t:
                        nc.gpsimd.tensor_tensor(row(x, t), row(x, t), xn[:, bass.ds(t, 1), 0:DIM].rearrange("p a d -> p (a d)"),
                                                ALU.add).then_inc(based, 1)
                    for t in range(TILES):
                        pool.wait_ge(normed, t + 1)
                        nc.gpsimd.tensor_tensor(row(out, t), row(out, t), gamma[:], ALU.mult).then_inc(gained, 1)

                @block.vector
                def _(dve):
                    nc.vector.memset(heads_vk[:], 0.0).then_inc(zeroed, 1)
                    dve.wait_ge(based, TILES)
                    with dve.Fori(0, TILES) as t:
                        nc.vector.scalar_tensor_tensor(row(x, t), b2[:], in_degree[:, bass.ds(t, 1)], row(x, t),
                                                       ALU.mult, ALU.add).then_inc(degreed, 1)
                    dve.wait_ge(vk_ready, 1)
                    nc.vector.reciprocal(k_share[:].unsqueeze(2), k_sum[:, :, 0:1]).then_inc(k_inverted, 1)
                    dve.wait_ge(k_inverted, 1)
                    dve.wait_ge(kv_wo_ready, 1)
                    for b in range(KB):
                        last = nc.vector.tensor_scalar(kv_wo[:, b, :], vk[:, b, 0:DIM], k_share[:, b:b + 1], HEAD1 ** -0.5,
                                                       ALU.mult, ALU.mult)
                    last.then_inc(kv_wo_kept, 1)
                    with dve.Fori(0, TILES) as t:
                        dve.wait_ge(out_ready, t + 1)
                        nc.vector.tensor_copy(row(out, t), outs[:, bass.ds(t % 2, 1), 0:DIM].rearrange("p a d -> p (a d)")).then_inc(out_kept, 1)
                        dve.wait_ge(out_kept, t + 1)
                        nc.vector.bn_stats(stats[:, bass.ds(t * 6, 6)], row(out, t)).then_inc(measured, 1)
                    dve.wait_ge(measured, TILES)
                    nc.vector.tensor_tensor(half[:], s6[:, 1, :], s6[:, 4, :], ALU.subtract)
                    nc.vector.tensor_tensor(mean[:], s6[:, 1, :], s6[:, 4, :], ALU.add)
                    chain.tick(nc.vector.tensor_tensor(var[:], s6[:, 2, :], s6[:, 5, :], ALU.add))
                    chain.wait(dve)
                    nc.vector.tensor_scalar(mean[:], mean[:], 0.5, None, ALU.mult)
                    chain.tick(nc.vector.scalar_tensor_tensor(half[:], half[:], 0.25, half[:], ALU.mult, ALU.mult))
                    chain.wait(dve)
                    chain.tick(nc.vector.scalar_tensor_tensor(var[:], var[:], 1.0 / DIM, half[:], ALU.mult, ALU.add))
                    chain.wait(dve)
                    nc.vector.tensor_scalar(var[:], var[:], LN_EPS, None, ALU.add).then_inc(var_ready, 1)
                    dve.wait_ge(degreed, TILES)
                    with dve.Fori(0, TILES) as t:
                        dve.wait_ge(message_ready, t + 1)
                        nc.vector.tensor_tensor(row(x, t), outs[:, bass.ds(t % 2, 1), 0:DIM].rearrange("p a d -> p (a d)"),
                                                row(x, t), ALU.add).then_inc(added, 1)
                    dve.wait_ge(std_ready, 1)
                    inverse_root(dve, nc, chain, std, var, half)
                    with dve.Fori(0, TILES) as t:
                        nc.vector.tensor_scalar(row(out, t), row(out, t), mean[:, bass.ds(t, 1)], std[:, bass.ds(t, 1)],
                                                ALU.subtract, ALU.mult).then_inc(normed, 1)
                    dve.wait_ge(added, TILES)
                    with dve.Fori(0, TILES) as t:
                        dve.wait_ge(gained, t + 1)
                        nc.vector.tensor_tensor(row(x, t), row(out, t), row(x, t), ALU.add)


def layer1(p, c, A, x, xn, xn_T, ranges, SUB, src, dst, in_degree):
    table = p.nc.dram_tensor("edge_table", [NODES, DIM], F32).ap()
    layer_norm(p, c, "ln2", x, xn, xn_T)
    to_nodes_first(p, c, A, xn_T, A["gnn1_W1"], A["gnn1_b1"], table)
    with ExitStack() as scope:
        hidden_sum = p.sb("hidden_sum", [P, TILES, DIM], scope=scope)
        edge_messages(p, c, ranges, SUB, A, src, dst, table, hidden_sum)
        softmax_attention(p, c, A, x, xn, xn_T, hidden_sum, in_degree)


def one_expert(p, c, A, state, xn_T_flat, out):
    nc = p.nc
    HB = HIDDEN // 128
    with ExitStack() as scope:
        sb = lambda name, shape, dtype=F32: p.sb("oe_" + name, shape, dtype, scope)
        gate_bias = sb("bg", [P, EXPERTS])
        gate = Gate(p, scope, "og", 1, gate_bias)
        way = Dispatch(p, c, scope, "od", 1)
        GROUPS = (way.tiles + 3) // 4
        SLOTS = GROUPS * 4 * P
        sorted_rows = nc.dram_tensor("sorted_rows", [SLOTS, ROW], F32).ap()
        w1 = sb("w1", [128, KB, HIDDEN])
        wg = sb("wg", [128, HB, EXPERTS])
        b1 = sb("b1", [128, HB])
        bd = sb("bd", [P, EXPERTS * DIM])
        wd = sb("wd", [128, EXPERTS * HB * DIM])
        hidden = sb("hidden", [128, 2, HB, CHUNK])
        xn_T = xn_T_flat[:].rearrange("p (k n) -> p k n", k=KB)
        RESULTS = 4
        at_T, at_result = 4 * ROW, 4 * ROW + KB * CHUNK
        rows = [sb("rows", [P, 4 * ROW])[:], xn_T_flat[:P, 0:at_T]]
        rows = [r.rearrange("p (j d) -> p j d", d=ROW) for r in rows]
        rows_T = xn_T_flat[:, at_T:at_result].rearrange("p (k n) -> p k n", k=KB)
        result = xn_T_flat[:P, at_result:at_result + RESULTS * DIM].rearrange("p (i d) -> p i d", d=DIM)
        blank = rows[0][:, 0, :]
        number = sb("number", [P, 2, 4], I32)
        node_i, node = sb("node_i", [P, TILES], I32), sb("node", [P, TILES])
        logits = p.ps("oe_logits", [P, TILES, EXPERTS], scope=scope)
        up = p.ps("oe_up", [128, 2, 512], scope=scope)
        down = p.ps("oe_down", [P, 2, 512], scope=scope)
        turned = p.ps("oe_turned", [128, 512], scope=scope)
        sem = lambda n: p.sem("oe_" + n)
        loaded, up_ready, hidden_ready, logits_ready = sem("loaded"), sem("up_ready"), sem("hidden_ready"), sem("logits_ready")
        wd_loaded, blanked, filled, numbered, sent = sem("wd_loaded"), sem("blanked"), sem("filled"), sem("numbered"), sem("sent")
        rows_loaded = [sem(f"rows_loaded{u}") for u in range(2)]
        turn_ready, turn_copied, down_ready, biased, result_ready = (sem("turn_ready"), sem("turn_copied"), sem("down_ready"),
                                                                     sem("biased"), sem("result_ready"))
        number_ready = sem("number_ready")
        written = [sem(f"written{u}") for u in range(RESULTS)]
        by_block = lambda a: a.rearrange("(k p) n -> p k n", p=128)
        LOADS = 5
        with nc.Block() as block:
            @block.sync
            def _(sp):
                sp.dma_start(w1[:], by_block(A["ffn1_W1"])).then_inc(loaded, 16)
                sp.dma_start(wg[:], by_block(A["ffn1_Wg"])).then_inc(loaded, 16)
                sp.dma_start(b1[:], A["ffn1_b1_T"]).then_inc(loaded, 16)
                sp.dma_start(gate_bias[:], A["ffn1_bg"].partition_broadcast(P)).then_inc(loaded, 16)
                sp.dma_start(bd[:], A["ffn1_bd"].rearrange("e n -> (e n)").partition_broadcast(P)).then_inc(loaded, 16)
                sp.wait_ge(blanked, 1)
                for g in range(GROUPS * 4):
                    sp.dma_start(sorted_rows[g * P:(g + 1) * P, :], blank[:]).then_inc(filled, 16)
                for e in range(EXPERTS):
                    sp.dma_start(wd[:, e * HB * DIM:(e + 1) * HB * DIM].rearrange("p (k n) -> p k n", k=HB),
                                 by_block(A["ffn1_Wd"][e])).then_inc(wd_loaded, 16)
                sp.wait_ge(loaded, LOADS * 16)
                sp.wait_ge(sent, TILES * 16)
                for g in range(GROUPS):
                    if g >= 2:
                        sp.wait_ge(result_ready, 4 * (g - 1))
                    sp.dma_start(rows[g % 2][:], sorted_rows[g * 4 * P:(g + 1) * 4 * P, :]
                                 .rearrange("(j p) d -> p j d", p=P)).then_inc(rows_loaded[g % 2], 16)

            @block.gpsimd
            def _(pool):
                gate.pool_steps(pool)
                way.pool_steps(pool)
                nc.gpsimd.iota(node_i[:], [[P, TILES]], base=0, channel_multiplier=1).then_inc(numbered, 1)
                pool.wait_ge(filled, GROUPS * 4 * 16)
                pool.wait_ge(way.ready, 1)
                for t in range(TILES):
                    nc.gpsimd.indirect_dma_start(out=sorted_rows, out_offset=bass.IndirectOffsetOnAxis(
                        ap=way.slot[0][:, t:t + 1].bitcast(mybir.dt.uint32), axis=0), in_=state[:, t, :],
                        in_offset=None).then_inc(sent, 16)
                for i in range(GROUPS * 4):
                    pool.wait_ge(number_ready, i // 4 + 1)
                    pool.wait_ge(result_ready, i + 1)
                    nc.gpsimd.indirect_dma_start(out=out, out_offset=bass.IndirectOffsetOnAxis(
                        ap=number[:, (i // 4) % 2, i % 4:i % 4 + 1].bitcast(mybir.dt.uint32), axis=0), in_=result[:, i % RESULTS, :],
                        in_offset=None, bounds_check=NODES - 1, oob_is_err=False).then_inc(written[i % RESULTS], 16)
                for u in range(RESULTS):
                    pool.wait_ge(written[u], GROUPS * 4 // RESULTS * 16)

            @block.tensor
            def _(pe):
                def raise_up(n, columns):
                    for m in range(HB):
                        i = n * HB + m
                        if i >= 2:
                            pe.wait_ge(hidden_ready, i - 1)
                        for k in range(KB):
                            last = nc.tensor.matmul(up[:, i % 2, 0:CHUNK], w1[:, k, m * 128:(m + 1) * 128], columns[:, k, :],
                                                    start=(k == 0), stop=(k == KB - 1))
                        last.then_inc(up_ready, 1)

                def gate_tiles(q):
                    pe.wait_ge(hidden_ready, (q + 1) * HB)
                    for j in range(4):
                        t = q * 4 + j
                        for m in range(HB):
                            last = nc.tensor.matmul(logits[:, t, :], hidden[:, q % 2, m, j * P:(j + 1) * P], wg[:, m, :],
                                                    start=(m == 0), stop=(m == HB - 1))
                        last.then_inc(logits_ready, 1)

                def turn(g):
                    pe.wait_ge(rows_loaded[g % 2], 16 * (g // 2 + 1))
                    for k in range(KB):
                        if g * KB + k:
                            pe.wait_ge(turn_copied, g * KB + k)
                        for j in range(4):
                            last = nc.tensor.transpose(turned[:, j * P:(j + 1) * P],
                                                       rows[g % 2][:, j, DIM + k * 128:DIM + (k + 1) * 128], c.ident[:P, :P])
                        last.then_inc(turn_ready, 1)

                def bring_down(g):
                    n = CHUNKS + g
                    pe.wait_ge(hidden_ready, (n + 1) * HB)
                    for j in range(4):
                        i = g * 4 + j
                        if i >= 2:
                            pe.wait_ge(biased, i - 1)
                        owner = pe.value_load(way.owner[0:1, min(i, way.tiles - 1):min(i, way.tiles - 1) + 1], min_val=0, max_val=EXPERTS - 1)
                        for m in range(HB):
                            last = nc.tensor.matmul(down[:, i % 2, 0:DIM], hidden[:, n % 2, m, j * P:(j + 1) * P],
                                                    wd[:, bass.ds(owner * (HB * DIM) + m * DIM, DIM)], start=(m == 0),
                                                    stop=(m == HB - 1))
                        last.then_inc(down_ready, 1)

                pe.wait_ge(loaded, LOADS * 16)
                raise_up(0, xn_T[:, :, 0:CHUNK])
                for q in range(CHUNKS):
                    if q + 1 < CHUNKS:
                        raise_up(q + 1, xn_T[:, :, (q + 1) * CHUNK:(q + 2) * CHUNK])
                    gate_tiles(q)
                way.tensor_steps(pe, gate)
                turn(0)
                pe.wait_ge(wd_loaded, EXPERTS * 16)
                pe.wait_ge(way.ready, 1)
                for g in range(GROUPS):
                    pe.wait_ge(turn_copied, (g + 1) * KB)
                    raise_up(CHUNKS + g, rows_T)
                    if g + 1 < GROUPS:
                        turn(g + 1)
                    bring_down(g)

            @block.scalar
            def _(act):
                def activate(n):
                    if n >= CHUNKS + 2:
                        act.wait_ge(down_ready, 4 * (n - CHUNKS - 1))
                    elif n >= 2:
                        act.wait_ge(logits_ready, 4 * min(n - 1, CHUNKS))
                    for m in range(HB):
                        i = n * HB + m
                        act.wait_ge(up_ready, i + 1)
                        nc.scalar.activation(hidden[:, n % 2, m, :], up[:, i % 2, 0:CHUNK], ACT.Gelu,
                                             bias=b1[:, m:m + 1]).then_inc(hidden_ready, 1)

                def keep_turned(g):
                    for k in range(KB):
                        act.wait_ge(turn_ready, g * KB + k + 1)
                        nc.scalar.activation(rows_T[:, k, :], turned[:, 0:CHUNK], ACT.Copy).then_inc(turn_copied, 1)

                act.wait_ge(loaded, LOADS * 16)
                for q in range(CHUNKS):
                    activate(q)
                gate.scalar_steps(act)
                keep_turned(0)
                for g in range(GROUPS):
                    activate(CHUNKS + g)
                    if g + 1 < GROUPS:
                        keep_turned(g + 1)

            @block.vector
            def _(dve):
                chain = Chain(sem("chain"))
                nc.vector.memset(blank[:, 0:NUMBER], 0.0)
                nc.vector.memset(blank[:, NUMBER:ROW], float(2 * NODES)).then_inc(blanked, 1)
                dve.wait_ge(numbered, 1)
                chain.tick(nc.vector.tensor_copy(state[:, :, NUMBER:ROW], node_i[:].unsqueeze(2)))
                dve.wait_ge(loaded, LOADS * 16)
                gate.vector_steps(dve, logits[:], logits_ready, TILES)
                chain.tick(nc.vector.tensor_copy(state[:, :, SHARE:NUMBER], gate.best[0][:].unsqueeze(2)))
                chain.wait(dve)
                way.vector_steps(dve, gate)
                for g in range(GROUPS):
                    dve.wait_ge(rows_loaded[g % 2], 16 * (g // 2 + 1))
                    nc.vector.tensor_copy(number[:, g % 2, :].unsqueeze(2), rows[g % 2][:, :, NUMBER:ROW]).then_inc(number_ready, 1)
                    for j in range(4):
                        i = g * 4 + j
                        owner = dve.value_load(way.owner[0:1, min(i, way.tiles - 1):min(i, way.tiles - 1) + 1], min_val=0, max_val=EXPERTS - 1)
                        dve.wait_ge(down_ready, i + 1)
                        if g >= 1:
                            dve.wait_ge(written[i % RESULTS], 16 * g)
                        nc.vector.tensor_tensor(result[:, i % RESULTS, :], down[:, i % 2, 0:DIM], bd[:, bass.ds(owner * DIM, DIM)],
                                                ALU.add).then_inc(biased, 1)
                        dve.wait_ge(biased, i + 1)
                        nc.vector.scalar_tensor_tensor(result[:, i % RESULTS, :], result[:, i % RESULTS, :], rows[g % 2][:, j, SHARE:NUMBER],
                                                       rows[g % 2][:, j, 0:DIM], ALU.mult, ALU.add).then_inc(result_ready, 1)


class Names:
    pass


def gps_layers(nc, A, out, upto=99):
    with ExitStack() as ctx:
        p, c = Program(nc, ctx), Names()
        state = p.sb("state", [P, TILES, ROW])
        x, xn = state[:, :, 0:DIM], state[:, :, DIM:2 * DIM + 1]
        xn_T = p.sb("xn_T", [128, KB * NODES])
        xn_T_flat, xn_T = xn_T, xn_T[:].rearrange("p (k n) -> p k n", k=KB)
        c.ident = p.sb("ident", [128, 128])
        c.ones = p.sb("ones", [128, 128])
        c.zero = p.sb("zero", [1, P], BF16)
        with ExitStack() as graph:
            graph_layers(p, c, A, x, xn, xn_T, graph, upto)
        if upto >= 4:
            layer_norm(p, c, "ln3", x, xn, xn_T)
            one_expert(p, c, A, state, xn_T_flat, out)
            return
        done = p.sem("done")
        with nc.Block() as block:
            @block.sync
            def _(sp):
                sp.dma_start(out.rearrange("(t p) d -> p t d", p=P), x[:]).then_inc(done, 16)
                sp.wait_ge(done, 16)


def graph_layers(p, c, A, x, xn, xn_T, graph, upto):
    nc = p.nc
    constants(p, c, graph)
    src = p.sb("src_cols", [P, EDGE_TILES], I32, graph)
    dst = p.sb("dst_cols", [P, EDGE_TILES], I32, graph)
    in_degree = p.sb("in_degree", [P, TILES], scope=graph)
    loaded = p.sem("x_loaded")
    with nc.Block() as block:
        @block.vector
        def _(dve):
            nc.vector.memset(c.zero[:], 0.0)
            nc.vector.memset(xn[:, :, DIM:DIM + 1], 1.0)

        @block.sync
        def _(sp):
            sp.dma_start(x[:], A["x"].rearrange("(t p) d -> p t d", p=P)).then_inc(loaded, 16)
            sp.dma_start(src[:], A["src_cols"]).then_inc(loaded, 16)
            sp.dma_start(dst[:], A["dst_cols"]).then_inc(loaded, 16)
            sp.wait_ge(loaded, 48)
    ranges0 = edge_ranges(p, "two", A, 2, graph)
    ranges1 = edge_ranges(p, "four", A, 4, graph)
    with ExitStack() as layer0:
        mean_in = p.sb("mean_in", [P, TILES, DIM + 1], scope=layer0)
        mean_out = p.sb("mean_out", [P, TILES, DIM + 1], scope=layer0)
        mixer = p.sb("mixer", [128, KB, DIM], scope=layer0)
        layer_norm(p, c, "ln0", x, xn, xn_T)
        neighbour_means(p, c, ranges0, 2, xn, src, dst, mean_in, mean_out, in_degree)
        if upto >= 1:
            linear_attention(p, c, A, xn_T, mixer)
            sage_and_mix(p, c, A, x, xn_T, mean_in[:, :, 0:DIM], mean_out, mixer)
    if upto >= 2:
        layer_norm(p, c, "ln1", x, xn, xn_T)
        mixture(p, c, A, x, xn, xn_T)
    if upto >= 3:
        p.clear_semaphores()
        layer1(p, c, A, x, xn, xn_T, ranges1, 4, src, dst, in_degree)


def laid_out(i):
    import numpy as np
    turn = lambda a: np.ascontiguousarray(np.asarray(a).T)
    keep = lambda a: np.ascontiguousarray(np.asarray(a))
    a = {
        "x": keep(i["x"]),
        "src_cols": turn(keep(i["src"]).reshape(EDGE_TILES, P)),
        "dst_cols": turn(keep(i["dst"]).reshape(EDGE_TILES, P)),
        "dst_blocks": keep(i["dst"]).reshape(RANGE_ROWS, -1),
        "edge_attr_T": np.ascontiguousarray(keep(i["edge_attr_256"]).reshape(EDGE_TILES, P, KB, 128).transpose(0, 3, 2, 1)),
        "wk_T": turn(i["L0_mix_wk"]), "wv_T": turn(i["L0_mix_wv"]), "wq": keep(i["L0_mix_wq"]), "wo_T": turn(i["L0_mix_wo"]),
        "ln_k_g": keep(i["L0_mix_ln_k_g"]), "ln_k_b": keep(i["L0_mix_ln_k_b"]),
        "ln_v_g": keep(i["L0_mix_ln_v_g"]), "ln_v_b": keep(i["L0_mix_ln_v_b"]),
        "W_l_f_T": turn(i["L0_gnn_W_l_f"]), "W_r_f_T": turn(i["L0_gnn_W_r_f"]), "b_l_f": keep(i["L0_gnn_b_l_f"]),
        "W_l_b_T": turn(i["L0_gnn_W_l_b"]), "W_r_b_T": turn(i["L0_gnn_W_r_b"]), "b_l_b": keep(i["L0_gnn_b_l_b"]),
        "bn_gamma": keep(i["L0_gnn_gamma"]), "bn_beta": keep(i["L0_gnn_beta"]), "bo": keep(i["L0_mix_bo"]),
        "router_T": turn(i["L0_ffn_router_w"]),
        "ffn0_b1_T": turn(keep(i["L0_ffn_b1"]).reshape(EXPERTS * KB, 128)),
        "ffn0_w1": keep(i["L0_ffn_w1"]), "ffn0_w2": keep(i["L0_ffn_w2"]), "ffn0_b2": keep(i["L0_ffn_b2"]),
        "gnn1_W1": keep(i["L1_gnn_W1"]), "gnn1_b1": keep(i["L1_gnn_b1"]),
        "gnn1_W2": keep(i["L1_gnn_W2"]), "gnn1_b2": keep(i["L1_gnn_b2"]),
        "Wqkv": keep(i["L1_mix_Wqkv"]), "Wout": keep(i["L1_mix_Wout"]), "mix1_gamma": keep(i["L1_mix_gamma"]),
        "ffn1_W1": keep(i["L1_ffn_W1"]), "ffn1_b1_T": turn(keep(i["L1_ffn_b1"]).reshape(HIDDEN // 128, 128)),
        "ffn1_Wg": keep(i["L1_ffn_Wg"]), "ffn1_bg": keep(i["L1_ffn_bg"]),
        "ffn1_Wd": keep(i["L1_ffn_Wd"]), "ffn1_bd": keep(i["L1_ffn_bd"]),
    }
    return a


def kernel(**inputs):
    import concourse.bacc as bacc
    from concourse.bass_utils import run_bass_kernel_spmd

    arrays = laid_out(inputs)
    nc = bacc.Bacc("TRN2", target_bir_lowering=False, num_devices=1)
    A = {n: nc.dram_tensor(f"in_{n}", a.shape, mybir.dt.from_np(a.dtype), kind="ExternalInput").ap()
         for n, a in arrays.items()}
    out = nc.dram_tensor("out", [NODES, DIM], F32, kind="ExternalOutput").ap()
    gps_layers(nc, A, out)
    result = run_bass_kernel_spmd(nc, [{f"in_{n}": a for n, a in arrays.items()}], core_ids=[0])
    return result.results[0]["out"]
```

```python
from contextlib import ExitStack, nullcontext

import concourse.bass as bass
from concourse import mybir

F32 = mybir.dt.float32
F16 = mybir.dt.float16
BF16 = mybir.dt.bfloat16
I32 = mybir.dt.int32
I16 = mybir.dt.int16
ALU = mybir.AluOpType
ACT = mybir.ActivationFunctionType
AX = mybir.AxisListType

NODES, DIM, EDGES = 2500, 256, 40000
P = 125
TILES = NODES // P
KB = DIM // 128
CHUNK = 4 * P
CHUNKS = NODES // CHUNK
EDGE_TILES = EDGES // P
RANGE_ROWS = 80
HEADS0, HEADS1, EXPERTS, HIDDEN = 4, 8, 8, 1024
ROW = 2 * DIM + 3
SHARE, NUMBER = 2 * DIM + 1, 2 * DIM + 2
HEAD0, HEAD1 = DIM // HEADS0, DIM // HEADS1
CROWD = 2048
LN_EPS = 1e-5


class Names:
    pass


def load_rows(engine, out, in_, sem):
    cut = P // 16 * 16
    engine.dma_start(out[:cut], in_[:cut]).then_inc(sem, 16)
    engine.dma_start(out[cut:P], in_[cut:P]).then_inc(sem, 16)


class Chain:

    def __init__(self, sem):
        self.sem, self.n = sem, 0

    def tick(self, instruction):
        self.n += 1
        instruction.then_inc(self.sem, 1)

    def wait(self, engine):
        engine.wait_ge(self.sem, self.n)


class Program:

    def __init__(self, nc, ctx):
        self.nc, self.ctx = nc, ctx
        self.used, self.free = [], []

    def sb(self, name, shape, dtype=F32, scope=None):
        return (scope or self.ctx).enter_context(self.nc.sbuf_tensor(name, shape, dtype))

    def ps(self, name, shape, dtype=F32, scope=None):
        return (scope or self.ctx).enter_context(self.nc.psum_tensor(name, shape, dtype))

    def sem(self, name, recycled=True):
        if not recycled:
            return self.ctx.enter_context(self.nc.semaphore(name))
        sem = self.free.pop() if self.free else self.ctx.enter_context(self.nc.semaphore(name))
        self.used.append(sem)
        return sem

    def clear_semaphores(self):
        done, self.used = self.used, []
        with self.nc.Block() as block:
            for n, engine in enumerate((block.sync, block.gpsimd, block.scalar, block.vector, block.tensor)):
                @engine
                def _(e, share=done[n::5]):
                    for sem in share:
                        e.sem_clear(sem)
        self.free = done + self.free


def sorted_tiles(top):
    return -(-((top * NODES + EXPERTS * (P - 1)) // P) // 4) * 4


def row(x, t):
    return x[:, bass.ds(t, 1), :].rearrange("p a d -> p (a d)")


def inverse_root(dve, nc, chain, root, value, work):
    chain.tick(nc.vector.reciprocal(root[:], root[:]))
    chain.wait(dve)
    chain.tick(nc.vector.tensor_tensor(work[:], root[:], root[:], ALU.mult))
    chain.wait(dve)
    chain.tick(nc.vector.scalar_tensor_tensor(work[:], work[:], -0.5, value[:], ALU.mult, ALU.mult))
    chain.wait(dve)
    chain.tick(nc.vector.scalar_tensor_tensor(root[:], work[:], 1.5, root[:], ALU.add, ALU.mult))
    chain.wait(dve)


def constants(p, c, scope):
    nc = p.nc
    c.iota_node_i = p.sb("iota_node_i", [P, NODES], I16, scope)
    made = p.sem("constants_made")
    with nc.Block() as block:
        @block.gpsimd
        def _(pool):
            nc.gpsimd.memset(c.ident[:], 0.0)
            nc.gpsimd.memset(c.ones[:], 1.0)
            nc.gpsimd.iota(c.iota_node_i[:], [[1, NODES]], base=0, channel_multiplier=0).then_inc(made, 1)
            pool.wait_ge(made, 1)
            nc.gpsimd.affine_select(out=c.ident[:], in_=c.ident[:], compare_op=ALU.not_equal, fill=1.0,
                                    base=0, pattern=[[-1, 128]], channel_multiplier=1).then_inc(made, 1)


class Blanks:

    def __init__(self, p, scope):
        self.nc = p.nc
        self.few, self.many = sorted_tiles(1), sorted_tiles(2)
        self.choice_rows = p.nc.dram_tensor("choice_rows", [self.many * P, ROW - DIM], F32).ap()
        self.best_rows = p.nc.dram_tensor("best_rows", [self.few * P, ROW], F32).ap()
        self.blank = p.sb("blank", [128, ROW], scope=scope)
        self.made, self.filled = p.sem("blank_made"), p.sem("blank_filled")

    def vector_steps(self, dve):
        self.nc.vector.memset(self.blank[:, 0:NUMBER], 0.0)
        self.nc.vector.memset(self.blank[:, NUMBER:ROW], float(4 * NODES)).then_inc(self.made, 1)

    def sync_steps(self, sp):
        sp.wait_ge(self.made, 1)
        for rows, parts, columns in ((self.choice_rows, 120, slice(DIM, ROW)), (self.best_rows, 100, slice(0, ROW))):
            n, width = rows.shape[0] // parts, columns.stop - columns.start
            sp.dma_start(rows.rearrange("(p n) d -> p n d", p=parts),
                         self.blank[:parts, columns].unsqueeze(1).broadcast_to([parts, n, width])).then_inc(self.filled, 16)
        sp.wait_ge(self.filled, 32)


def layer_norm(p, c, name, x, xn, xn_T, measured_before=False, beside=None):
    nc = p.nc
    with ExitStack() as scope:
        mean = p.sb(f"{name}_mean", [P, TILES], scope=scope)
        var = p.sb(f"{name}_var", [P, TILES], scope=scope)
        half = p.sb(f"{name}_half", [P, TILES], scope=scope)
        std = p.sb(f"{name}_std", [P, TILES], scope=scope)
        turned = p.ps(f"{name}_turned", [128, 4, 512], scope=scope)
        chain = Chain(p.sem(f"{name}_chain"))
        var_ready, std_ready = p.sem(f"{name}_var_ready"), p.sem(f"{name}_std_ready")
        normed, transposed, copied = p.sem(f"{name}_normed"), p.sem(f"{name}_transposed"), p.sem(f"{name}_copied")
        measured = p.sem(f"{name}_measured")
        s = c.stats[:].rearrange("p (t k) -> p k t", k=6)
        with nc.Block() as block:
            @block.vector
            def _(dve):
                for t in range(0 if measured_before else TILES):
                    nc.vector.bn_stats(c.stats[:, t * 6:(t + 1) * 6], x[:, t, :]).then_inc(measured, 1)
                if beside is not None:
                    beside.vector_first(dve)
                if not measured_before:
                    dve.wait_ge(measured, TILES)
                nc.vector.tensor_tensor(half[:], s[:, 1, :], s[:, 4, :], ALU.subtract)
                nc.vector.tensor_tensor(mean[:], s[:, 1, :], s[:, 4, :], ALU.add)
                chain.tick(nc.vector.tensor_tensor(var[:], s[:, 2, :], s[:, 5, :], ALU.add))
                chain.wait(dve)
                nc.vector.tensor_scalar(mean[:], mean[:], 0.5, None, ALU.mult)
                chain.tick(nc.vector.scalar_tensor_tensor(half[:], half[:], 0.25, half[:], ALU.mult, ALU.mult))
                chain.wait(dve)
                chain.tick(nc.vector.scalar_tensor_tensor(var[:], var[:], 1.0 / DIM, half[:], ALU.mult, ALU.add))
                chain.wait(dve)
                nc.vector.tensor_scalar(var[:], var[:], LN_EPS, None, ALU.add).then_inc(var_ready, 1)
                if beside is not None:
                    beside.vector_last(dve)
                dve.wait_ge(std_ready, 1)
                inverse_root(dve, nc, chain, std, var, half)
                for t in range(TILES):
                    nc.vector.tensor_scalar(xn[:, t, 0:DIM], x[:, t, :], mean[:, t:t + 1], std[:, t:t + 1],
                                            ALU.subtract, ALU.mult).then_inc(normed, 1)

            @block.tensor
            def _(pe):
                if beside is not None:
                    beside.tensor(pe)
                for t in range(TILES):
                    pe.wait_ge(normed, t + 1)
                    if t >= 4:
                        pe.wait_ge(copied, t - 3)
                    for k in range(KB):
                        last = nc.tensor.transpose(turned[:, t % 4, k * P:(k + 1) * P],
                                                   xn[:, t, k * 128:(k + 1) * 128], c.ident[:P, :P])
                    last.then_inc(transposed, 1)

            @block.scalar
            def _(act):
                act.wait_ge(var_ready, 1)
                nc.scalar.activation(std[:], var[:], ACT.Sqrt).then_inc(std_ready, 1)
                for t in range(TILES):
                    act.wait_ge(transposed, t + 1)
                    nc.scalar.activation(xn_T[:, :, t * P:(t + 1) * P],
                                         turned[:, t % 4, 0:KB * P].rearrange("p (k n) -> p k n", k=KB),
                                         ACT.Copy).then_inc(copied, 1)

            if beside is not None:
                @block.sync
                def _(sp):
                    beside.sync(sp)

                @block.gpsimd
                def _(pool):
                    beside.pool(pool)


def edge_ranges(p, A, SUB, outer, scope):
    nc = p.nc
    BLOCKS = EDGE_TILES // SUB
    ROWS_IN_RANGES, PER_ROW = RANGE_ROWS, BLOCKS // RANGE_ROWS
    ranges = p.sb("er_ranges", [1, 3 * TILES], I32, outer)
    row_ranges = p.sb("er_row_ranges", [1, 3 * RANGE_ROWS], I32, outer)
    low_dram = nc.dram_tensor("er_low_dram", [BLOCKS], F32).ap()
    high_dram = nc.dram_tensor("er_high_dram", [BLOCKS], F32).ap()
    ranges_dram = nc.dram_tensor("er_ranges_dram", [TILES, 3], I32).ap()
    row_ranges_dram = nc.dram_tensor("er_row_ranges_dram", [RANGE_ROWS, 3], I32).ap()
    later_i = p.sb("er_later_i", [RANGE_ROWS, TILES - 1], I32, scope)
    later = p.sb("er_later", [RANGE_ROWS, TILES - 1], F32, scope)
    behind = p.sb("er_behind", [RANGE_ROWS, 2, TILES - 1], F32, scope)
    edge = p.sb("er_edge", [RANGE_ROWS, 2], F32, scope)
    tile_of = p.sb("er_tile_of", [RANGE_ROWS, 2], F32, scope)
    earlier_rows = p.sb("er_earlier_rows", [RANGE_ROWS, RANGE_ROWS], F32, scope)
    further = p.sb("er_further", [RANGE_ROWS, 1], F32, scope)
    row_found = p.sb("er_row_found", [RANGE_ROWS, 3], F32, scope)
    row_found_i = p.sb("er_row_found_i", [RANGE_ROWS, 3], I32, scope)
    row_base = p.ps("er_row_base", [RANGE_ROWS, 1], F32, scope)
    row_counted, row_summed, row_ready = p.sem("er_row_counted"), p.sem("er_row_summed"), p.sem("er_row_ready")
    dst = p.sb("er_dst_by_block", [ROWS_IN_RANGES, PER_ROW, SUB * P], I32, scope)
    low = p.sb("er_block_low", [ROWS_IN_RANGES, PER_ROW], F32, scope)
    high = p.sb("er_block_high", [ROWS_IN_RANGES, PER_ROW], F32, scope)
    lows = p.sb("er_lows", [TILES, BLOCKS], F32, scope)
    highs = p.sb("er_highs", [TILES, BLOCKS], F32, scope)
    up_i = p.sb("er_up_i", [TILES, BLOCKS], I32, scope)
    up = p.sb("er_up", [TILES, BLOCKS], F32, scope)
    down = p.sb("er_down", [TILES, BLOCKS], F32, scope)
    start_i = p.sb("er_tile_start_i", [TILES, 1], I32, scope)
    start = p.sb("er_tile_start", [TILES, 1], F32, scope)
    end = p.sb("er_tile_end", [TILES, 1], F32, scope)
    earlier = p.sb("er_earlier", [TILES, TILES], F32, scope)
    first = p.sb("er_first", [TILES, 1], F32, scope)
    stop = p.sb("er_stop", [TILES, 1], F32, scope)
    found = p.sb("er_found", [TILES, 3], F32, scope)
    found_i = p.sb("er_found_i", [TILES, 3], I32, scope)
    base = p.ps("er_base", [TILES, 1], F32, scope)
    loaded, reduced, stored = p.sem("er_r_loaded"), p.sem("er_r_reduced"), p.sem("er_r_stored")
    made, counted, summed = p.sem("er_r_made"), p.sem("er_r_counted"), p.sem("er_r_summed")
    ready, kept = p.sem("er_r_ready"), p.sem("er_r_kept")
    chain = Chain(p.sem("er_r_chain"))

    def sync_steps(sp):
        sp.dma_start(dst[:], A["dst_blocks"].rearrange("p (b e) -> p b e", b=PER_ROW)).then_inc(loaded, 16)
        sp.wait_ge(reduced, 1)
        sp.dma_start(low_dram.rearrange("(p b) -> p b", b=PER_ROW), low[:]).then_inc(stored, 16)
        sp.dma_start(high_dram.rearrange("(p b) -> p b", b=PER_ROW), high[:]).then_inc(stored, 16)
        sp.wait_ge(stored, 32)
        sp.dma_start(lows[:], low_dram.partition_broadcast(TILES)).then_inc(loaded, 16)
        sp.dma_start(highs[:], high_dram.partition_broadcast(TILES)).then_inc(loaded, 16)
        sp.wait_ge(row_ready, 1)
        sp.dma_start(row_ranges_dram, row_found_i[:]).then_inc(stored, 16)
        sp.wait_ge(ready, 1)
        sp.dma_start(ranges_dram, found_i[:]).then_inc(stored, 16)
        sp.wait_ge(stored, 64)
        sp.dma_start(ranges[:], ranges_dram.rearrange("t k -> (t k)").unsqueeze(0)).then_inc(kept, 16)
        sp.dma_start(row_ranges[:], row_ranges_dram.rearrange("t k -> (t k)").unsqueeze(0)).then_inc(kept, 16)
        sp.wait_ge(kept, 32)

    def pool_steps(pool):
        nc.gpsimd.iota(up_i[:], [[1, BLOCKS]], base=1, channel_multiplier=0)
        nc.gpsimd.iota(start_i[:], [[0, 1]], base=0, channel_multiplier=P)
        nc.gpsimd.iota(later_i[:], [[P, TILES - 1]], base=P, channel_multiplier=0)
        nc.gpsimd.memset(earlier_rows[:], 1.0)
        nc.gpsimd.memset(earlier[:], 1.0).then_inc(made, 1)
        pool.wait_ge(made, 1)
        nc.gpsimd.affine_select(out=earlier_rows[:], in_=earlier_rows[:], compare_op=ALU.is_gt, fill=0.0,
                                base=0, pattern=[[1, RANGE_ROWS]], channel_multiplier=-1)
        nc.gpsimd.affine_select(out=earlier[:], in_=earlier[:], compare_op=ALU.is_gt, fill=0.0,
                                base=0, pattern=[[1, TILES]], channel_multiplier=-1).then_inc(made, 1)

    def first_vector_steps(dve):
        dve.wait_ge(loaded, 16)
        nc.vector.tensor_reduce(low[:], dst[:], AX.X, ALU.min)
        nc.vector.tensor_reduce(high[:], dst[:], AX.X, ALU.max).then_inc(reduced, 1)
        dve.wait_ge(made, 2)
        dve.wait_ge(reduced, 1)
        nc.vector.tensor_copy(later[:], later_i[:])
        nc.vector.tensor_reduce(edge[:, 0:1], low[:], AX.X, ALU.min)
        chain.tick(nc.vector.tensor_reduce(edge[:, 1:2], high[:], AX.X, ALU.max))
        chain.wait(dve)
        chain.tick(nc.vector.tensor_tensor(behind[:], edge[:].unsqueeze(2).broadcast_to([RANGE_ROWS, 2, TILES - 1]),
                                           later[:].unsqueeze(1).broadcast_to([RANGE_ROWS, 2, TILES - 1]), ALU.is_ge))
        chain.wait(dve)
        chain.tick(nc.vector.tensor_reduce(tile_of[:], behind[:], AX.X, ALU.add))
        chain.wait(dve)
        nc.vector.tensor_copy(row_found[:, 0:1], tile_of[:, 0:1])
        nc.vector.tensor_tensor(further[:], tile_of[:, 1:2], tile_of[:, 0:1], ALU.subtract).then_inc(row_counted, 1)
        dve.wait_ge(row_counted, 1)
        nc.vector.tensor_scalar(row_found[:, 1:2], further[:], 1.0, None, ALU.add)
        nc.vector.tensor_copy(up[:], up_i[:])
        chain.tick(nc.vector.tensor_copy(start[:], start_i[:]))
        chain.wait(dve)
        nc.vector.tensor_scalar(down[:], up[:], -1.0, float(BLOCKS + 1), ALU.mult, ALU.add)
        chain.tick(nc.vector.tensor_scalar(end[:], start[:], float(P - 1), None, ALU.add))

    def last_vector_steps(dve):
        dve.wait_ge(row_summed, 1)
        chain.tick(nc.vector.tensor_copy(row_found[:, 2:3], row_base[:]))
        chain.wait(dve)
        nc.vector.tensor_copy(row_found_i[:], row_found[:]).then_inc(row_ready, 1)
        dve.wait_ge(loaded, 48)
        chain.wait(dve)
        nc.vector.scalar_tensor_tensor(highs[:], highs[:], start[:], down[:], ALU.is_ge, ALU.mult)
        chain.tick(nc.vector.scalar_tensor_tensor(lows[:], lows[:], end[:], up[:], ALU.is_le, ALU.mult))
        chain.wait(dve)
        nc.vector.tensor_reduce(first[:], highs[:], AX.X, ALU.max)
        chain.tick(nc.vector.tensor_reduce(stop[:], lows[:], AX.X, ALU.max))
        chain.wait(dve)
        chain.tick(nc.vector.tensor_scalar(first[:], first[:], -1.0, float(BLOCKS), ALU.mult, ALU.add))
        chain.wait(dve)
        chain.tick(nc.vector.tensor_scalar(found[:, 0:1], first[:], float(BLOCKS - 1), None, ALU.min))
        chain.wait(dve)
        chain.tick(nc.vector.tensor_tensor(found[:, 1:2], stop[:], found[:, 0:1], ALU.subtract))
        chain.wait(dve)
        nc.vector.tensor_scalar(found[:, 1:2], found[:, 1:2], 1.0, None, ALU.max).then_inc(counted, 1)
        dve.wait_ge(summed, 1)
        chain.tick(nc.vector.tensor_copy(found[:, 2:3], base[:]))
        chain.wait(dve)
        nc.vector.tensor_copy(found_i[:], found[:]).then_inc(ready, 1)

    def tensor_steps(pe):
        pe.wait_ge(made, 2)
        pe.wait_ge(row_counted, 1)
        nc.tensor.matmul(row_base[:], earlier_rows[:], further[:], start=True, stop=True).then_inc(row_summed, 1)
        pe.wait_ge(counted, 1)
        nc.tensor.matmul(base[:], earlier[:], found[:, 1:2], start=True, stop=True).then_inc(summed, 1)

    steps = Names()
    steps.sync, steps.pool, steps.tensor = sync_steps, pool_steps, tensor_steps
    steps.vector_first, steps.vector_last = first_vector_steps, last_vector_steps
    return ranges, row_ranges, steps


def load_range(engine, ranges, t, SUB):
    BLOCKS = EDGE_TILES // SUB
    return (engine.value_load(ranges[0:1, bass.ds(t * 3, 1)], min_val=0, max_val=BLOCKS - 1),
            engine.value_load(ranges[0:1, bass.ds(t * 3 + 1, 1)], min_val=1, max_val=BLOCKS),
            engine.value_load(ranges[0:1, bass.ds(t * 3 + 2, 1)], min_val=0, max_val=BLOCKS * TILES))


def only_if(engine, flag):
    return nullcontext() if flag is None else engine.If(engine.value_load(flag[0:1, 0:1], min_val=0, max_val=1) == 1)


def neighbour_sums(p, c, name, dtype, GROUP, ranges, SUB, xn, src, dst, sum_in, sum_out, flag=None, beside=None):
    nc = p.nc
    W = DIM + 1
    BLOCKS = EDGE_TILES // SUB
    GROUPS = TILES // GROUP
    BATCH = 5 if dtype is F16 else 4
    BATCHES = TILES // BATCH
    with ExitStack() as scope:
        sb = lambda n, shape, dtype=F32: p.sb(f"{name}_{n}", shape, dtype, scope)
        sem = lambda n: p.sem(f"{name}_{n}")
        hot_src = sb("hot_src", [P, 2 * SUB, NODES], BF16)
        hot_dst = sb("hot_dst", [P, 2 * SUB, P], BF16)
        adj = sb("adj", [P, GROUP, NODES], dtype)
        adj_T = sb("adj_T", [P, TILES, P], dtype)
        dst_f = sb("dst_f", [P, EDGE_TILES])
        src_f = sb("src_f", [P, EDGE_TILES])
        if dtype is F16:
            parts = [sb("high", [P, TILES, W], F16), sb("low", [P, TILES, W], F16)]
            ident = sb("ident", [P, P], F16)
        else:
            parts, ident = [xn], c.ident
        rows = p.ps(f"{name}_rows", [P, CHUNKS, 512], scope=scope)
        turned = p.ps(f"{name}_turned", [P, 2, 1024 if dtype is F16 else 512], dtype, scope)
        bank_in = p.ps(f"{name}_bank_in", [P, 512], scope=scope)
        hot_ready = [sem(f"hot_ready{s}") for s in range(SUB)]
        hot_used = [sem(f"hot_used{s}") for s in range(SUB)]
        rows_copied, turn_ready, turn_copied = sem("rows_copied"), sem("turn_ready"), sem("turn_copied")
        in_ready, in_copied, out_ready, out_added = sem("in_ready"), sem("in_copied"), sem("out_ready"), sem("out_added")
        cleared, high_ready, parts_ready, floats_ready = sem("cleared"), sem("high_ready"), sem("parts_ready"), sem("floats_ready")
        buffer = lambda before, i, s: bass.ds(((before + i) % 2).with_bounds(min_val=0, max_val=1) * SUB + s, 1)
        flat = lambda a: a.rearrange("p a n -> p (a n)")
        with nc.Block() as block:
            if beside is not None:
                @block.sync
                def _(sp):
                    beside.sync_steps(sp)

            @block.gpsimd
            def _(pool):
                with only_if(pool, flag):
                    nc.gpsimd.memset(sum_out[:], 0.0).then_inc(cleared, 1)
                    if dtype is F16:
                        pool.wait_ge(high_ready, 1)
                        nc.gpsimd.tensor_tensor(parts[1][:], xn[:], parts[0][:], ALU.subtract).then_inc(parts_ready, 1)

            @block.vector
            def _(dve):
                def build(t, found):
                    lo, n, before = found
                    with dve.Fori(0, n) as i:
                        for s in range(SUB):
                            col = (lo + i).with_bounds(min_val=0, max_val=BLOCKS - 1) * SUB + s
                            dve.wait_ge(hot_used[s], before + i + 1)
                            nc.vector.tensor_scalar(flat(hot_src[:, buffer(before, i, s), :]), c.iota_node_i[:],
                                                    src_f[:, bass.ds(col, 1)], None, ALU.is_equal)
                            nc.vector.tensor_scalar(flat(hot_dst[:, buffer(before, i, s), :]), c.iota_node_i[:, bass.ds(t * P, P)],
                                                    dst_f[:, bass.ds(col, 1)], None,
                                                    ALU.is_equal).then_inc(hot_ready[s], 1)

                def keep_turned(t):
                    for b in range(BATCHES):
                        dve.wait_ge(turn_ready, t * BATCHES + b + 1)
                        nc.vector.tensor_copy(adj_T[:, b * BATCH:(b + 1) * BATCH, :],
                                              turned[:, b % 2, 0:BATCH * 128].rearrange("p (j n) -> p j n", j=BATCH)[:, :, 0:P]
                                              ).then_inc(turn_copied, 1)

                if beside is not None:
                    beside.vector_steps(dve)
                with only_if(dve, flag):
                    nc.vector.tensor_copy(src_f[:], src[:])
                    nc.vector.tensor_copy(dst_f[:], dst[:]).then_inc(floats_ready, 1)
                    dve.wait_ge(floats_ready, 1)
                    dve.sem_inc(turn_copied, 2)
                    dve.sem_inc(out_added, 1)
                    with dve.Fori(0, GROUPS) as g:
                        build(g * GROUP, load_range(dve, ranges, g * GROUP, SUB))
                        found = load_range(dve, ranges, g * GROUP + 1, SUB)
                        for tt in range(GROUP):
                            t = g * GROUP + tt
                            if tt + 1 < GROUP:
                                build(t + 1, found)
                            if tt + 2 < GROUP:
                                found = load_range(dve, ranges, t + 2, SUB)
                            keep_turned(t)
                        for s in range(TILES):
                            dve.wait_ge(cleared, 1)
                            dve.wait_ge(out_ready, g * TILES + s + 1)
                            nc.vector.tensor_tensor(sum_out[:, s, :], rows[:, s % CHUNKS, 0:W], sum_out[:, s, :],
                                                    ALU.add).then_inc(out_added, 1)

            @block.tensor
            def _(pe):
                def build(t, found):
                    lo, n, before = found
                    pe.wait_ge(rows_copied, t + 1)
                    for q in range(CHUNKS):
                        nc.tensor.matmul(rows[:, q, 0:2], c.zero[:], c.zero[:, 0:2], start=True, stop=False,
                                         skip_group_check=True)
                    with pe.Fori(0, n) as i:
                        for s in range(SUB):
                            pe.wait_ge(hot_ready[s], before + i + 1)
                            for q in range(CHUNKS):
                                last = nc.tensor.matmul(rows[:, q, 0:CHUNK], flat(hot_dst[:, buffer(before, i, s), :]),
                                                        flat(hot_src[:, buffer(before, i, s), q * CHUNK:(q + 1) * CHUNK]),
                                                        start=False, stop=(s == SUB - 1), skip_group_check=True)
                            last.then_inc(hot_used[s], 1)

                def turn(t, tt, b):
                    pe.wait_ge(turn_copied, t * BATCHES + b + 1)
                    for j in range(BATCH):
                        s = b * BATCH + j
                        last = nc.tensor.transpose(turned[:, b % 2, j * 128:j * 128 + P],
                                                   adj[:, tt, s * P:(s + 1) * P], ident[:P, :P])
                    last.then_inc(turn_ready, 1)

                def sum_sources(t, tt):
                    found = None
                    pe.wait_ge(rows_copied, t + 2)
                    turn(t, tt, 0)
                    pe.wait_ge(in_copied, t + 1)
                    for b in range(BATCHES):
                        if b + 1 < BATCHES:
                            turn(t, tt, b + 1)
                        if b == 0 and tt + 2 < GROUP:
                            found = load_range(pe, ranges, t + 2, SUB)
                        pe.wait_ge(turn_copied, t * BATCHES + b + 3)
                        for s in range(b * BATCH, (b + 1) * BATCH):
                            for part in parts:
                                last = nc.tensor.matmul(bank_in[:, 0:W], adj_T[:, s, :], part[:, s, :],
                                                        start=(s == 0 and part is parts[0]),
                                                        stop=(s == TILES - 1 and part is parts[-1]))
                    last.then_inc(in_ready, 1)
                    return found

                with only_if(pe, flag):
                    for s in range(SUB):
                        pe.sem_inc(hot_used[s], 2)
                    with pe.Fori(0, GROUPS) as g:
                        build(g * GROUP, load_range(pe, ranges, g * GROUP, SUB))
                        if dtype is F16:
                            pe.wait_ge(parts_ready, 1)
                        found = load_range(pe, ranges, g * GROUP + 1, SUB)
                        for tt in range(GROUP):
                            if tt + 1 < GROUP:
                                build(g * GROUP + tt + 1, found)
                            found = sum_sources(g * GROUP + tt, tt)
                        pe.wait_ge(rows_copied, g * GROUP + GROUP + 1)
                        for s in range(TILES):
                            if s >= CHUNKS:
                                pe.wait_ge(out_added, g * TILES + s - CHUNKS + 2)
                            for tt in range(GROUP):
                                for part in parts:
                                    last = nc.tensor.matmul(rows[:, s % CHUNKS, 0:W], adj[:, tt, s * P:(s + 1) * P],
                                                            flat(part[:, bass.ds(g * GROUP + tt, 1), :]),
                                                            start=(tt == 0 and part is parts[0]),
                                                            stop=(tt == GROUP - 1 and part is parts[-1]))
                            last.then_inc(out_ready, 1)
                        pe.wait_ge(out_added, g * TILES + TILES + 1)

            @block.scalar
            def _(act):
                def keep_rows(t, tt):
                    lo, n, before = load_range(act, ranges, t, SUB)
                    act.wait_ge(hot_used[SUB - 1], before + n + 2)
                    if tt == 0:
                        act.wait_ge(out_added, (t - tt) * (TILES // GROUP) + 1)
                    nc.scalar.activation(adj[:, tt, :].rearrange("p (q n) -> p q n", q=CHUNKS), rows[:, :, 0:CHUNK],
                                         ACT.Copy).then_inc(rows_copied, 1)

                def keep_sum(t):
                    act.wait_ge(in_ready, t + 1)
                    nc.scalar.activation(row(sum_in, t), bank_in[:, 0:W], ACT.Copy).then_inc(in_copied, 1)

                with only_if(act, flag):
                    if dtype is F16:
                        nc.scalar.activation(ident[:], c.ident[:P, :P], ACT.Copy)
                        nc.scalar.activation(parts[0][:], xn[:], ACT.Copy).then_inc(high_ready, 1)
                    act.sem_inc(rows_copied, 1)
                    act.sem_inc(in_copied, 1)
                    with act.Fori(0, GROUPS) as g:
                        keep_rows(g * GROUP, 0)
                        for tt in range(GROUP):
                            if tt + 1 < GROUP:
                                keep_rows(g * GROUP + tt + 1, tt + 1)
                            keep_sum(g * GROUP + tt)


def all_neighbour_sums(p, c, ranges, SUB, xn, src, dst, sum_in, sum_out, beside):
    nc = p.nc
    neighbour_sums(p, c, "nm", F16, 5, ranges, SUB, xn, src, dst, sum_in, sum_out, beside=beside)
    with ExitStack() as scope:
        most = p.sb("nm_most", [P, 1], scope=scope)
        most_of_all = p.sb("nm_most_of_all", [1, 1], scope=scope)
        crowded = p.sb("nm_crowded", [1, 1], I32, scope)
        chain, most_ready, most_turned = Chain(p.sem("nm_most_chain")), p.sem("nm_most_ready"), p.sem("nm_most_turned")
        with nc.psum_tensor("nm_most_T", [1, P], F32) as most_T, nc.Block() as block:
            @block.vector
            def _(dve):
                nc.vector.tensor_reduce(most[:], sum_in[:, :, DIM], AX.X, ALU.max).then_inc(most_ready, 1)
                dve.wait_ge(most_turned, 1)
                chain.tick(nc.vector.tensor_reduce(most_of_all[:], most_T[:], AX.X, ALU.max))
                chain.wait(dve)
                nc.vector.tensor_scalar(crowded[:], most_of_all[:], float(CROWD), None, ALU.is_ge)

            @block.tensor
            def _(pe):
                pe.wait_ge(most_ready, 1)
                nc.tensor.transpose(most_T[:], most[:], c.ident[:P, :P]).then_inc(most_turned, 1)
        neighbour_sums(p, c, "ns", F32, 2, ranges, SUB, xn, src, dst, sum_in, sum_out, crowded)


def linear_attention(p, c, A, xn_T, mixer, mean_in, mean_out, in_degree):
    nc = p.nc
    HEADS = 2 * HEADS0
    GROUP = 5
    GROUPS = TILES // GROUP
    with ExitStack() as scope:
        sb = lambda name, shape, dtype=F32: p.sb("la_" + name, shape, dtype, scope)
        w_kv = sb("w_kv", [128, KB, 2 * DIM])
        w_q = sb("w_q", [128, KB, DIM])
        w_o = sb("w_o", [128, KB, DIM])
        gain = sb("gain", [P, 2, HEAD0])
        shift = sb("shift", [P, 2, HEAD0])
        kv = sb("kv", [P, TILES, 2 * DIM])
        square = sb("square", [P, 2, 2 * DIM])
        total = sb("total", [P, TILES, HEADS])
        var = sb("var", [P, GROUPS, GROUP * HEADS])
        std = sb("std", [P, GROUPS, GROUP * HEADS])
        work = sb("work", [P, GROUP * HEADS])
        degrees = sb("degrees", [P, 2, TILES, 1])
        heads_vk = sb("heads_vk", [128, KB, 128])
        kv_wo = sb("kv_wo", [128, KB, DIM])
        projected = p.ps("la_projected", [P, 2, 512], scope=scope)
        vk = p.ps("la_vk", [128, KB, 512], scope=scope)
        product = p.ps("la_product", [128, KB, 512], scope=scope)
        w_loaded, loaded, projected_ready, centred = p.sem("la_w_loaded"), p.sem("la_loaded"), p.sem("la_projected_ready"), p.sem("la_centred")
        squared, summed = p.sem("la_squared"), p.sem("la_summed")
        var_ready, std_ready, scaled, shifted = (p.sem("la_var_ready"), p.sem("la_std_ready"), p.sem("la_scaled"),
                                                 p.sem("la_shifted"))
        gained, vk_ready, heads_ready = p.sem("la_gained"), p.sem("la_vk_ready"), p.sem("la_heads_ready")
        kv_wo_ready, kv_wo_kept, mixer_ready = p.sem("la_kv_wo_ready"), p.sem("la_kv_wo_kept"), p.sem("la_mixer_ready")
        zeroed, totalled = p.sem("la_zeroed"), p.sem("la_totalled")
        chain = Chain(p.sem("la_chain"))
        by_head = lambda x: x.rearrange("p (h d) -> p h d", d=HEAD0)
        with nc.Block() as block:
            @block.sync
            def _(sp):
                sp.dma_start(w_kv[:, :, 0:DIM], A["wk_T"].rearrange("(k p) n -> p k n", p=128)).then_inc(w_loaded, 16)
                sp.dma_start(w_kv[:, :, DIM:], A["wv_T"].rearrange("(k p) n -> p k n", p=128)).then_inc(w_loaded, 16)
                sp.dma_start(w_q[:], A["wq"].rearrange("(k p) n -> p k n", p=128)).then_inc(loaded, 16)
                sp.dma_start(w_o[:], A["wo_T"].rearrange("(k p) n -> p k n", p=128)).then_inc(loaded, 16)
                for n, (g, b) in enumerate((("ln_k_g", "ln_k_b"), ("ln_v_g", "ln_v_b"))):
                    sp.dma_start(gain[:, n, :], A[g].partition_broadcast(P)).then_inc(loaded, 16)
                    sp.dma_start(shift[:, n, :], A[b].partition_broadcast(P)).then_inc(loaded, 16)
                sp.wait_ge(loaded, 6 * 16)

            @block.tensor
            def _(pe):
                pe.wait_ge(w_loaded, 32)
                for t in range(TILES):
                    if t >= 2:
                        pe.wait_ge(centred, t - 1)
                    for k in range(KB):
                        last = nc.tensor.matmul(projected[:, t % 2, :], xn_T[:, k, t * P:(t + 1) * P], w_kv[:, k, :],
                                                start=(k == 0), stop=(k == KB - 1))
                    last.then_inc(projected_ready, 1)
                for t in range(TILES):
                    pe.wait_ge(shifted, t + 1)
                    for b in range(KB):
                        last = nc.tensor.matmul(vk[:, b, 0:128], kv[:, t, DIM + b * 128:DIM + (b + 1) * 128],
                                                kv[:, t, b * 128:(b + 1) * 128], start=(t == 0), stop=(t == TILES - 1))
                last.then_inc(vk_ready, 1)
                pe.wait_ge(heads_ready, 1)
                pe.wait_ge(loaded, 6 * 16)
                for b in range(KB):
                    last = nc.tensor.matmul(product[:, b, 0:DIM], heads_vk[:, b, :], w_o[:, b, :], start=True, stop=True)
                last.then_inc(kv_wo_ready, 1)
                pe.wait_ge(kv_wo_kept, 1)
                for m in range(KB):
                    for b in range(KB):
                        last = nc.tensor.matmul(product[:, m, 0:DIM], w_q[:, b, m * 128:(m + 1) * 128], kv_wo[:, b, :],
                                                start=(b == 0), stop=(b == KB - 1))
                last.then_inc(mixer_ready, 1)

            @block.vector
            def _(dve):
                def measure(g):
                    for t in range(g * GROUP, (g + 1) * GROUP):
                        dve.wait_ge(projected_ready, t + 1)
                        nc.vector.tensor_reduce(total[:, t, :], by_head(projected[:, t % 2, :]), AX.X, ALU.add).then_inc(totalled, 1)
                        if t > g * GROUP:
                            sum_squares(t - 1)
                        dve.wait_ge(totalled, t + 1)
                        nc.vector.scalar_tensor_tensor(by_head(kv[:, t, :]), total[:, t, :].unsqueeze(2).broadcast_to([P, HEADS, HEAD0]),
                                                       -1.0 / HEAD0, by_head(projected[:, t % 2, :]), ALU.mult,
                                                       ALU.add).then_inc(centred, 1)
                    sum_squares(t)
                    dve.wait_ge(summed, t + 1)
                    nc.vector.tensor_scalar(var[:, g], var[:, g], 1.0 / HEAD0, LN_EPS, ALU.mult, ALU.add).then_inc(var_ready, 1)

                def sum_squares(t):
                    dve.wait_ge(squared, t + 1)
                    nc.vector.tensor_reduce(var[:, t // GROUP, (t % GROUP) * HEADS:(t % GROUP + 1) * HEADS],
                                            by_head(square[:, t % 2, :]), AX.X, ALU.add).then_inc(summed, 1)

                def normalise(g):
                    dve.wait_ge(std_ready, g + 1)
                    inverse_root(dve, nc, chain, std[:, g], var[:, g], work)
                    for t in range(g * GROUP, (g + 1) * GROUP):
                        nc.vector.tensor_tensor(by_head(kv[:, t, :]), by_head(kv[:, t, :]),
                                                std[:, g, (t % GROUP) * HEADS:(t % GROUP + 1) * HEADS].unsqueeze(2)
                                                .broadcast_to([P, HEADS, HEAD0]), ALU.mult).then_inc(scaled, 1)

                nc.vector.memset(heads_vk[:], 0.0).then_inc(zeroed, 1)
                measure(0)
                for g in range(GROUPS):
                    if g + 1 < GROUPS:
                        measure(g + 1)
                    normalise(g)
                nc.vector.tensor_copy(in_degree[:].unsqueeze(2), mean_in[:, :, DIM:])
                for d, sums in enumerate((mean_in, mean_out)):
                    last = nc.vector.tensor_scalar(degrees[:, d], sums[:, :, DIM:], 1.0, None, ALU.max)
                chain.tick(last)
                chain.wait(dve)
                chain.tick(nc.vector.reciprocal(degrees[:], degrees[:]))
                chain.wait(dve)
                for d, sums in enumerate((mean_in, mean_out)):
                    nc.vector.tensor_tensor(sums[:, :, 0:DIM], sums[:, :, 0:DIM], degrees[:, d].broadcast_to([P, TILES, DIM]),
                                            ALU.mult)

            @block.gpsimd
            def _(pool):
                pool.wait_ge(loaded, 6 * 16)
                for t in range(TILES):
                    tile = row(kv, t).rearrange("p (n h d) -> p n h d", n=2, d=HEAD0)
                    pool.wait_ge(scaled, t + 1)
                    nc.gpsimd.tensor_tensor(tile, tile, gain[:].unsqueeze(2).broadcast_to([P, 2, HEADS0, HEAD0]),
                                            ALU.mult).then_inc(gained, 1)
                    pool.wait_ge(gained, t + 1)
                    nc.gpsimd.tensor_tensor(tile, tile, shift[:].unsqueeze(2).broadcast_to([P, 2, HEADS0, HEAD0]),
                                            ALU.add).then_inc(shifted, 1)

            @block.scalar
            def _(act):
                for t in range(TILES):
                    act.wait_ge(centred, t + 1)
                    if t >= 2:
                        act.wait_ge(summed, t - 1)
                    nc.scalar.activation(square[:, t % 2, :], kv[:, t, :], ACT.Square).then_inc(squared, 1)
                    if t % GROUP == GROUP - 1:
                        g = t // GROUP
                        act.wait_ge(var_ready, g + 1)
                        nc.scalar.activation(std[:, g], var[:, g], ACT.Sqrt).then_inc(std_ready, 1)
                act.wait_ge(vk_ready, 1)
                act.wait_ge(zeroed, 1)
                for b in range(KB):
                    for h in range(128 // HEAD0):
                        d = slice(h * HEAD0, (h + 1) * HEAD0)
                        last = nc.scalar.activation(heads_vk[d, b, d], vk[d, b, d], ACT.Copy, scale=1.0 / NODES)
                last.then_inc(heads_ready, 1)
                act.wait_ge(kv_wo_ready, 1)
                nc.scalar.activation(kv_wo[:], product[:, :, 0:DIM], ACT.Copy).then_inc(kv_wo_kept, 1)
                act.wait_ge(mixer_ready, 1)
                nc.scalar.activation(mixer[:], product[:, :, 0:DIM], ACT.Copy)


def sage_and_mix(p, c, A, x, xn_T, mean_in, mean_out, mixer):
    nc = p.nc
    HALF = DIM // 2
    with ExitStack() as scope:
        sb = lambda name, shape, dtype=F32: p.sb("sg_" + name, shape, dtype, scope)
        w_r = sb("w_r", [128, KB, DIM])
        w_l = sb("w_l", [128, 2, KB, HALF])
        bias, gamma, beta, bo = (sb(n, [P, DIM]) for n in ("bias", "gamma", "beta", "bo"))
        means_T = sb("means_T", [128, 2, 2 * KB * P])
        h = mean_in
        square = sb("square", [P, 2, DIM])
        total = sb("total", [P, 2, DIM])
        average, var, std, work = (sb(n, [P, DIM]) for n in ("average", "var", "std", "work"))
        turned = p.ps("sg_turned", [128, 2, 512], scope=scope)
        projected = p.ps("sg_projected", [P, 2, 512], scope=scope)
        sums = p.ps("sg_sums", [P, 2, 512], scope=scope)
        mixed = p.ps("sg_mixed", [P, 2, 512], scope=scope)
        w_loaded, loaded, turn_ready, turn_copied = p.sem("sg_w_loaded"), p.sem("sg_loaded"), p.sem("sg_turn_ready"), p.sem("sg_turn_copied")
        projected_ready, h_ready = p.sem("sg_projected_ready"), p.sem("sg_h_ready")
        sum_ready, centred, squared, square_summed = (p.sem("sg_sum_ready"), p.sem("sg_centred"), p.sem("sg_squared"),
                                                      p.sem("sg_square_summed"))
        var_ready, std_ready = p.sem("sg_var_ready"), p.sem("sg_std_ready")
        scaled, shifted, mixed_ready, added, finished = (p.sem("sg_scaled"), p.sem("sg_shifted"), p.sem("sg_mixed_ready"),
                                                         p.sem("sg_added"), p.sem("sg_finished"))
        joined, totalled, squares_ready = p.sem("sg_joined"), p.sem("sg_totalled"), p.sem("sg_squares_ready")
        chain = Chain(p.sem("sg_chain"))
        LOADS = 5
        with nc.Block() as block:
            @block.sync
            def _(sp):
                by_block = lambda a: a.rearrange("(k p) n -> p k n", p=128)
                for d, (l, r, b) in enumerate((("W_l_f_T", "W_r_f_T", "b_l_f"), ("W_l_b_T", "W_r_b_T", "b_l_b"))):
                    at = slice(d * HALF, (d + 1) * HALF)
                    sp.dma_start(w_r[:, :, at], by_block(A[r])).then_inc(w_loaded, 16)
                    sp.dma_start(w_l[:, d, :, :], by_block(A[l])).then_inc(w_loaded, 16)
                    sp.dma_start(bias[:, at], A[b].partition_broadcast(P)).then_inc(loaded, 16)
                for to, name in ((gamma, "bn_gamma"), (beta, "bn_beta"), (bo, "bo")):
                    sp.dma_start(to[:], A[name].partition_broadcast(P)).then_inc(loaded, 16)
                sp.wait_ge(loaded, LOADS * 16)

            @block.tensor
            def _(pe):
                def turn(t):
                    if t >= 2:
                        pe.wait_ge(turn_copied, t - 1)
                    for d, means in enumerate((mean_in, mean_out)):
                        for k in range(KB):
                            n = d * KB + k
                            last = nc.tensor.transpose(turned[:, t % 2, n * P:(n + 1) * P],
                                                       means[:, t, k * 128:(k + 1) * 128], c.ident[:P, :P])
                    last.then_inc(turn_ready, 1)

                turn(0)
                pe.wait_ge(w_loaded, 4 * 16)
                for t in range(TILES):
                    if t + 1 < TILES:
                        turn(t + 1)
                    if t >= 2:
                        pe.wait_ge(h_ready, t - 1)
                    for k in range(KB):
                        nc.tensor.matmul(projected[:, t % 2, 0:DIM], xn_T[:, k, t * P:(t + 1) * P], w_r[:, k, :],
                                         start=(k == 0), stop=False, skip_group_check=True)
                    pe.wait_ge(turn_copied, t + 1)
                    for d in range(2):
                        for k in range(KB):
                            n = d * KB + k
                            last = nc.tensor.matmul(projected[:, t % 2, d * HALF:(d + 1) * HALF],
                                                    means_T[:, t % 2, n * P:(n + 1) * P], w_l[:, d, k, :],
                                                    start=False, stop=(k == KB - 1), skip_group_check=True)
                    last.then_inc(projected_ready, 1)
                pe.wait_ge(totalled, TILES + 1)
                nc.tensor.matmul(sums[:, 0, 0:DIM], c.ones[:P, :P], total[:, 0, :], start=True, stop=True).then_inc(sum_ready, 1)
                for t in range(TILES):
                    if t >= 2:
                        pe.wait_ge(added, t - 1)
                    for k in range(KB):
                        last = nc.tensor.matmul(mixed[:, t % 2, 0:DIM], xn_T[:, k, t * P:(t + 1) * P], mixer[:, k, :],
                                                start=(k == 0), stop=(k == KB - 1))
                    last.then_inc(mixed_ready, 1)
                pe.wait_ge(square_summed, TILES)
                nc.tensor.matmul(sums[:, 1, 0:DIM], c.ones[:P, :P], total[:, 1, :], start=True, stop=True).then_inc(squares_ready, 1)

            @block.scalar
            def _(act):
                for t in range(TILES):
                    act.wait_ge(turn_ready, t + 1)
                    nc.scalar.activation(means_T[:, bass.ds(t % 2, 1), :].rearrange("p a d -> p (a d)"),
                                         turned[:, bass.ds(t % 2, 1), 0:2 * KB * P].rearrange("p a d -> p (a d)"),
                                         ACT.Copy).then_inc(turn_copied, 1)
                for t in range(TILES):
                    act.wait_ge(centred, t + 1)
                    if t >= 2:
                        act.wait_ge(square_summed, t - 1)
                    nc.scalar.activation(square[:, bass.ds(t % 2, 1), :].rearrange("p a d -> p (a d)"), row(h, t),
                                         ACT.Square).then_inc(squared, 1)
                act.wait_ge(var_ready, 1)
                nc.scalar.activation(std[:], var[:], ACT.Sqrt).then_inc(std_ready, 1)

            @block.vector
            def _(dve):
                def mix(t):
                    dve.wait_ge(mixed_ready, t + 1)
                    dve.wait_ge(finished, t + 1)
                    nc.vector.tensor_tensor(x[:, t, :], mixed[:, t % 2, 0:DIM], x[:, t, :], ALU.add).then_inc(added, 1)

                def measure(t):
                    dve.wait_ge(joined, t + 1)
                    nc.vector.bn_stats(c.stats[:, t * 6:(t + 1) * 6], x[:, t, :])

                dve.wait_ge(loaded, LOADS * 16)
                for t in range(TILES):
                    dve.wait_ge(projected_ready, t + 1)
                    nc.vector.tensor_tensor(row(h, t), projected[:, bass.ds(t % 2, 1), 0:DIM].rearrange("p a d -> p (a d)"),
                                            bias[:], ALU.add).then_inc(h_ready, 1)
                dve.wait_ge(sum_ready, 1)
                chain.tick(nc.vector.tensor_scalar(average[:], sums[:, 0, 0:DIM], 1.0 / NODES, None, ALU.mult))
                chain.wait(dve)
                for t in range(TILES):
                    nc.vector.tensor_tensor(row(h, t), row(h, t), average[:], ALU.subtract).then_inc(centred, 1)
                    if t >= 1:
                        mix(t - 1)
                mix(TILES - 1)
                dve.wait_ge(squares_ready, 1)
                chain.tick(nc.vector.tensor_scalar(var[:], sums[:, 1, 0:DIM], 1.0 / NODES, LN_EPS, ALU.mult, ALU.add))
                chain.wait(dve)
                nc.vector.engine_nop().then_inc(var_ready, 1)
                dve.wait_ge(std_ready, 1)
                inverse_root(dve, nc, chain, std, var, work)
                chain.tick(nc.vector.tensor_tensor(std[:], std[:], gamma[:], ALU.mult))
                chain.wait(dve)
                dve.wait_ge(centred, TILES)
                for t in range(TILES):
                    nc.vector.tensor_tensor(row(h, t), row(h, t), std[:], ALU.mult).then_inc(scaled, 1)
                dve.wait_ge(added, TILES)
                for t in range(TILES):
                    dve.wait_ge(shifted, t + 1)
                    nc.vector.scalar_tensor_tensor(row(x, t), row(h, t), 0.0, row(x, t), ALU.max, ALU.add).then_inc(joined, 1)
                    if t >= 1:
                        measure(t - 1)
                measure(TILES - 1)

            @block.gpsimd
            def _(pool):
                nc.gpsimd.memset(total[:], 0.0).then_inc(totalled, 1)
                pool.wait_ge(loaded, LOADS * 16)
                for t in range(TILES):
                    nc.gpsimd.tensor_tensor(row(x, t), row(x, t), bo[:], ALU.add).then_inc(finished, 1)
                    pool.wait_ge(totalled, t + 1)
                    pool.wait_ge(h_ready, t + 1)
                    nc.gpsimd.tensor_tensor(total[:, 0, :], total[:, 0, :], h[:, t, :], ALU.add).then_inc(totalled, 1)
                for t in range(TILES):
                    if t >= 1:
                        pool.wait_ge(square_summed, t)
                    pool.wait_ge(squared, t + 1)
                    nc.gpsimd.tensor_tensor(total[:, 1, :], total[:, 1, :], square[:, t % 2, :], ALU.add).then_inc(square_summed, 1)
                for t in range(TILES):
                    pool.wait_ge(scaled, t + 1)
                    nc.gpsimd.tensor_tensor(row(h, t), row(h, t), beta[:], ALU.add).then_inc(shifted, 1)


class Gate:

    def __init__(self, p, scope, name, top, bias=None):
        self.nc, self.top, self.bias = p.nc, top, bias
        sb = lambda n, shape, dtype=F32: p.sb(f"{name}_{n}", shape, dtype, scope)
        self.raw, self.prob = sb("raw", [P, TILES, EXPERTS]), sb("prob", [P, TILES, EXPERTS])
        self.order_i, self.order = sb("order_i", [P, EXPERTS], I32), sb("order", [P, EXPERTS])
        self.peak, self.total, self.place = sb("peak", [P, TILES]), sb("total", [P, TILES]), sb("place", [P, TILES])
        self.chosen = [sb(f"chosen{n}", [P, TILES, EXPERTS]) for n in range(top)]
        self.best = [sb(f"best{n}", [P, TILES]) for n in range(top)]
        self.shifted, self.exped, self.numbered = (p.sem(f"{name}_shifted"), p.sem(f"{name}_exped"),
                                                   p.sem(f"{name}_numbered"))
        self.chain = Chain(p.sem(f"{name}_chain"))

    def pool_steps(self, pool):
        self.nc.gpsimd.iota(self.order_i[:], [[-1, EXPERTS]], base=EXPERTS, channel_multiplier=0).then_inc(self.numbered, 1)

    def scalar_steps(self, act):
        act.wait_ge(self.shifted, 1)
        self.nc.scalar.activation(self.prob[:], self.raw[:], ACT.Exp).then_inc(self.exped, 1)

    def vector_steps(self, dve, logits, ready, count):
        nc, chain = self.nc, self.chain
        over = lambda a: a[:].unsqueeze(2).broadcast_to([P, TILES, EXPERTS])
        across = lambda a: a[:].unsqueeze(1).broadcast_to([P, TILES, EXPERTS])

        def then(instruction):
            chain.tick(instruction)
            chain.wait(dve)

        dve.wait_ge(self.numbered, 1)
        nc.vector.tensor_copy(self.order[:], self.order_i[:])
        dve.wait_ge(ready, count)
        if self.bias is None:
            then(nc.vector.tensor_copy(self.raw[:], logits))
        else:
            then(nc.vector.tensor_tensor(self.raw[:], logits, across(self.bias), ALU.add))
        then(nc.vector.tensor_reduce(self.peak[:], self.raw[:], AX.X, ALU.max))
        nc.vector.tensor_tensor(self.raw[:], self.raw[:], over(self.peak), ALU.subtract).then_inc(self.shifted, 1)
        dve.wait_ge(self.exped, 1)
        then(nc.vector.tensor_reduce(self.total[:], self.prob[:], AX.X, ALU.add))
        then(nc.vector.reciprocal(self.total[:], self.total[:]))
        then(nc.vector.tensor_tensor(self.prob[:], self.prob[:], over(self.total), ALU.mult))
        for n in range(self.top):
            then(nc.vector.tensor_reduce(self.best[n][:], self.prob[:], AX.X, ALU.max))
            then(nc.vector.tensor_tensor(self.raw[:], self.prob[:], over(self.best[n]), ALU.is_equal))
            then(nc.vector.tensor_tensor(self.raw[:], self.raw[:], across(self.order), ALU.mult))
            then(nc.vector.tensor_reduce(self.place[:], self.raw[:], AX.X, ALU.max))
            then(nc.vector.tensor_tensor(self.chosen[n][:], self.raw[:], over(self.place), ALU.is_equal))
            if n + 1 < self.top:
                then(nc.vector.scalar_tensor_tensor(self.prob[:], self.chosen[n][:], -2.0, self.prob[:], ALU.mult, ALU.add))


class Dispatch:

    def __init__(self, p, c, scope, name, top):
        self.nc, self.c, self.top = p.nc, c, top
        self.tiles = (top * NODES + EXPERTS * (P - 1)) // P
        sb = lambda n, shape, dtype=F32: p.sb(f"{name}_{n}", shape, dtype, scope)
        W = TILES * EXPERTS
        self.width = W
        self.earlier = sb("earlier", [P, P])
        self.tile_start_i, self.tile_start = sb("tile_start_i", [P, top * TILES], I32), sb("tile_start", [P, top * TILES])
        self.tile_i, self.tile = sb("tile_i", [1, self.tiles], I32), sb("tile", [1, self.tiles])
        self.counts = [sb(f"counts{i}", [P, top * TILES, EXPERTS]) for i in range(2)]
        self.place = sb("place", [P, TILES, EXPERTS])
        self.size = sb("size", [P, EXPERTS])
        self.full = sb("full", [P, EXPERTS, top * TILES])
        self.first = [sb(f"first{i}", [P, EXPERTS]) for i in range(2)]
        self.own = sb("own", [1, self.tiles, EXPERTS - 1])
        self.owner_f, self.owner = sb("owner_f", [1, self.tiles]), sb("owner", [1, self.tiles], I32)
        self.slot_f = sb("slot_f", [P, TILES])
        self.slot = [sb(f"slot{n}", [P, TILES], I32) for n in range(top)]
        self.before = p.ps(f"{name}_before", [P, top, W], scope=scope)
        self.number = p.ps(f"{name}_number", [P, top, W], scope=scope)
        self.made, self.counted, self.ready = p.sem(f"{name}_made"), p.sem(f"{name}_counted"), p.sem(f"{name}_ready")
        self.chosen_ready = p.sem(f"{name}_chosen_ready")
        self.chain = Chain(p.sem(f"{name}_chain"))

    def pool_steps(self, pool):
        nc = self.nc
        nc.gpsimd.memset(self.earlier[:], 1.0)
        nc.gpsimd.iota(self.tile_start_i[:], [[P, self.top * TILES]], base=0, channel_multiplier=0)
        nc.gpsimd.iota(self.tile_i[:], [[1, self.tiles]], base=0, channel_multiplier=0).then_inc(self.made, 1)
        pool.wait_ge(self.made, 1)
        nc.gpsimd.affine_select(out=self.earlier[:], in_=self.earlier[:], compare_op=ALU.is_gt, fill=0.0, base=0,
                                pattern=[[1, P]], channel_multiplier=-1).then_inc(self.made, 1)

    def tensor_steps(self, pe, gate):
        nc = self.nc
        pe.wait_ge(self.made, 2)
        pe.wait_ge(self.chosen_ready, 1)
        for n in range(self.top):
            chosen = gate.chosen[n][:].rearrange("p t e -> p (t e)")
            nc.tensor.matmul(self.before[:, n, :], self.earlier[:], chosen, start=True, stop=True)
            last = nc.tensor.matmul(self.number[:, n, :], self.c.ones[:P, :P], chosen, start=True, stop=True)
        last.then_inc(self.counted, 1)

    def vector_steps(self, dve, gate):
        nc, chain, top = self.nc, self.chain, self.top

        def then(instruction):
            chain.tick(instruction)
            chain.wait(dve)

        nc.vector.engine_nop().then_inc(self.chosen_ready, 1)
        dve.wait_ge(self.made, 2)
        nc.vector.tensor_copy(self.tile[:], self.tile_i[:])
        then(nc.vector.tensor_copy(self.tile_start[:], self.tile_start_i[:]))
        dve.wait_ge(self.counted, 1)
        now, new = self.counts
        then(nc.vector.tensor_copy(now[:].rearrange("p (n t) e -> p n (t e)", n=top), self.number[:]))
        step = 1
        while step < top * TILES:
            nc.vector.tensor_copy(new[:, 0:step, :], now[:, 0:step, :])
            then(nc.vector.tensor_tensor(new[:, step:, :], now[:, step:, :], now[:, :top * TILES - step, :], ALU.add))
            now, new, step = new, now, 2 * step
        then(nc.vector.tensor_copy(self.size[:], now[:, top * TILES - 1, :]))
        then(nc.vector.tensor_tensor(self.full[:], self.size[:].unsqueeze(2).broadcast_to([P, EXPERTS, top * TILES]),
                                     self.tile_start[:].unsqueeze(1).broadcast_to([P, EXPERTS, top * TILES]), ALU.is_gt))
        a, b = self.first
        then(nc.vector.tensor_reduce(self.size[:], self.full[:], AX.X, ALU.add))
        then(nc.vector.tensor_copy(a[:], self.size[:]))
        step = 1
        while step < EXPERTS:
            nc.vector.tensor_copy(b[:, 0:step], a[:, 0:step])
            then(nc.vector.tensor_tensor(b[:, step:], a[:, step:], a[:, :EXPERTS - step], ALU.add))
            a, b, step = b, a, 2 * step
        then(nc.vector.tensor_tensor(b[:], a[:], self.size[:], ALU.subtract))
        then(nc.vector.tensor_tensor(self.own[:], self.tile[:].unsqueeze(2).broadcast_to([1, self.tiles, EXPERTS - 1]),
                                     b[0:1, 1:].unsqueeze(1).broadcast_to([1, self.tiles, EXPERTS - 1]), ALU.is_ge))
        then(nc.vector.tensor_reduce(self.owner_f[:], self.own[:], AX.X, ALU.add))
        nc.vector.tensor_copy(self.owner[:], self.owner_f[:])
        for n in range(top):
            mine = slice(n * TILES, (n + 1) * TILES)
            then(nc.vector.tensor_tensor(self.place[:], now[:, mine, :], self.number[:, n, :].rearrange("p (t e) -> p t e", e=EXPERTS),
                                         ALU.subtract))
            then(nc.vector.tensor_tensor(self.place[:], self.place[:], self.before[:, n, :].rearrange("p (t e) -> p t e", e=EXPERTS),
                                         ALU.add))
            then(nc.vector.scalar_tensor_tensor(self.place[:], b[:].unsqueeze(1).broadcast_to([P, TILES, EXPERTS]), float(P),
                                                self.place[:], ALU.mult, ALU.add))
            then(nc.vector.tensor_tensor(self.place[:], self.place[:], gate.chosen[n][:], ALU.mult))
            then(nc.vector.tensor_reduce(self.slot_f[:], self.place[:], AX.X, ALU.add))
            then(nc.vector.tensor_copy(self.slot[n][:], self.slot_f[:]))
        nc.vector.engine_nop().then_inc(self.ready, 1)


def mixture(p, c, A, state, x, xn, xn_T):
    nc = p.nc
    TOP, QUAD, RESULTS, AHEAD = 2, 4, 4, 2
    W1 = KB * DIM + KB
    SENT = ROW - DIM
    with ExitStack() as scope:
        sb = lambda name, shape, dtype=F32: p.sb("mx_" + name, shape, dtype, scope)
        sem = lambda n, recycled=True: p.sem("mx_" + n, recycled)
        gate = Gate(p, scope, "mg", TOP)
        way = Dispatch(p, c, scope, "md", TOP)
        SORTED = sorted_tiles(TOP)
        GROUPS = SORTED // QUAD
        sorted_rows = c.blanks.choice_rows
        answers = nc.dram_tensor("mx_answers", [TOP * NODES, DIM], F32).ap()
        router = sb("router", [128, KB, EXPERTS])
        w1 = sb("w1", [128, EXPERTS * W1])
        w2 = sb("w2", [128, EXPERTS * KB * DIM])
        b2 = sb("b2", [P, EXPERTS * DIM])
        w1_now = [sb(f"w1_now{u}", [128, W1]) for u in range(AHEAD + 1)]
        rows = sb("rows", [P, 2, QUAD, SENT])
        rows_T = sb("rows_T", [128, 2, KB, CHUNK])
        hidden = sb("hidden", [128, 2, KB, P])
        result = sb("result", [P, RESULTS, DIM])
        number = sb("number", [P, 2, QUAD], I32)
        node_i = sb("node_i", [P, TILES], I32)
        answer = sb("answer", [P, TOP, TILES, DIM])
        logits = p.ps("mx_logits", [P, TILES, EXPERTS], scope=scope)
        turned = p.ps("mx_turned", [128, 512], scope=scope)
        up = p.ps("mx_up", [128, 2, 512], scope=scope)
        down = p.ps("mx_down", [P, 2, 512], scope=scope)
        router_loaded, w_loaded, numbered = sem("router_loaded"), sem("w_loaded"), sem("numbered")
        logits_ready, based, rows_numbered, sent = sem("logits_ready"), sem("based"), sem("rows_numbered"), sem("sent", False)
        rows_loaded = [sem(f"rows_loaded{u}") for u in range(2)]
        turn_ready, turn_copied, w1_ready, up_ready, hidden_ready = (sem("turn_ready"), sem("turn_copied"), sem("w1_ready"),
                                                                     sem("up_ready"), sem("hidden_ready"))
        down_ready, result_ready, number_ready = sem("down_ready"), sem("result_ready"), sem("number_ready")
        written = [sem(f"written{u}", False) for u in range(RESULTS)]
        answered = [[sem(f"answered{n}_{q}") for q in range(CHUNKS)] for n in range(TOP)]
        added = sem("added")
        by_block = lambda a: a.rearrange("(k p) n -> p k n", p=128)
        WEIGHTS = 3 * EXPERTS + 1

        def owner(engine, i):
            i = min(i, way.tiles - 1)
            return engine.value_load(way.owner[0:1, i:i + 1], min_val=0, max_val=EXPERTS - 1)

        with nc.Block() as block:
            @block.sync
            def _(sp):
                sp.dma_start(router[:], by_block(A["router_T"])).then_inc(router_loaded, 16)
                for e in range(EXPERTS):
                    mine = w1[:, e * W1:(e + 1) * W1]
                    sp.dma_start(mine[:, 0:KB * DIM].rearrange("p (k n) -> p k n", k=KB), by_block(A["ffn0_w1"][e])).then_inc(w_loaded, 16)
                    sp.dma_start(mine[:, KB * DIM:], A["ffn0_b1_T"][:, e * KB:(e + 1) * KB]).then_inc(w_loaded, 16)
                    sp.dma_start(w2[:, e * KB * DIM:(e + 1) * KB * DIM].rearrange("p (k n) -> p k n", k=KB),
                                 by_block(A["ffn0_w2"][e])).then_inc(w_loaded, 16)
                sp.dma_start(b2[:], A["ffn0_b2"].rearrange("e n -> (e n)").partition_broadcast(P)).then_inc(w_loaded, 16)
                sp.wait_ge(router_loaded, 16)
                sp.wait_ge(sent, TOP * TILES * 16)
                for g in range(GROUPS):
                    if g >= 2:
                        sp.wait_ge(turn_ready, (g - 1) * KB)
                        sp.wait_ge(number_ready, g - 1)
                    load_rows(sp, rows[:, g % 2], sorted_rows[g * QUAD * P:(g + 1) * QUAD * P, :]
                              .rearrange("(j p) d -> p j d", p=P), rows_loaded[g % 2])
                for u in range(RESULTS):
                    sp.wait_ge(written[u], SORTED // RESULTS * 16)
                for q in range(CHUNKS):
                    for n in range(TOP):
                        load_rows(sp, answer[:, n, q * QUAD:(q + 1) * QUAD, :],
                                  answers[n * NODES + q * CHUNK:n * NODES + (q + 1) * CHUNK, :]
                                  .rearrange("(t p) d -> p t d", p=P), answered[n][q])

            @block.gpsimd
            def _(pool):
                gate.pool_steps(pool)
                way.pool_steps(pool)
                nc.gpsimd.iota(node_i[:], [[P, TILES]], base=0, channel_multiplier=1).then_inc(numbered, 1)
                for t in range(TILES):
                    nc.gpsimd.tensor_tensor(x[:, t, :], x[:, t, :], xn[:, t, 0:DIM], ALU.add).then_inc(based, 1)
                pool.wait_ge(way.ready, 1)
                for n in range(TOP):
                    pool.wait_ge(rows_numbered, n + 1)
                    for t in range(TILES):
                        nc.gpsimd.indirect_dma_start(out=sorted_rows, out_offset=bass.IndirectOffsetOnAxis(
                            ap=way.slot[n][:, t:t + 1].bitcast(mybir.dt.uint32), axis=0), in_=state[:, t, DIM:ROW],
                            in_offset=None).then_inc(sent, 16)
                for i in range(SORTED):
                    pool.wait_ge(number_ready, i // QUAD + 1)
                    pool.wait_ge(result_ready, i + 1)
                    nc.gpsimd.indirect_dma_start(out=answers, out_offset=bass.IndirectOffsetOnAxis(
                        ap=number[:, (i // QUAD) % 2, i % QUAD:i % QUAD + 1].bitcast(mybir.dt.uint32), axis=0),
                        in_=result[:, i % RESULTS, :], in_offset=None, bounds_check=TOP * NODES - 1,
                        oob_is_err=False).then_inc(written[i % RESULTS], 16)

            @block.tensor
            def _(pe):
                def turn(g, k):
                    pe.wait_ge(rows_loaded[g % 2], 32 * (g // 2 + 1))
                    if g * KB + k:
                        pe.wait_ge(turn_copied, g * KB + k)
                    for j in range(QUAD):
                        last = nc.tensor.transpose(turned[:, j * P:(j + 1) * P], rows[:, g % 2, j, k * 128:(k + 1) * 128],
                                                   c.ident[:P, :P])
                    last.then_inc(turn_ready, 1)

                def raise_up(i):
                    g, j = i // QUAD, i % QUAD
                    pe.wait_ge(turn_copied, (g + 1) * KB)
                    pe.wait_ge(w1_ready, i + 1)
                    if i >= 2:
                        pe.wait_ge(hidden_ready, i - 1)
                    for m in range(KB):
                        for k in range(KB):
                            last = nc.tensor.matmul(up[:, i % 2, m * P:(m + 1) * P],
                                                    w1_now[i % (AHEAD + 1)][:, k * DIM + m * 128:k * DIM + (m + 1) * 128],
                                                    rows_T[:, g % 2, k, j * P:(j + 1) * P], start=(k == 0), stop=(k == KB - 1))
                    last.then_inc(up_ready, 1)

                def bring_down(i, expert):
                    pe.wait_ge(hidden_ready, i + 1)
                    if i >= 2:
                        pe.wait_ge(result_ready, i - 1)
                    for m in range(KB):
                        last = nc.tensor.matmul(down[:, i % 2, 0:DIM], hidden[:, i % 2, m, :],
                                                w2[:, bass.ds(expert * (KB * DIM) + m * DIM, DIM)], start=(m == 0),
                                                stop=(m == KB - 1))
                    last.then_inc(down_ready, 1)

                pe.wait_ge(router_loaded, 16)
                for t in range(TILES):
                    for k in range(KB):
                        last = nc.tensor.matmul(logits[:, t, :], xn_T[:, k, t * P:(t + 1) * P], router[:, k, :],
                                                start=(k == 0), stop=(k == KB - 1))
                    last.then_inc(logits_ready, 1)
                way.tensor_steps(pe, gate)
                pe.wait_ge(way.ready, 1)
                pe.wait_ge(w_loaded, WEIGHTS * 16)
                experts = [owner(pe, j) for j in range(QUAD)]
                for k in range(KB):
                    turn(0, k)
                raise_up(0)
                for i in range(SORTED):
                    g, j = i // QUAD, i % QUAD
                    if j < KB and g + 1 < GROUPS:
                        turn(g + 1, j)
                    if i + 1 < SORTED:
                        raise_up(i + 1)
                    bring_down(i, experts[j])
                    if j == QUAD - 1 and g + 1 < GROUPS:
                        experts = [owner(pe, i + 1 + k) for k in range(QUAD)]

            @block.scalar
            def _(act):
                def keep_turned(g, k):
                    act.wait_ge(turn_ready, g * KB + k + 1)
                    nc.scalar.activation(rows_T[:, g % 2, k, :], turned[:, 0:CHUNK], ACT.Copy).then_inc(turn_copied, 1)

                gate.scalar_steps(act)
                for k in range(KB):
                    keep_turned(0, k)
                for i in range(SORTED):
                    act.wait_ge(up_ready, i + 1)
                    if i >= 2:
                        act.wait_ge(down_ready, i - 1)
                    for m in range(KB):
                        last = nc.scalar.activation(hidden[:, i % 2, m, :], up[:, i % 2, m * P:(m + 1) * P], ACT.Gelu,
                                                    bias=w1_now[i % (AHEAD + 1)][:, KB * DIM + m:KB * DIM + m + 1])
                    last.then_inc(hidden_ready, 1)
                    if i % QUAD < KB and i // QUAD + 1 < GROUPS:
                        keep_turned(i // QUAD + 1, i % QUAD)

            @block.vector
            def _(dve):
                chain = Chain(sem("chain"))

                def then(instruction):
                    chain.tick(instruction)
                    chain.wait(dve)

                def fetch_w1(i, expert):
                    if i > AHEAD:
                        dve.wait_ge(hidden_ready, i - AHEAD)
                    nc.vector.tensor_copy(w1_now[i % (AHEAD + 1)][:], w1[:, bass.ds(expert * W1, W1)]).then_inc(w1_ready, 1)

                dve.wait_ge(numbered, 1)
                then(nc.vector.memset(state[:, :, SHARE:NUMBER], 0.0))
                nc.vector.tensor_copy(state[:, :, NUMBER:ROW], node_i[:].unsqueeze(2)).then_inc(rows_numbered, 1)
                gate.vector_steps(dve, logits[:], logits_ready, TILES)
                way.vector_steps(dve, gate)
                then(nc.vector.tensor_tensor(gate.total[:], gate.best[0][:], gate.best[1][:], ALU.add))
                then(nc.vector.tensor_scalar(gate.total[:], gate.total[:], 1e-12, None, ALU.max))
                then(nc.vector.reciprocal(gate.total[:], gate.total[:]))
                for n in range(TOP):
                    then(nc.vector.tensor_tensor(gate.best[n][:], gate.best[n][:], gate.total[:], ALU.mult))
                for n in range(1, TOP):
                    dve.wait_ge(sent, n * TILES * 16)
                    dve.wait_ge(rows_numbered, n)
                    nc.vector.tensor_scalar(state[:, :, NUMBER:ROW], state[:, :, NUMBER:ROW], float(NODES), None,
                                            ALU.add).then_inc(rows_numbered, 1)
                dve.wait_ge(w_loaded, WEIGHTS * 16)
                experts = [owner(dve, i) for i in range(AHEAD + 1)]
                for i in range(AHEAD):
                    fetch_w1(i, experts[i])
                for i in range(SORTED):
                    g, j = i // QUAD, i % QUAD
                    if j == 0:
                        dve.wait_ge(rows_loaded[g % 2], 32 * (g // 2 + 1))
                        if g >= 2:
                            for u in range(RESULTS):
                                dve.wait_ge(written[u], 16 * (g - 1))
                        nc.vector.tensor_copy(number[:, g % 2, :].unsqueeze(2), rows[:, g % 2, :, SENT - 1:]).then_inc(number_ready, 1)
                    if i + AHEAD < SORTED:
                        fetch_w1(i + AHEAD, experts[(i + AHEAD) % (AHEAD + 1)])
                    dve.wait_ge(down_ready, i + 1)
                    if i >= RESULTS:
                        dve.wait_ge(written[i % RESULTS], 16 * (i // RESULTS))
                    nc.vector.tensor_tensor(result[:, i % RESULTS, :], down[:, i % 2, 0:DIM], b2[:, bass.ds(experts[i % (AHEAD + 1)] * DIM, DIM)],
                                            ALU.add).then_inc(result_ready, 1)
                    experts[i % (AHEAD + 1)] = owner(dve, i + AHEAD + 1)
                dve.wait_ge(based, TILES)
                for t in range(TILES):
                    for n in range(TOP):
                        dve.wait_ge(answered[n][t // QUAD], 32)
                        if n:
                            dve.wait_ge(added, t * (TOP - 1) + n)
                        last = nc.vector.scalar_tensor_tensor(x[:, t, :], answer[:, n, t, :], gate.best[n][:, t:t + 1], x[:, t, :],
                                                              ALU.mult, ALU.add)
                        if n + 1 < TOP:
                            last.then_inc(added, 1)


def load_attributes(sp, A, attr, attr_loaded, h, u):
    sp.dma_start(attr[:, u].rearrange("p s k e -> p (s k e)"), A["edge_attr_T"][bass.ds(h * 2 + u, 1)]
                 .rearrange("a p x -> p (a x)")).then_inc(attr_loaded[u], 16)


def to_nodes_first(p, c, A, xn_T, w, attr, attr_loaded, hidden_sum, table):
    nc = p.nc
    with ExitStack() as scope:
        b = p.sb("nf_b", [P, DIM], scope=scope)
        rows = p.sb("nf_rows", [P, TILES, DIM], scope=scope)
        projected = p.ps("nf_projected", [P, 4, 512], scope=scope)
        w_loaded, loaded, ready, kept, stored = p.sem("nf_w_loaded"), p.sem("nf_loaded"), p.sem("nf_ready"), p.sem("nf_kept"), p.sem("nf_stored")
        with nc.Block() as block:
            @block.sync
            def _(sp):
                sp.dma_start(w[:], A["gnn1_W1"].rearrange("(k p) n -> p k n", p=128)).then_inc(w_loaded, 16)
                sp.dma_start(b[:], A["gnn1_b1"].partition_broadcast(P)).then_inc(loaded, 16)
                for u in range(2):
                    load_attributes(sp, A, attr, attr_loaded, 0, u)
                sp.wait_ge(kept, TILES)
                load_rows(sp, table.rearrange("(t p) d -> p t d", p=P), rows[:], stored)
                sp.wait_ge(stored, 32)

            @block.gpsimd
            def _(pool):
                nc.gpsimd.memset(hidden_sum[:], 0.0)

            @block.tensor
            def _(pe):
                pe.wait_ge(w_loaded, 16)
                for t in range(TILES):
                    if t >= 4:
                        pe.wait_ge(kept, t - 3)
                    for k in range(KB):
                        last = nc.tensor.matmul(projected[:, t % 4, 0:DIM], xn_T[:, k, t * P:(t + 1) * P], w[:, k, :],
                                                start=(k == 0), stop=(k == KB - 1))
                    last.then_inc(ready, 1)

            @block.vector
            def _(dve):
                dve.wait_ge(loaded, 16)
                for t in range(TILES):
                    dve.wait_ge(ready, t + 1)
                    nc.vector.tensor_tensor(row(rows, t), projected[:, bass.ds(t % 4, 1), 0:DIM].rearrange("p a d -> p (a d)"),
                                            b[:], ALU.add).then_inc(kept, 1)


def edge_messages(p, c, row_ranges, A, src, dst, w1, attr, attr_loaded, table, hidden_sum):
    nc = p.nc
    SUB = EDGE_TILES // RANGE_ROWS
    TWO, BANKS = 2, SUB // 2
    PAIRS = RANGE_ROWS // 2
    SETS = 4
    TURNS = RANGE_ROWS // SETS
    with ExitStack() as scope:
        sb = lambda name, shape, dtype=F32: p.sb("em_" + name, shape, dtype, scope)
        sem = lambda n: p.sem("em_" + n)
        both = lambda name: [sem(f"{name}{u}") for u in range(2)]
        which = sb("which", [P, SETS, SUB], I32)
        gathered = sb("gathered", [P, SETS, SUB, DIM])
        pre = sb("pre", [P, 2, SUB, DIM])
        hidden = sb("hidden", [P, 2, SUB, DIM])
        hot = sb("hot", [P, 3, SUB, P])
        dst_f = sb("dst_f", [P, EDGE_TILES])
        projected = p.ps("em_projected", [P, 2, BANKS, TWO, DIM], scope=scope)
        total = p.ps("em_total", [P, 3, 512], scope=scope)
        prepared, copied, passed = sem("prepared"), sem("copied"), sem("passed")
        projected_ready, pre_ready, hidden_ready = both("projected_ready"), both("pre_ready"), both("hidden_ready")
        got = [[sem(f"got{v}_{s}") for s in range(SUB)] for v in range(SETS)]
        hot_ready, summed, added = sem("hot_ready"), sem("summed"), sem("added")
        more_hot, more_summed, more_added, more_passed = sem("more_hot"), sem("more_summed"), sem("more_added"), sem("more_passed")

        def load(engine, b, k, low, high):
            return engine.value_load(row_ranges[0:1, bass.ds(b * 3 + k, 1)], min_val=low, max_val=high)

        def load_further(engine, b):
            return load(engine, b, 2, 0, TILES * RANGE_ROWS)

        with nc.Block() as block:
            @block.sync
            def _(sp):
                with sp.Fori(1, PAIRS) as h:
                    for u in range(2):
                        sp.wait_ge(projected_ready[u], h * BANKS)
                        load_attributes(sp, A, attr, attr_loaded, h, u)

            @block.gpsimd
            def _(pool):
                def gather(turn, v):
                    nc.gpsimd.tensor_copy(which[:, v, :], src[:, bass.ds((turn * SETS + v) * SUB, SUB)]).then_inc(copied, 1)
                    pool.wait_ge(copied, turn * SETS + v + 1)
                    pool.sem_inc(passed, 1)
                    for s in range(SUB):
                        nc.gpsimd.indirect_dma_start(
                            out=gathered[:, v, s, :], out_offset=None, in_=table, in_offset=bass.IndirectOffsetOnAxis(
                                ap=which[:, v, s:s + 1].bitcast(mybir.dt.uint32), axis=0)).then_inc(got[v][s], 16)

                for v in range(SETS):
                    gather(0, v)
                with pool.Fori(1, TURNS) as turn:
                    for v in range(SETS):
                        pool.wait_ge(pre_ready[v % 2], (turn * (SETS // 2) + v // 2) * BANKS)
                        gather(turn, v)

            @block.tensor
            def _(pe):
                def project(h, u):
                    pe.wait_ge(attr_loaded[u], (h + 1) * 16)
                    for k in range(BANKS):
                        pe.wait_ge(pre_ready[u], h * BANKS + k + 1)
                        for j in range(TWO):
                            for f in range(KB):
                                last = nc.tensor.matmul(projected[:, u, k, j, :], attr[:, u, k * TWO + j, f, :], w1[:, f, :],
                                                        start=(f == 0), stop=(f == KB - 1))
                        last.then_inc(projected_ready[u], 1)

                def sum_tile(h, u, at, done):
                    for s in range(SUB):
                        pe.wait_ge(hidden_ready[u], h * BANKS + s // TWO + 1)
                        last = nc.tensor.matmul(total[:, at, 0:DIM], hot[:, at, s, :], hidden[:, u, s, :],
                                                start=(s == 0), stop=(s == SUB - 1))
                    last.then_inc(done, 1)

                def add_up(h, u):
                    b = h * 2 + u
                    n, further = load(pe, b, 1, 1, TILES), load_further(pe, b)
                    pe.wait_ge(added, b + 1)
                    pe.wait_ge(hot_ready, b + 1)
                    sum_tile(h, u, u, summed)
                    with pe.If(n > 1):
                        with pe.Fori(1, n) as i:
                            pe.wait_ge(more_added, further + i)
                            pe.wait_ge(more_hot, further + i)
                            sum_tile(h, u, 2, more_summed)

                for u in range(2):
                    pe.sem_inc(pre_ready[u], BANKS)
                project(0, 0)
                project(0, 1)
                with pe.Fori(0, PAIRS - 1) as h:
                    project(h + 1, 0)
                    add_up(h, 0)
                    project(h + 1, 1)
                    add_up(h, 1)
                add_up(PAIRS - 1, 0)
                add_up(PAIRS - 1, 1)

            @block.vector
            def _(dve):
                def combine(turn, v):
                    h, u = turn * (SETS // 2) + v // 2, v % 2
                    for k in range(BANKS):
                        at = slice(k * TWO, (k + 1) * TWO)
                        dve.wait_ge(projected_ready[u], h * BANKS + k + 1)
                        for s in range(k * TWO, (k + 1) * TWO):
                            dve.wait_ge(got[v][s], (turn + 1) * 16)
                        nc.vector.tensor_tensor(pre[:, u, at, :], projected[:, u, k], gathered[:, v, at, :],
                                                ALU.add).then_inc(pre_ready[u], 1)

                def sums(turn, v, meanwhile):
                    b, u = turn * SETS + v, v % 2
                    first, n = load(dve, b, 0, 0, TILES - 1), load(dve, b, 1, 1, TILES)
                    tile = lambda i: (first + i).with_bounds(min_val=0, max_val=TILES - 1)

                    def one_hot(t, at):
                        return nc.vector.tensor_tensor(
                            hot[:, at], c.iota_node_i[:, bass.ds(t * P, P)].unsqueeze(1).broadcast_to([P, SUB, P]),
                            dst_f[:, bass.ds(b * SUB, SUB)].unsqueeze(2).broadcast_to([P, SUB, P]), ALU.is_equal)

                    def keep(t, at):
                        return nc.vector.tensor_tensor(row(hidden_sum, t), total[:, at, 0:DIM], row(hidden_sum, t), ALU.add)

                    one_hot(first, u).then_inc(hot_ready, 1)
                    with dve.If(n > 1):
                        one_hot(tile(1), 2).then_inc(more_hot, 1)
                    meanwhile()
                    dve.wait_ge(summed, b + 1)
                    dve.wait_ge(added, b + 2)
                    keep(first, u).then_inc(added, 1)
                    with dve.If(n > 1):
                        further = load_further(dve, b)
                        dve.wait_ge(more_summed, further + 1)
                        dve.wait_ge(added, b + 3)
                        keep(tile(1), 2).then_inc(more_added, 1)
                        with dve.If(n > 2):
                            with dve.Fori(2, n) as i:
                                one_hot(tile(i), 2).then_inc(more_hot, 1)
                                dve.wait_ge(more_summed, further + i)
                                dve.wait_ge(more_added, further + i)
                                keep(tile(i), 2).then_inc(more_added, 1)
                        dve.wait_ge(more_added, further + n)
                        dve.sem_inc(more_passed, 1)

                nc.vector.tensor_copy(dst_f[:], dst[:]).then_inc(prepared, 1)
                dve.wait_ge(prepared, 1)
                dve.sem_inc(added, 2)
                dve.sem_inc(more_added, 1)
                combine(0, 0)
                with dve.Fori(0, TURNS - 1) as turn:
                    for v in range(SETS):
                        sums(turn, v, lambda: combine(turn, v + 1) if v + 1 < SETS else combine(turn + 1, 0))
                for v in range(SETS):
                    sums(TURNS - 1, v, lambda: v + 1 < SETS and combine(TURNS - 1, v + 1))

            @block.scalar
            def _(act):
                with act.Fori(0, PAIRS) as h:
                    for u in range(2):
                        for k in range(BANKS):
                            at = slice(k * TWO, (k + 1) * TWO)
                            act.wait_ge(pre_ready[u], (h + 1) * BANKS + k + 1)
                            nc.scalar.activation(hidden[:, u, at, :], pre[:, u, at, :], ACT.Relu).then_inc(hidden_ready[u], 1)


def softmax_attention(p, c, A, x, xn, xn_T, hidden_sum, in_degree):
    nc = p.nc
    with ExitStack() as scope:
        sb = lambda name, shape, dtype=F32: p.sb("at_" + name, shape, dtype, scope)
        w = sb("w", [128, KB, 3 * DIM])
        w_out = sb("w_out", [128, KB, DIM])
        w2 = sb("w2", [128, KB, DIM])
        b2, gamma = sb("b2", [P, DIM]), sb("gamma", [P, DIM])
        q, k, v = (sb(n, [P, TILES, DIM]) for n in "qkv")
        q_T = sb("q_T", [128, KB, NODES])
        peak = sb("peak", [P, DIM])
        peak_col = sb("peak_col", [128, KB])
        k_total = sb("k_total", [P, DIM])
        q_peak, q_sum = sb("q_peak", [P, HEADS1]), sb("q_sum", [P, HEADS1])
        heads_vk = sb("heads_vk", [128, KB, 128])
        k_share = sb("k_share", [128, KB])
        kv_wo = sb("kv_wo", [128, KB, DIM])
        sum_T = sb("sum_T", [128, 2, KB * P])
        stats = sb("stats", [P, TILES * 6])
        mean, var, std, half = (sb(n, [P, TILES]) for n in ("mean", "var", "std", "half"))
        out = k
        w_loaded, loaded = p.sem("at_w_loaded"), p.sem("at_loaded")
        chain = Chain(p.sem("at_chain"))
        sem = lambda n: p.sem("at_" + n)
        by_head = lambda a: a.rearrange("p (h d) -> p h d", d=HEAD1)
        spread = lambda a: a[:].unsqueeze(2).broadcast_to([P, HEADS1, HEAD1])
        LOADS = 4
        LAG = 3

        with ExitStack() as first:
            q_bank = p.ps("at_q_bank", [P, 2, 512], scope=first)
            kv_bank = p.ps("at_kv_bank", [P, 2, 512], scope=first)
            turned = p.ps("at_turned", [128, 2, 512], scope=first)
            peaks = p.ps("at_peaks", [128, KB, 512], scope=first)
            qkkv_ready, kv_read = sem("qkkv_ready"), sem("kv_read")
            q_less, q_exped, q_added, q_inverted, q_ready = sem("q_less"), sem("q_exped"), sem("q_added"), sem("q_inverted"), sem("q_ready")
            q_peaked, turn_ready, turn_copied, peaked = sem("q_peaked"), sem("turn_ready"), sem("turn_copied"), sem("peaked")
            passed, peak_turned, peak_found, peak_spread, k_less = sem("passed"), sem("peak_turned"), sem("peak_found"), sem("peak_spread"), sem("k_less")
            with nc.Block() as block:
                @block.sync
                def _(sp):
                    by_block = lambda a: a.rearrange("(k p) n -> p k n", p=128)
                    sp.dma_start(w[:], by_block(A["Wqkv"])).then_inc(w_loaded, 16)
                    sp.dma_start(w_out[:], by_block(A["Wout"])).then_inc(loaded, 16)
                    sp.dma_start(w2[:], by_block(A["gnn1_W2"])).then_inc(loaded, 16)
                    sp.dma_start(b2[:], A["gnn1_b2"].partition_broadcast(P)).then_inc(loaded, 16)
                    sp.dma_start(gamma[:], A["mix1_gamma"].partition_broadcast(P)).then_inc(loaded, 16)
                    sp.wait_ge(loaded, LOADS * 16)

                @block.tensor
                def _(pe):
                    def turn(t):
                        pe.wait_ge(q_ready, t + 1)
                        if t >= 2:
                            pe.wait_ge(turn_copied, t - 1)
                        for b in range(KB):
                            last = nc.tensor.transpose(turned[:, t % 2, b * P:(b + 1) * P], q[:, t, b * 128:(b + 1) * 128],
                                                       c.ident[:P, :P])
                        last.then_inc(turn_ready, 1)

                    pe.wait_ge(w_loaded, 16)
                    for t in range(TILES):
                        if t >= 2:
                            pe.wait_ge(q_less, t - 1)
                            pe.wait_ge(kv_read, 2 * (t - 1))
                        for b in range(KB):
                            nc.tensor.matmul(q_bank[:, t % 2, 0:DIM], xn_T[:, b, t * P:(t + 1) * P], w[:, b, 0:DIM],
                                             start=(b == 0), stop=(b == KB - 1))
                        for b in range(KB):
                            last = nc.tensor.matmul(kv_bank[:, t % 2, :], xn_T[:, b, t * P:(t + 1) * P], w[:, b, DIM:],
                                                    start=(b == 0), stop=(b == KB - 1))
                        last.then_inc(qkkv_ready, 1)
                        if t >= LAG:
                            turn(t - LAG)
                    for t in range(TILES - LAG, TILES):
                        turn(t)
                    pe.wait_ge(peaked, TILES + 1)
                    for b in range(KB):
                        last = nc.tensor.transpose(peaks[:, b, 0:P], peak[:, b * 128:(b + 1) * 128], c.ident[:P, :P])
                    last.then_inc(peak_turned, 1)
                    pe.wait_ge(peak_found, 1)
                    for b in range(KB):
                        last = nc.tensor.matmul(peaks[:P, b, 128:256], peak_col[:, b:b + 1].broadcast_to([128, P]), c.ident[:],
                                                start=True, stop=True)
                    last.then_inc(peak_spread, 1)

                @block.gpsimd
                def _(pool):
                    for t in range(TILES):
                        nc.gpsimd.tensor_tensor(x[:, t, :], x[:, t, :], xn[:, t, 0:DIM], ALU.add)

                @block.scalar
                def _(act):
                    def keep_turned(t):
                        act.wait_ge(turn_ready, t + 1)
                        nc.scalar.activation(q_T[:, :, bass.ds(t * P, P)],
                                             turned[:, bass.ds(t % 2, 1), 0:KB * P].rearrange("p a (k n) -> p (a k) n", k=KB),
                                             ACT.Copy).then_inc(turn_copied, 1)

                    for t in range(TILES):
                        act.wait_ge(qkkv_ready, t + 1)
                        nc.scalar.activation(row(k, t), kv_bank[:, bass.ds(t % 2, 1), 0:DIM].rearrange("p a d -> p (a d)"),
                                             ACT.Copy).then_inc(kv_read, 1)
                        nc.scalar.activation(row(v, t), kv_bank[:, bass.ds(t % 2, 1), DIM:].rearrange("p a d -> p (a d)"),
                                             ACT.Copy).then_inc(kv_read, 1)
                        act.wait_ge(q_less, t + 1)
                        nc.scalar.activation(row(q, t), row(q, t), ACT.Exp).then_inc(q_exped, 1)
                        if t >= LAG:
                            keep_turned(t - LAG)
                    for t in range(TILES - LAG, TILES):
                        keep_turned(t)

                @block.vector
                def _(dve):
                    nc.vector.memset(peak[:], -3.0e38).then_inc(peaked, 1)
                    for t in range(TILES):
                        dve.wait_ge(qkkv_ready, t + 1)
                        heads = by_head(q_bank[:, bass.ds(t % 2, 1), 0:DIM].rearrange("p a d -> p (a d)"))
                        nc.vector.tensor_reduce(q_peak[:], heads, AX.X, ALU.max).then_inc(q_peaked, 1)
                        dve.wait_ge(q_peaked, t + 1)
                        nc.vector.tensor_tensor(by_head(row(q, t)), heads, spread(q_peak), ALU.subtract).then_inc(q_less, 1)
                        dve.wait_ge(peaked, t + 1)
                        dve.wait_ge(kv_read, t * 2 + 1)
                        nc.vector.tensor_tensor(peak[:], row(k, t), peak[:], ALU.max).then_inc(peaked, 1)
                        dve.wait_ge(q_exped, t + 1)
                        dve.sem_inc(passed, 1)
                        nc.vector.tensor_reduce(q_sum[:], by_head(row(q, t)), AX.X, ALU.add).then_inc(q_added, 1)
                        dve.wait_ge(q_added, t + 1)
                        nc.vector.reciprocal(q_sum[:], q_sum[:]).then_inc(q_inverted, 1)
                        dve.wait_ge(q_inverted, t + 1)
                        nc.vector.tensor_tensor(by_head(row(q, t)), by_head(row(q, t)), spread(q_sum), ALU.mult).then_inc(q_ready, 1)
                    dve.wait_ge(peak_turned, 1)
                    nc.vector.tensor_reduce(peak_col[:], peaks[:, :, 0:P], AX.X, ALU.max).then_inc(peak_found, 1)
                    dve.wait_ge(peak_spread, 1)
                    chain.tick(nc.vector.tensor_copy(peak[:].rearrange("p (b d) -> p b d", b=KB), peaks[:P, :, 128:256]))
                    chain.wait(dve)
                    dve.wait_ge(kv_read, 2 * TILES)
                    for t in range(TILES):
                        nc.vector.tensor_tensor(row(k, t), row(k, t), peak[:], ALU.subtract)

        with ExitStack() as second:
            vk = p.ps("at_vk", [128, KB, 512], scope=second)
            k_sum = p.ps("at_k_sum", [128, KB, 512], scope=second)
            outs = p.ps("at_outs", [P, 2, 512], scope=second)
            turned = p.ps("at_turned2", [128, 2, 512], scope=second)
            zeroed, k_exped, vk_ready, heads_ready = sem("zeroed"), sem("k_exped"), sem("vk_ready"), sem("heads_ready")
            k_inverted, kv_wo_ready, kv_wo_kept = sem("k_inverted"), sem("kv_wo_ready"), sem("kv_wo_kept")
            out_ready, out_kept, measured = sem("out_ready"), sem("out_kept"), sem("measured")
            var_ready, std_ready, degreed = sem("var_ready"), sem("std_ready"), sem("degreed")
            sum_turned, sum_copied, message_ready, added = sem("sum_turned"), sem("sum_copied"), sem("message_ready"), sem("added")
            gained, joined, totalled, k_summed = sem("gained"), sem("joined"), sem("totalled"), sem("k_summed")
            s6 = stats[:].rearrange("p (t k) -> p k t", k=6)
            with nc.Block() as block:
                @block.scalar
                def _(act):
                    for t in range(TILES):
                        nc.scalar.activation(row(k, t), row(k, t), ACT.Exp).then_inc(k_exped, 1)
                    act.wait_ge(vk_ready, 1)
                    act.wait_ge(zeroed, 1)
                    for b in range(KB):
                        for h in range(128 // HEAD1):
                            d = slice(h * HEAD1, (h + 1) * HEAD1)
                            last = nc.scalar.activation(heads_vk[d, b, d], vk[d, b, d], ACT.Copy)
                    last.then_inc(heads_ready, 1)
                    act.wait_ge(var_ready, 1)
                    nc.scalar.activation(std[:], var[:], ACT.Sqrt).then_inc(std_ready, 1)
                    for t in range(TILES):
                        act.wait_ge(sum_turned, t + 1)
                        nc.scalar.activation(sum_T[:, t % 2, :], turned[:, t % 2, 0:KB * P], ACT.Copy).then_inc(sum_copied, 1)

                @block.tensor
                def _(pe):
                    for t in range(TILES):
                        pe.wait_ge(k_exped, t + 1)
                        for b in range(KB):
                            f = slice(b * 128, (b + 1) * 128)
                            last = nc.tensor.matmul(vk[:, b, 0:128], v[:, t, f], k[:, t, f], start=(t == 0),
                                                    stop=(t == TILES - 1))
                    last.then_inc(vk_ready, 1)
                    pe.wait_ge(totalled, TILES + 1)
                    for b in range(KB):
                        last = nc.tensor.matmul(k_sum[:, b, 0:1], k_total[:, b * 128:(b + 1) * 128], c.ones[:P, 0:1],
                                                start=True, stop=True)
                    last.then_inc(k_summed, 1)
                    pe.wait_ge(heads_ready, 1)
                    for b in range(KB):
                        last = nc.tensor.matmul(vk[:, b, 0:DIM], heads_vk[:, b, :],
                                                w_out[:, b, :], start=True, stop=True)
                    last.then_inc(kv_wo_ready, 1)
                    pe.wait_ge(kv_wo_kept, 1)
                    for t in range(TILES):
                        if t >= 2:
                            pe.wait_ge(out_kept, t - 1)
                        for b in range(KB):
                            last = nc.tensor.matmul(outs[:, t % 2, 0:DIM], q_T[:, b, t * P:(t + 1) * P], kv_wo[:, b, :],
                                                    start=(b == 0), stop=(b == KB - 1))
                        last.then_inc(out_ready, 1)

                    def turn(t):
                        if t >= 2:
                            pe.wait_ge(sum_copied, t - 1)
                        for b in range(KB):
                            last = nc.tensor.transpose(turned[:, t % 2, b * P:(b + 1) * P],
                                                       hidden_sum[:, t, b * 128:(b + 1) * 128], c.ident[:P, :P])
                        last.then_inc(sum_turned, 1)

                    pe.wait_ge(out_kept, TILES)
                    turn(0)
                    for t in range(TILES):
                        if t + 1 < TILES:
                            turn(t + 1)
                        pe.wait_ge(sum_copied, t + 1)
                        if t >= 2:
                            pe.wait_ge(added, t - 1)
                        for b in range(KB):
                            last = nc.tensor.matmul(outs[:, t % 2, 0:DIM], sum_T[:, t % 2, b * P:(b + 1) * P], w2[:, b, :],
                                                    start=(b == 0), stop=(b == KB - 1))
                        last.then_inc(message_ready, 1)

                @block.gpsimd
                def _(pool):
                    nc.gpsimd.memset(k_total[:], 0.0).then_inc(totalled, 1)
                    for t in range(TILES):
                        pool.wait_ge(totalled, t + 1)
                        pool.wait_ge(k_exped, t + 1)
                        nc.gpsimd.tensor_tensor(k_total[:], k_total[:], k[:, t, :], ALU.add).then_inc(totalled, 1)

                @block.vector
                def _(dve):
                    def attend(t):
                        dve.wait_ge(gained, t + 1)
                        dve.wait_ge(added, t + 1)
                        nc.vector.scalar_tensor_tensor(row(x, t), row(out, t), std[:, bass.ds(t, 1)], row(x, t), ALU.mult,
                                                       ALU.add).then_inc(joined, 1)

                    def measure(t):
                        dve.wait_ge(joined, t + 1)
                        nc.vector.bn_stats(c.stats[:, t * 6:(t + 1) * 6], x[:, t, :])

                    nc.vector.memset(heads_vk[:], 0.0).then_inc(zeroed, 1)
                    for t in range(TILES):
                        nc.vector.scalar_tensor_tensor(row(x, t), b2[:], in_degree[:, bass.ds(t, 1)], row(x, t),
                                                       ALU.mult, ALU.add).then_inc(degreed, 1)
                    dve.wait_ge(k_summed, 1)
                    nc.vector.reciprocal(k_share[:].unsqueeze(2), k_sum[:, :, 0:1]).then_inc(k_inverted, 1)
                    dve.wait_ge(k_inverted, 1)
                    dve.wait_ge(kv_wo_ready, 1)
                    for b in range(KB):
                        last = nc.vector.tensor_scalar(kv_wo[:, b, :], vk[:, b, 0:DIM], k_share[:, b:b + 1], HEAD1 ** -0.5,
                                                       ALU.mult, ALU.mult)
                    last.then_inc(kv_wo_kept, 1)
                    for t in range(TILES):
                        dve.wait_ge(out_ready, t + 1)
                        nc.vector.tensor_copy(row(out, t), outs[:, bass.ds(t % 2, 1), 0:DIM].rearrange("p a d -> p (a d)")).then_inc(out_kept, 1)
                        dve.wait_ge(out_kept, t + 1)
                        nc.vector.bn_stats(stats[:, bass.ds(t * 6, 6)], row(out, t)).then_inc(measured, 1)
                    dve.wait_ge(measured, TILES)
                    nc.vector.tensor_tensor(half[:], s6[:, 1, :], s6[:, 4, :], ALU.subtract)
                    nc.vector.tensor_tensor(mean[:], s6[:, 1, :], s6[:, 4, :], ALU.add)
                    chain.tick(nc.vector.tensor_tensor(var[:], s6[:, 2, :], s6[:, 5, :], ALU.add))
                    chain.wait(dve)
                    nc.vector.tensor_scalar(mean[:], mean[:], 0.5, None, ALU.mult)
                    chain.tick(nc.vector.scalar_tensor_tensor(half[:], half[:], 0.25, half[:], ALU.mult, ALU.mult))
                    chain.wait(dve)
                    chain.tick(nc.vector.scalar_tensor_tensor(var[:], var[:], 1.0 / DIM, half[:], ALU.mult, ALU.add))
                    chain.wait(dve)
                    nc.vector.tensor_scalar(var[:], var[:], LN_EPS, None, ALU.add).then_inc(var_ready, 1)
                    dve.wait_ge(std_ready, 1)
                    inverse_root(dve, nc, chain, std, var, half)
                    dve.wait_ge(degreed, TILES)
                    for t in range(TILES):
                        nc.vector.scalar_tensor_tensor(row(out, t), row(out, t), mean[:, bass.ds(t, 1)], gamma[:],
                                                       ALU.subtract, ALU.mult).then_inc(gained, 1)
                        dve.wait_ge(message_ready, t + 1)
                        nc.vector.tensor_tensor(row(x, t), outs[:, t % 2, 0:DIM], row(x, t), ALU.add).then_inc(added, 1)
                        if t >= 1:
                            attend(t - 1)
                        if t >= 2:
                            measure(t - 2)
                    attend(TILES - 1)
                    measure(TILES - 2)
                    measure(TILES - 1)


def layer1(p, c, A, x, xn, xn_T, row_ranges, src, dst, in_degree):
    table = p.nc.dram_tensor("edge_table", [NODES, DIM], F32).ap()
    layer_norm(p, c, "ln2", x, xn, xn_T)
    with ExitStack() as scope:
        hidden_sum = p.sb("hidden_sum", [P, TILES, DIM], scope=scope)
        with ExitStack() as edges:
            w1 = p.sb("em_w1", [128, KB, DIM], scope=edges)
            attr = p.sb("em_attr", [128, 2, EDGE_TILES // RANGE_ROWS, KB, P], scope=edges)
            attr_loaded = [p.sem(f"em_attr_loaded{u}") for u in range(2)]
            to_nodes_first(p, c, A, xn_T, w1, attr, attr_loaded, hidden_sum, table)
            edge_messages(p, c, row_ranges, A, src, dst, w1, attr, attr_loaded, table, hidden_sum)
        softmax_attention(p, c, A, x, xn, xn_T, hidden_sum, in_degree)


def one_expert(p, c, A, state, xn_T_flat, out):
    nc = p.nc
    HB = HIDDEN // 128
    with ExitStack() as scope:
        sb = lambda name, shape, dtype=F32: p.sb("oe_" + name, shape, dtype, scope)
        gate_bias = sb("bg", [P, EXPERTS])
        gate = Gate(p, scope, "og", 1, gate_bias)
        way = Dispatch(p, c, scope, "od", 1)
        GROUPS = sorted_tiles(1) // 4
        sorted_rows = c.blanks.best_rows
        w1 = sb("w1", [128, KB, HIDDEN])
        wg = sb("wg", [128, HB, EXPERTS])
        b1 = sb("b1", [128, HB])
        bd = sb("bd", [P, EXPERTS * DIM])
        wd = sb("wd", [128, EXPERTS * HB * DIM])
        hidden = sb("hidden", [128, 2, HB, CHUNK])
        xn_T = xn_T_flat[:].rearrange("p (k n) -> p k n", k=KB)
        RESULTS = 4
        at_T, at_result = 4 * ROW, 4 * ROW + KB * CHUNK
        rows = [sb("rows", [P, 4 * ROW])[:], xn_T_flat[:P, 0:at_T]]
        logits_T = rows[0][:EXPERTS, ROW:ROW + 2 * CHUNK].rearrange("p (u n) -> p u n", u=2)
        rows = [r.rearrange("p (j d) -> p j d", d=ROW) for r in rows]
        rows_T = xn_T_flat[:, at_T:at_result].rearrange("p (k n) -> p k n", k=KB)
        result = xn_T_flat[:P, at_result:at_result + RESULTS * DIM].rearrange("p (i d) -> p i d", d=DIM)
        number = sb("number", [P, 2, 4], I32)
        node_i, node = sb("node_i", [P, TILES], I32), sb("node", [P, TILES])
        logits = p.ps("oe_logits", [P, TILES, EXPERTS], scope=scope)
        up = p.ps("oe_up", [128, 2, 512], scope=scope)
        down = p.ps("oe_down", [P, 2, 512], scope=scope)
        turned = p.ps("oe_turned", [128, 512], scope=scope)
        sem = lambda n: p.sem("oe_" + n)
        w1_loaded, loaded, up_ready, hidden_ready, logits_ready = sem("w1_loaded"), sem("loaded"), sem("up_ready"), sem("hidden_ready"), sem("logits_ready")
        wd_loaded, numbered, sent = sem("wd_loaded"), sem("numbered"), sem("sent")
        rows_loaded = [sem(f"rows_loaded{u}") for u in range(2)]
        turn_ready, turn_copied, down_ready, biased, result_ready = (sem("turn_ready"), sem("turn_copied"), sem("down_ready"),
                                                                     sem("biased"), sem("result_ready"))
        number_ready, gated, logits_kept = sem("number_ready"), sem("gated"), sem("logits_kept")
        written = [sem(f"written{u}") for u in range(RESULTS)]
        by_block = lambda a: a.rearrange("(k p) n -> p k n", p=128)
        LOADS = 3

        def owner(engine, i):
            i = min(i, way.tiles - 1)
            return engine.value_load(way.owner[0:1, i:i + 1], min_val=0, max_val=EXPERTS - 1)

        with nc.Block() as block:
            @block.sync
            def _(sp):
                sp.dma_start(w1[:], by_block(A["ffn1_W1"])).then_inc(w1_loaded, 16)
                sp.dma_start(b1[:], A["ffn1_b1_T"]).then_inc(w1_loaded, 16)
                sp.dma_start(wg[:], by_block(A["ffn1_Wg"])).then_inc(loaded, 16)
                sp.dma_start(gate_bias[:], A["ffn1_bg"].partition_broadcast(P)).then_inc(loaded, 16)
                sp.dma_start(bd[:], A["ffn1_bd"].rearrange("e n -> (e n)").partition_broadcast(P)).then_inc(loaded, 16)
                for e in range(EXPERTS):
                    sp.dma_start(wd[:, e * HB * DIM:(e + 1) * HB * DIM].rearrange("p (k n) -> p k n", k=HB),
                                 by_block(A["ffn1_Wd"][e])).then_inc(wd_loaded, 16)
                sp.wait_ge(loaded, LOADS * 16)
                sp.wait_ge(sent, TILES * 16)
                for g in range(GROUPS):
                    if g >= 2:
                        sp.wait_ge(result_ready, 4 * (g - 1))
                    load_rows(sp, rows[g % 2], sorted_rows[g * 4 * P:(g + 1) * 4 * P, :]
                              .rearrange("(j p) d -> p j d", p=P), rows_loaded[g % 2])

            @block.gpsimd
            def _(pool):
                gate.pool_steps(pool)
                way.pool_steps(pool)
                nc.gpsimd.iota(node_i[:], [[P, TILES]], base=0, channel_multiplier=1).then_inc(numbered, 1)
                pool.wait_ge(way.ready, 1)
                for t in range(TILES):
                    nc.gpsimd.indirect_dma_start(out=sorted_rows, out_offset=bass.IndirectOffsetOnAxis(
                        ap=way.slot[0][:, t:t + 1].bitcast(mybir.dt.uint32), axis=0), in_=state[:, t, :],
                        in_offset=None).then_inc(sent, 16)
                for i in range(GROUPS * 4):
                    pool.wait_ge(number_ready, i // 4 + 1)
                    pool.wait_ge(result_ready, i + 1)
                    nc.gpsimd.indirect_dma_start(out=out, out_offset=bass.IndirectOffsetOnAxis(
                        ap=number[:, (i // 4) % 2, i % 4:i % 4 + 1].bitcast(mybir.dt.uint32), axis=0), in_=result[:, i % RESULTS, :],
                        in_offset=None, bounds_check=NODES - 1, oob_is_err=False).then_inc(written[i % RESULTS], 16)
                for u in range(RESULTS):
                    pool.wait_ge(written[u], GROUPS * 4 // RESULTS * 16)

            @block.tensor
            def _(pe):
                def raise_up(n, columns):
                    for m in range(HB):
                        i = n * HB + m
                        if i >= 2:
                            pe.wait_ge(hidden_ready, i - 1)
                        for k in range(KB):
                            last = nc.tensor.matmul(up[:, i % 2, 0:CHUNK], w1[:, k, m * 128:(m + 1) * 128], columns[:, k, :],
                                                    start=(k == 0), stop=(k == KB - 1))
                        last.then_inc(up_ready, 1)

                def gate_chunk(q):
                    pe.wait_ge(hidden_ready, (q + 1) * HB)
                    if q >= 1:
                        pe.wait_ge(logits_kept, q)
                    for m in range(HB):
                        last = nc.tensor.matmul(turned[:EXPERTS, 0:CHUNK], wg[:, m, :], hidden[:, q % 2, m, :],
                                                start=(m == 0), stop=(m == HB - 1))
                    last.then_inc(gated, 1)

                def turn_logits(q):
                    pe.wait_ge(logits_kept, q + 1)
                    for t in range(q * 4, (q + 1) * 4):
                        nc.tensor.transpose(logits[:, t, :], logits_T[:, q % 2, (t % 4) * P:(t % 4 + 1) * P],
                                            c.ident[:EXPERTS, :EXPERTS]).then_inc(logits_ready, 1)

                def turn(g):
                    pe.wait_ge(rows_loaded[g % 2], 32 * (g // 2 + 1))
                    for k in range(KB):
                        if g * KB + k:
                            pe.wait_ge(turn_copied, g * KB + k)
                        for j in range(4):
                            last = nc.tensor.transpose(turned[:, j * P:(j + 1) * P],
                                                       rows[g % 2][:, j, DIM + k * 128:DIM + (k + 1) * 128], c.ident[:P, :P])
                        last.then_inc(turn_ready, 1)

                def bring_down(g, experts):
                    n = CHUNKS + g
                    pe.wait_ge(hidden_ready, (n + 1) * HB)
                    for j in range(4):
                        i = g * 4 + j
                        if i >= 2:
                            pe.wait_ge(biased, i - 1)
                        for m in range(HB):
                            last = nc.tensor.matmul(down[:, i % 2, 0:DIM], hidden[:, n % 2, m, j * P:(j + 1) * P],
                                                    wd[:, bass.ds(experts[j] * (HB * DIM) + m * DIM, DIM)], start=(m == 0),
                                                    stop=(m == HB - 1))
                        last.then_inc(down_ready, 1)

                pe.wait_ge(w1_loaded, 32)
                raise_up(0, xn_T[:, :, 0:CHUNK])
                pe.wait_ge(loaded, LOADS * 16)
                for q in range(CHUNKS):
                    if q + 1 < CHUNKS:
                        raise_up(q + 1, xn_T[:, :, (q + 1) * CHUNK:(q + 2) * CHUNK])
                    gate_chunk(q)
                    if q >= 1:
                        turn_logits(q - 1)
                turn_logits(CHUNKS - 1)
                way.tensor_steps(pe, gate)
                turn(0)
                pe.wait_ge(wd_loaded, EXPERTS * 16)
                pe.wait_ge(way.ready, 1)
                for g in range(GROUPS):
                    pe.wait_ge(turn_copied, (g + 1) * KB)
                    experts = [owner(pe, g * 4 + j) for j in range(4)]
                    raise_up(CHUNKS + g, rows_T)
                    if g + 1 < GROUPS:
                        turn(g + 1)
                    bring_down(g, experts)

            @block.scalar
            def _(act):
                def activate(n):
                    if n >= CHUNKS + 2:
                        act.wait_ge(down_ready, 4 * (n - CHUNKS - 1))
                    elif n >= 2:
                        act.wait_ge(gated, min(n - 1, CHUNKS))
                    for m in range(HB):
                        i = n * HB + m
                        act.wait_ge(up_ready, i + 1)
                        nc.scalar.activation(hidden[:, n % 2, m, :], up[:, i % 2, 0:CHUNK], ACT.Gelu,
                                             bias=b1[:, m:m + 1]).then_inc(hidden_ready, 1)

                def keep_turned(g):
                    for k in range(KB):
                        act.wait_ge(turn_ready, g * KB + k + 1)
                        nc.scalar.activation(rows_T[:, k, :], turned[:, 0:CHUNK], ACT.Copy).then_inc(turn_copied, 1)

                act.wait_ge(w1_loaded, 32)
                activate(0)
                for q in range(CHUNKS):
                    if q + 1 < CHUNKS:
                        activate(q + 1)
                    act.wait_ge(gated, q + 1)
                    if q >= 2:
                        act.wait_ge(logits_ready, 4 * (q - 1))
                    nc.scalar.activation(logits_T[:, q % 2, :], turned[:EXPERTS, 0:CHUNK],
                                         ACT.Copy).then_inc(logits_kept, 1)
                gate.scalar_steps(act)
                keep_turned(0)
                for g in range(GROUPS):
                    activate(CHUNKS + g)
                    if g + 1 < GROUPS:
                        keep_turned(g + 1)

            @block.vector
            def _(dve):
                chain = Chain(sem("chain"))
                dve.wait_ge(numbered, 1)
                chain.tick(nc.vector.tensor_copy(state[:, :, NUMBER:ROW], node_i[:].unsqueeze(2)))
                dve.wait_ge(loaded, LOADS * 16)
                gate.vector_steps(dve, logits[:], logits_ready, TILES)
                chain.tick(nc.vector.tensor_copy(state[:, :, SHARE:NUMBER], gate.best[0][:].unsqueeze(2)))
                chain.wait(dve)
                way.vector_steps(dve, gate)
                for g in range(GROUPS):
                    dve.wait_ge(rows_loaded[g % 2], 32 * (g // 2 + 1))
                    nc.vector.tensor_copy(number[:, g % 2, :].unsqueeze(2), rows[g % 2][:, :, NUMBER:ROW]).then_inc(number_ready, 1)
                    for j in range(4):
                        i = g * 4 + j
                        expert = owner(dve, i)
                        dve.wait_ge(down_ready, i + 1)
                        if g >= 1:
                            dve.wait_ge(written[i % RESULTS], 16 * g)
                        nc.vector.tensor_tensor(result[:, i % RESULTS, :], down[:, i % 2, 0:DIM], bd[:, bass.ds(expert * DIM, DIM)],
                                                ALU.add).then_inc(biased, 1)
                        dve.wait_ge(biased, i + 1)
                        nc.vector.scalar_tensor_tensor(result[:, i % RESULTS, :], result[:, i % RESULTS, :], rows[g % 2][:, j, SHARE:NUMBER],
                                                       rows[g % 2][:, j, 0:DIM], ALU.mult, ALU.add).then_inc(result_ready, 1)


def gps_layers(nc, A, out, upto=99):
    with ExitStack() as ctx:
        p, c = Program(nc, ctx), Names()
        state = p.sb("state", [P, TILES, ROW])
        x, xn = state[:, :, 0:DIM], state[:, :, DIM:2 * DIM + 1]
        xn_T = p.sb("xn_T", [128, KB * NODES])
        xn_T_flat, xn_T = xn_T, xn_T[:].rearrange("p (k n) -> p k n", k=KB)
        c.ident = p.sb("ident", [128, 128])
        c.ones = p.sb("ones", [128, 128])
        c.zero = p.sb("zero", [1, P], BF16)
        c.stats = p.sb("stats", [P, TILES * 6])
        with ExitStack() as graph:
            graph_layers(p, c, A, state, x, xn, xn_T, graph, upto)
        if upto >= 4:
            layer_norm(p, c, "ln3", x, xn, xn_T, measured_before=True)
            one_expert(p, c, A, state, xn_T_flat, out)
            return
        done = p.sem("done")
        with nc.Block() as block:
            @block.sync
            def _(sp):
                sp.dma_start(out.rearrange("(t p) d -> p t d", p=P), x[:]).then_inc(done, 16)
                sp.wait_ge(done, 16)


def graph_layers(p, c, A, state, x, xn, xn_T, graph, upto):
    nc = p.nc
    constants(p, c, graph)
    src = p.sb("src_cols", [P, EDGE_TILES], I32, graph)
    dst = p.sb("dst_cols", [P, EDGE_TILES], I32, graph)
    in_degree = p.sb("in_degree", [P, TILES], scope=graph)
    loaded = p.sem("x_loaded")
    with nc.Block() as block:
        @block.vector
        def _(dve):
            nc.vector.memset(c.zero[:], 0.0)
            nc.vector.memset(xn[:, :, DIM:DIM + 1], 1.0)

        @block.sync
        def _(sp):
            load_rows(sp, x[:], A["x"].rearrange("(t p) d -> p t d", p=P), loaded)
            sp.dma_start(src[:], A["src_cols"]).then_inc(loaded, 16)
            sp.dma_start(dst[:], A["dst_cols"]).then_inc(loaded, 16)
            sp.wait_ge(loaded, 64)
    with ExitStack() as scope:
        ranges, row_ranges, steps = edge_ranges(p, A, 2, graph, scope)
        layer_norm(p, c, "ln0", x, xn, xn_T, beside=steps)
    c.blanks = Blanks(p, graph)
    with ExitStack() as layer0:
        mean_in = p.sb("mean_in", [P, TILES, DIM + 1], scope=layer0)
        mean_out = p.sb("mean_out", [P, TILES, DIM + 1], scope=layer0)
        mixer = p.sb("mixer", [128, KB, DIM], scope=layer0)
        all_neighbour_sums(p, c, ranges, 2, xn, src, dst, mean_in, mean_out, c.blanks)
        if upto >= 1:
            linear_attention(p, c, A, xn_T, mixer, mean_in, mean_out, in_degree)
            sage_and_mix(p, c, A, x, xn_T, mean_in[:, :, 0:DIM], mean_out, mixer)
    if upto >= 2:
        layer_norm(p, c, "ln1", x, xn, xn_T, measured_before=True)
        mixture(p, c, A, state, x, xn, xn_T)
    if upto >= 3:
        p.clear_semaphores()
        layer1(p, c, A, x, xn, xn_T, row_ranges, src, dst, in_degree)


def laid_out(i):
    import numpy as np
    turn = lambda a: np.ascontiguousarray(np.asarray(a).T)
    keep = lambda a: np.ascontiguousarray(np.asarray(a))
    a = {
        "x": keep(i["x"]),
        "src_cols": turn(keep(i["src"]).reshape(EDGE_TILES, P)),
        "dst_cols": turn(keep(i["dst"]).reshape(EDGE_TILES, P)),
        "dst_blocks": keep(i["dst"]).reshape(RANGE_ROWS, -1),
        "edge_attr_T": np.ascontiguousarray(keep(i["edge_attr_256"]).reshape(RANGE_ROWS, -1, P, KB, 128)
                                            .transpose(0, 4, 1, 3, 2)).reshape(RANGE_ROWS, 128, -1),
        "wk_T": turn(i["L0_mix_wk"]), "wv_T": turn(i["L0_mix_wv"]), "wq": keep(i["L0_mix_wq"]), "wo_T": turn(i["L0_mix_wo"]),
        "ln_k_g": keep(i["L0_mix_ln_k_g"]), "ln_k_b": keep(i["L0_mix_ln_k_b"]),
        "ln_v_g": keep(i["L0_mix_ln_v_g"]), "ln_v_b": keep(i["L0_mix_ln_v_b"]),
        "W_l_f_T": turn(i["L0_gnn_W_l_f"]), "W_r_f_T": turn(i["L0_gnn_W_r_f"]), "b_l_f": keep(i["L0_gnn_b_l_f"]),
        "W_l_b_T": turn(i["L0_gnn_W_l_b"]), "W_r_b_T": turn(i["L0_gnn_W_r_b"]), "b_l_b": keep(i["L0_gnn_b_l_b"]),
        "bn_gamma": keep(i["L0_gnn_gamma"]), "bn_beta": keep(i["L0_gnn_beta"]), "bo": keep(i["L0_mix_bo"]),
        "router_T": turn(i["L0_ffn_router_w"]),
        "ffn0_b1_T": turn(keep(i["L0_ffn_b1"]).reshape(EXPERTS * KB, 128)),
        "ffn0_w1": keep(i["L0_ffn_w1"]), "ffn0_w2": keep(i["L0_ffn_w2"]), "ffn0_b2": keep(i["L0_ffn_b2"]),
        "gnn1_W1": keep(i["L1_gnn_W1"]), "gnn1_b1": keep(i["L1_gnn_b1"]),
        "gnn1_W2": keep(i["L1_gnn_W2"]), "gnn1_b2": keep(i["L1_gnn_b2"]),
        "Wqkv": keep(i["L1_mix_Wqkv"]), "Wout": keep(i["L1_mix_Wout"]), "mix1_gamma": keep(i["L1_mix_gamma"]),
        "ffn1_W1": keep(i["L1_ffn_W1"]), "ffn1_b1_T": turn(keep(i["L1_ffn_b1"]).reshape(HIDDEN // 128, 128)),
        "ffn1_Wg": keep(i["L1_ffn_Wg"]), "ffn1_bg": keep(i["L1_ffn_bg"]),
        "ffn1_Wd": keep(i["L1_ffn_Wd"]), "ffn1_bd": keep(i["L1_ffn_bd"]),
    }
    return a


def kernel(**inputs):
    import concourse.bacc as bacc
    from concourse.bass_utils import run_bass_kernel_spmd

    arrays = laid_out(inputs)
    nc = bacc.Bacc("TRN2", target_bir_lowering=False, num_devices=1)
    A = {n: nc.dram_tensor(f"in_{n}", a.shape, mybir.dt.from_np(a.dtype), kind="ExternalInput").ap()
         for n, a in arrays.items()}
    out = nc.dram_tensor("out", [NODES, DIM], F32, kind="ExternalOutput").ap()
    gps_layers(nc, A, out)
    result = run_bass_kernel_spmd(nc, [{f"in_{n}": a for n, a in arrays.items()}], core_ids=[0])
    return result.results[0]["out"]
```
